# Optimizing a Trainium2 kernel written in Bass

```python
import numpy as np
import jax
import jax.numpy as jnp

def _softmax(x, axis=-1):
    return jax.nn.softmax(x, axis=axis)

def _gelu(x):
    return jax.nn.gelu(x, approximate=True)

def _silu(x):
    return jax.nn.silu(x)

def _sigmoid(x):
    return jax.nn.sigmoid(x)

def _layernorm(x, axis=-1, eps=1e-05):
    m = jnp.mean(x, axis=axis, keepdims=True)
    v = jnp.var(x, axis=axis, keepdims=True)
    return (x - m) / jnp.sqrt(v + eps)

def _scatter_add(tgt, idx, src, axis=0):
    return tgt.at[idx].add(src)

def _segment_sum(src, seg, n):
    return jax.ops.segment_sum(src, seg, n)
kernel_name = 'mk_perceiver_d2_seqx_r8_8dc32c'

def setup_inputs(seed: int=0):
    np.random.seed(seed)
    _w = jnp.asarray

    def _rec_inputs():
        import jax
        import jax.numpy as jnp
        _rk = jax.random.key(seed)
        x = -0.0002928 + 1 * jax.random.normal(jax.random.fold_in(_rk, 1), (16, 64, 128), jnp.float32)
        _lenS = 64 - jax.random.randint(jax.random.fold_in(_rk, 7), (16,), 0, max(1, 64 // 4) + 1, jnp.int32)
        _lenS2 = 128 - jax.random.randint(jax.random.fold_in(_rk, 8), (16,), 0, max(1, 128 // 4) + 1, jnp.int32)
        _ctx_1024P = jax.random.normal(jax.random.fold_in(_rk, 11), (16, 16, 128), jnp.float32)
        _ctx_1024c = jax.random.dirichlet(jax.random.fold_in(_rk, 511), 0.3 * jnp.ones((16,), jnp.float32), (16, 128))
        _ctx_1024t = jnp.einsum('bsk,bkd->bsd', _ctx_1024c, _ctx_1024P)
        _ctx_1024t = _ctx_1024t * jax.lax.rsqrt(jnp.mean(jnp.square(_ctx_1024t)) + 1e-12) * 0.953939
        ctx_1024 = -1.39393e-06 + 0.999914 * (_ctx_1024t + 0.3 * jax.random.normal(jax.random.fold_in(_rk, 611), (16, 128, 128), jnp.float32))
        return (x, ctx_1024)
    x, ctx_1024 = _rec_inputs()

    def _L0_xattn_setup():
        import jax, jax.numpy as jnp
        import numpy as np
        EMBED_DIM = 128
        NUM_HEADS = 16
        HEAD_DIM = EMBED_DIM // NUM_HEADS
        WINDOW = 64
        B, S_Q, S_K = (2, 256, 256)

        def apply_rope(x):
            Dh = x.shape[-1]
            half = Dh // 2
            pos = jnp.arange(x.shape[2], dtype=jnp.float32)
            inv_freq = 1.0 / 10000.0 ** (jnp.arange(0, half, dtype=jnp.float32) / half)
            ang = pos[:, None] * inv_freq[None, :]
            cos = jnp.cos(ang)[None, None, :, :].astype(x.dtype)
            sin = jnp.sin(ang)[None, None, :, :].astype(x.dtype)
            x1, x2 = (x[..., :half], x[..., half:])
            return jnp.concatenate([x1 * cos - x2 * sin, x1 * sin + x2 * cos], axis=-1)
        key = jax.random.key(seed)
        ks = jax.random.split(key, 11)
        scale = 1.0 / np.sqrt(EMBED_DIM)
        inp = {'query': jax.random.normal(ks[0], (B, S_Q, EMBED_DIM), jnp.float32), 'key': jax.random.normal(ks[1], (B, S_K, EMBED_DIM), jnp.float32), 'value': jax.random.normal(ks[2], (B, S_K, EMBED_DIM), jnp.float32), 'Wq': jax.random.normal(ks[3], (EMBED_DIM, EMBED_DIM), jnp.float32) * scale, 'bq': jnp.zeros((EMBED_DIM,), jnp.float32), 'Wk': jax.random.normal(ks[4], (EMBED_DIM, EMBED_DIM), jnp.float32) * scale, 'bk': jnp.zeros((EMBED_DIM,), jnp.float32), 'Wv': jax.random.normal(ks[5], (EMBED_DIM, EMBED_DIM), jnp.float32) * scale, 'bv': jnp.zeros((EMBED_DIM,), jnp.float32), 'Wo': jax.random.normal(ks[6], (EMBED_DIM, EMBED_DIM), jnp.float32) * scale, 'bo': jnp.zeros((EMBED_DIM,), jnp.float32)}
        return inp
    _L0_xattn_all = _L0_xattn_setup()
    _L0_xattn_in = {k: v for k, v in _L0_xattn_all.items() if k in ('Wq', 'bq', 'Wk', 'bk', 'Wv', 'bv', 'Wo', 'bo')}
    del _L0_xattn_all

    def _L0_attn_setup():
        import jax, jax.numpy as jnp
        import numpy as np
        DIM = 128
        DEPTH = 6
        HEADS = 8
        FF_MULT = 4
        LN_EPS = 1e-05
        LEAKY_SLOPE = 0.01

        def _layernorm(x, w, b):
            m = jnp.mean(x, axis=-1, keepdims=True)
            v = jnp.mean(jnp.square(x - m), axis=-1, keepdims=True)
            return (x - m) * jax.lax.rsqrt(v + LN_EPS) * w + b

        def _linear_attn(q, k, v):
            q = jax.nn.softmax(q, axis=-1)
            k = jax.nn.softmax(k, axis=-2)
            context = jnp.einsum('bhnd,bhne->bhde', k, v)
            return jnp.einsum('bhnd,bhde->bhne', q, context)
        key = jax.random.key(seed)
        ks = jax.random.split(key, 12)
        b, t = (2, 512)
        s = 0.02
        return {'x': jax.random.normal(ks[0], (b, t, DIM), dtype=jnp.float32), 'ln1_w': jnp.ones((DEPTH, DIM), jnp.float32), 'ln1_b': jnp.zeros((DEPTH, DIM), jnp.float32), 'wq': jax.random.normal(ks[1], (DEPTH, DIM, DIM), jnp.float32) * s, 'wk': jax.random.normal(ks[2], (DEPTH, DIM, DIM), jnp.float32) * s, 'wv': jax.random.normal(ks[3], (DEPTH, DIM, DIM), jnp.float32) * s, 'wo': jax.random.normal(ks[4], (DEPTH, DIM, DIM), jnp.float32) * s, 'bo': jnp.zeros((DEPTH, DIM), jnp.float32), 'ln2_w': jnp.ones((DEPTH, DIM), jnp.float32), 'ln2_b': jnp.zeros((DEPTH, DIM), jnp.float32), 'w1': jax.random.normal(ks[5], (DEPTH, DIM, FF_MULT * DIM), jnp.float32) * s, 'w2': jax.random.normal(ks[6], (DEPTH, FF_MULT * DIM, DIM), jnp.float32) * s}
    _L0_attn_all = _L0_attn_setup()
    _L0_attn_in = {k: v for k, v in _L0_attn_all.items() if k in ('ln1_w', 'ln1_b', 'wq', 'wk', 'wv', 'wo', 'bo', 'ln2_w', 'ln2_b', 'w1', 'w2')}
    del _L0_attn_all

    def _L0_ffn_setup():
        import jax, jax.numpy as jnp
        import numpy as np
        N_EXPERTS = 8
        CAP_FACTOR = 1.25
        BATCH, SEQ, DMODEL, DFF = (4, 256, 128, 512)
        key = jax.random.key(seed)
        k0, k1, k2, k3 = jax.random.split(key, 4)
        x = jax.random.normal(k0, (BATCH, SEQ, DMODEL), dtype=jnp.float32)
        Wr = jax.random.normal(k1, (DMODEL, N_EXPERTS), dtype=jnp.float32) * 0.02
        W1 = jax.random.normal(k2, (N_EXPERTS, DMODEL, DFF), dtype=jnp.float32) * 0.02
        W2 = jax.random.normal(k3, (N_EXPERTS, DFF, DMODEL), dtype=jnp.float32) * 0.02
        return {'x': x, 'Wr': Wr, 'W1': W1, 'W2': W2}
    _L0_ffn_all = _L0_ffn_setup()
    _L0_ffn_in = {k: v for k, v in _L0_ffn_all.items() if k in ('Wr', 'W1', 'W2')}
    del _L0_ffn_all

    def _L1_xattn_setup():
        import jax, jax.numpy as jnp
        import numpy as np
        D_MODEL = 128
        NUM_HEADS = 16
        DEPTH = D_MODEL // NUM_HEADS
        key = jax.random.key(seed)
        ks = jax.random.split(key, 10)
        B, T, C = (2, 256, 384)
        s = 1.0 / np.sqrt(D_MODEL)
        inp = {'x': jax.random.normal(ks[0], (B, T, D_MODEL), dtype=jnp.float32), 'context': jax.random.normal(ks[1], (B, C, D_MODEL), dtype=jnp.float32), 'Wq': jax.random.normal(ks[2], (D_MODEL, D_MODEL), dtype=jnp.float32) * s, 'bq': jnp.zeros((D_MODEL,), dtype=jnp.float32), 'Wk': jax.random.normal(ks[3], (D_MODEL, D_MODEL), dtype=jnp.float32) * s, 'bk': jnp.zeros((D_MODEL,), dtype=jnp.float32), 'Wv': jax.random.normal(ks[4], (D_MODEL, D_MODEL), dtype=jnp.float32) * s, 'bv': jnp.zeros((D_MODEL,), dtype=jnp.float32), 'Wo': jax.random.normal(ks[5], (D_MODEL, D_MODEL), dtype=jnp.float32) * s, 'bo': jnp.zeros((D_MODEL,), dtype=jnp.float32)}
        return inp
    _L1_xattn_all = _L1_xattn_setup()
    _L1_xattn_in = {k: v for k, v in _L1_xattn_all.items() if k in ('Wq', 'bq', 'Wk', 'bk', 'Wv', 'bv', 'Wo', 'bo')}
    del _L1_xattn_all

    def _L1_attn_setup():
        import jax, jax.numpy as jnp
        import numpy as np
        NUM_HEADS = 16
        LN_EPS = 1e-05
        FEAT_EPS = 0.0001
        key = jax.random.key(seed)
        ks = jax.random.split(key, 4)
        B, L, D = (2, 256, 128)
        scale = 0.02
        return {'x': jax.random.normal(ks[0], (B, L, D), dtype=jnp.float32), 'Wqkv': jax.random.normal(ks[1], (3 * D, D), dtype=jnp.float32) * scale, 'bqkv': jnp.zeros((3 * D,), dtype=jnp.float32), 'Wout': jax.random.normal(ks[2], (D, D), dtype=jnp.float32) * scale, 'bout': jnp.zeros((D,), dtype=jnp.float32), 'gamma': jnp.ones((D,), dtype=jnp.float32), 'beta': jnp.zeros((D,), dtype=jnp.float32)}
    _L1_attn_all = _L1_attn_setup()
    _L1_attn_in = {k: v for k, v in _L1_attn_all.items() if k in ('Wqkv', 'bqkv', 'Wout', 'bout', 'gamma', 'beta')}
    del _L1_attn_all

    def _L1_ffn_setup():
        import jax, jax.numpy as jnp
        import numpy as np
        D_MODEL = 128
        HIDDEN = 512
        NUM_EXPERTS = 8
        TOP_K = 2
        key = jax.random.key(seed)
        k_x, k_g, k_in, k_out = jax.random.split(key, 4)
        bound_in = 1.0 / HIDDEN
        bound_out = 1.0 / D_MODEL
        x = jax.random.normal(k_x, (2, 256, D_MODEL), dtype=jnp.float32)
        w_gate = jax.random.uniform(k_g, (NUM_EXPERTS, D_MODEL), dtype=jnp.float32, minval=-D_MODEL ** (-0.5), maxval=D_MODEL ** (-0.5))
        w_in = jax.random.uniform(k_in, (NUM_EXPERTS, HIDDEN, D_MODEL), dtype=jnp.float32, minval=-bound_in, maxval=bound_in)
        w_out = jax.random.uniform(k_out, (NUM_EXPERTS, D_MODEL, HIDDEN), dtype=jnp.float32, minval=-bound_out, maxval=bound_out)
        return {'x': x, 'w_gate': w_gate, 'w_in': w_in, 'w_out': w_out}
    _L1_ffn_all = _L1_ffn_setup()
    _L1_ffn_in = {k: v for k, v in _L1_ffn_all.items() if k in ('w_gate', 'w_in', 'w_out')}
    del _L1_ffn_all
    return {'x': x, 'ctx_1024': ctx_1024, 'L0_xattn_Wq': _L0_xattn_in['Wq'], 'L0_xattn_bq': _L0_xattn_in['bq'], 'L0_xattn_Wk': _L0_xattn_in['Wk'], 'L0_xattn_bk': _L0_xattn_in['bk'], 'L0_xattn_Wv': _L0_xattn_in['Wv'], 'L0_xattn_bv': _L0_xattn_in['bv'], 'L0_xattn_Wo': _L0_xattn_in['Wo'], 'L0_xattn_bo': _L0_xattn_in['bo'], 'L0_attn_ln1_w': _L0_attn_in['ln1_w'], 'L0_attn_ln1_b': _L0_attn_in['ln1_b'], 'L0_attn_wq': _L0_attn_in['wq'], 'L0_attn_wk': _L0_attn_in['wk'], 'L0_attn_wv': _L0_attn_in['wv'], 'L0_attn_wo': _L0_attn_in['wo'], 'L0_attn_bo': _L0_attn_in['bo'], 'L0_attn_ln2_w': _L0_attn_in['ln2_w'], 'L0_attn_ln2_b': _L0_attn_in['ln2_b'], 'L0_attn_w1': _L0_attn_in['w1'], 'L0_attn_w2': _L0_attn_in['w2'], 'L0_ffn_Wr': _L0_ffn_in['Wr'], 'L0_ffn_W1': _L0_ffn_in['W1'], 'L0_ffn_W2': _L0_ffn_in['W2'], 'L1_xattn_Wq': _L1_xattn_in['Wq'], 'L1_xattn_bq': _L1_xattn_in['bq'], 'L1_xattn_Wk': _L1_xattn_in['Wk'], 'L1_xattn_bk': _L1_xattn_in['bk'], 'L1_xattn_Wv': _L1_xattn_in['Wv'], 'L1_xattn_bv': _L1_xattn_in['bv'], 'L1_xattn_Wo': _L1_xattn_in['Wo'], 'L1_xattn_bo': _L1_xattn_in['bo'], 'L1_attn_Wqkv': _L1_attn_in['Wqkv'], 'L1_attn_bqkv': _L1_attn_in['bqkv'], 'L1_attn_Wout': _L1_attn_in['Wout'], 'L1_attn_bout': _L1_attn_in['bout'], 'L1_attn_gamma': _L1_attn_in['gamma'], 'L1_attn_beta': _L1_attn_in['beta'], 'L1_ffn_w_gate': _L1_ffn_in['w_gate'], 'L1_ffn_w_in': _L1_ffn_in['w_in'], 'L1_ffn_w_out': _L1_ffn_in['w_out']}

def reference(x, ctx_1024, L0_xattn_Wq, L0_xattn_bq, L0_xattn_Wk, L0_xattn_bk, L0_xattn_Wv, L0_xattn_bv, L0_xattn_Wo, L0_xattn_bo, L0_attn_ln1_w, L0_attn_ln1_b, L0_attn_wq, L0_attn_wk, L0_attn_wv, L0_attn_wo, L0_attn_bo, L0_attn_ln2_w, L0_attn_ln2_b, L0_attn_w1, L0_attn_w2, L0_ffn_Wr, L0_ffn_W1, L0_ffn_W2, L1_xattn_Wq, L1_xattn_bq, L1_xattn_Wk, L1_xattn_bk, L1_xattn_Wv, L1_xattn_bv, L1_xattn_Wo, L1_xattn_bo, L1_attn_Wqkv, L1_attn_bqkv, L1_attn_Wout, L1_attn_bout, L1_attn_gamma, L1_attn_beta, L1_ffn_w_gate, L1_ffn_w_in, L1_ffn_w_out):
    import jax
    import jax.numpy as jnp

    def _L0_xattn_ref(query, key, value, Wq, bq, Wk, bk, Wv, bv, Wo, bo):
        import jax, jax.numpy as jnp
        import numpy as np
        EMBED_DIM = 128
        NUM_HEADS = 16
        HEAD_DIM = EMBED_DIM // NUM_HEADS
        WINDOW = 64
        B, S_Q, S_K = (2, 256, 256)

        def apply_rope(x):
            Dh = x.shape[-1]
            half = Dh // 2
            pos = jnp.arange(x.shape[2], dtype=jnp.float32)
            inv_freq = 1.0 / 10000.0 ** (jnp.arange(0, half, dtype=jnp.float32) / half)
            ang = pos[:, None] * inv_freq[None, :]
            cos = jnp.cos(ang)[None, None, :, :].astype(x.dtype)
            sin = jnp.sin(ang)[None, None, :, :].astype(x.dtype)
            x1, x2 = (x[..., :half], x[..., half:])
            return jnp.concatenate([x1 * cos - x2 * sin, x1 * sin + x2 * cos], axis=-1)
        Bq, Sq, D = query.shape
        Sk = key.shape[1]
        H, Dh = (NUM_HEADS, HEAD_DIM)

        def proj(x, W, b):
            return (x @ W.T + b).reshape(x.shape[0], x.shape[1], H, Dh).transpose(0, 2, 1, 3)
        q = apply_rope(proj(query, Wq, bq))
        k = apply_rope(proj(key, Wk, bk))
        v = proj(value, Wv, bv)
        q = q * Dh ** (-0.5)
        scores = jnp.einsum('bhqd,bhkd->bhqk', q, k)
        q_idx = jnp.arange(Sq)[:, None]
        kv_idx = jnp.arange(Sk)[None, :]
        rel = kv_idx - q_idx
        mask = (rel > 0) | (rel < -WINDOW)
        mask4 = mask[None, None, :, :]
        neg = jnp.finfo(scores.dtype).min
        scores = jnp.where(mask4, neg, scores)
        probs = jax.nn.softmax(scores, axis=-1)
        all_masked = jnp.all(mask4, axis=-1, keepdims=True)
        probs = jnp.where(all_masked, jnp.zeros((), probs.dtype), probs)
        out = jnp.einsum('bhqk,bhkd->bhqd', probs, v)
        out = out.transpose(0, 2, 1, 3).reshape(Bq, Sq, D)
        return out @ Wo.T + bo

    def _L0_attn_ref(x, ln1_w, ln1_b, wq, wk, wv, wo, bo, ln2_w, ln2_b, w1, w2):
        import jax, jax.numpy as jnp
        import numpy as np
        DIM = 128
        DEPTH = 6
        HEADS = 8
        FF_MULT = 4
        LN_EPS = 1e-05
        LEAKY_SLOPE = 0.01

        def _layernorm(x, w, b):
            m = jnp.mean(x, axis=-1, keepdims=True)
            v = jnp.mean(jnp.square(x - m), axis=-1, keepdims=True)
            return (x - m) * jax.lax.rsqrt(v + LN_EPS) * w + b

        def _linear_attn(q, k, v):
            q = jax.nn.softmax(q, axis=-1)
            k = jax.nn.softmax(k, axis=-2)
            context = jnp.einsum('bhnd,bhne->bhde', k, v)
            return jnp.einsum('bhnd,bhde->bhne', q, context)
        b, t, e = x.shape
        h, dh = (HEADS, e // HEADS)
        for i in range(DEPTH):
            xn = _layernorm(x, ln1_w[i], ln1_b[i])
            q = (xn @ wq[i]).reshape(b, t, h, dh).transpose(0, 2, 1, 3)
            k = (xn @ wk[i]).reshape(b, t, h, dh).transpose(0, 2, 1, 3)
            v = (xn @ wv[i]).reshape(b, t, h, dh).transpose(0, 2, 1, 3)
            attn = _linear_attn(q, k, v)
            attn = attn.transpose(0, 2, 1, 3).reshape(b, t, e)
            x = attn @ wo[i] + bo[i] + x
            xn = _layernorm(x, ln2_w[i], ln2_b[i])
            hdn = xn @ w1[i]
            hdn = jnp.where(hdn >= 0, hdn, LEAKY_SLOPE * hdn)
            x = hdn @ w2[i] + x
        return x

    def _L0_ffn_ref(x, Wr, W1, W2):
        import jax, jax.numpy as jnp
        import numpy as np
        N_EXPERTS = 8
        CAP_FACTOR = 1.25
        BATCH, SEQ, DMODEL, DFF = (4, 256, 128, 512)
        B, S, D = x.shape
        E = W1.shape[0]
        cap = int(CAP_FACTOR * B * S / E)
        t = x.reshape(-1, D)
        probs = jax.nn.softmax(t @ Wr, axis=-1)
        idx = jnp.argmax(probs, axis=-1)
        pmax = jnp.max(probs, axis=-1)
        onehot = jax.nn.one_hot(idx, E, dtype=jnp.int32)
        pos = jnp.sum(jnp.cumsum(onehot, axis=0) * onehot, axis=-1) - 1
        kept = pos < cap
        flat = idx * cap + jnp.minimum(pos, cap - 1)
        disp = jnp.zeros((E * cap, D), t.dtype).at[flat].add(t * kept[:, None].astype(t.dtype))
        ein = disp.reshape(E, cap, D)
        h = jax.nn.relu(jnp.einsum('ecd,edf->ecf', ein, W1))
        eout = jnp.einsum('ecf,efd->ecd', h, W2).reshape(E * cap, D)
        comb = jnp.where(kept[:, None], eout[flat], t)
        factor = jnp.where(kept, pmax, jnp.ones_like(pmax))
        out = (comb * factor[:, None]).reshape(B, S, D)
        return out

    def _L1_xattn_ref(x, context, Wq, bq, Wk, bk, Wv, bv, Wo, bo):
        import jax, jax.numpy as jnp
        import numpy as np
        D_MODEL = 128
        NUM_HEADS = 16
        DEPTH = D_MODEL // NUM_HEADS
        B, T, D = x.shape
        C = context.shape[1]
        H, d = (NUM_HEADS, DEPTH)
        q = x @ Wq.T + bq
        k = context @ Wk.T + bk
        v = context @ Wv.T + bv
        q = q.reshape(B, T, H, d).transpose(0, 2, 1, 3)
        k = k.reshape(B, C, H, d).transpose(0, 2, 1, 3)
        v = v.reshape(B, C, H, d).transpose(0, 2, 1, 3)
        scores = jnp.einsum('bhtd,bhcd->bhtc', q, k) / jnp.sqrt(jnp.asarray(d, x.dtype))
        attn = jax.nn.softmax(scores, axis=-1)
        out = jnp.einsum('bhtc,bhcd->bhtd', attn, v)
        out = out.transpose(0, 2, 1, 3).reshape(B, T, D)
        return out @ Wo.T + bo

    def _L1_attn_ref(x, Wqkv, bqkv, Wout, bout, gamma, beta):
        import jax, jax.numpy as jnp
        import numpy as np
        NUM_HEADS = 16
        LN_EPS = 1e-05
        FEAT_EPS = 0.0001
        B, L, D = x.shape
        H = NUM_HEADS
        E = D // H
        qkv = x @ Wqkv.T + bqkv
        q, k, v = jnp.split(qkv, 3, axis=-1)
        q = q.reshape(B, L, H, E)
        k = k.reshape(B, L, H, E)
        v = v.reshape(B, L, H, E)
        q = (jax.nn.elu(q) + 1.0 + FEAT_EPS) / jnp.sqrt(jnp.asarray(E, q.dtype))
        k = jax.nn.elu(k) + 1.0 + FEAT_EPS
        kv = jnp.einsum('blhe,blhf->blhef', k, v)
        kv_cumsum = jnp.cumsum(kv, axis=1)
        k_cumsum = jnp.cumsum(k, axis=1)
        num = jnp.einsum('blhe,blhef->blhf', q, kv_cumsum)
        den = jnp.einsum('blhe,blhe->blh', q, k_cumsum)[..., None] + FEAT_EPS
        out = (num / den).reshape(B, L, D)
        out = out @ Wout.T + bout
        mu = jnp.mean(out, axis=-1, keepdims=True)
        var = jnp.var(out, axis=-1, keepdims=True)
        return (out - mu) / jnp.sqrt(var + LN_EPS) * gamma + beta

    def _L1_ffn_ref(x, w_gate, w_in, w_out):
        import jax, jax.numpy as jnp
        import numpy as np
        D_MODEL = 128
        HIDDEN = 512
        NUM_EXPERTS = 8
        TOP_K = 2
        B, S, D = x.shape
        E = w_in.shape[0]
        xt = x.reshape(-1, D)
        logits = (xt @ w_gate.T).astype(jnp.float32)
        top_logits, top_idx = jax.lax.top_k(logits, TOP_K)
        top_gates = jax.nn.softmax(top_logits, axis=-1).astype(x.dtype)
        gates = (jax.nn.one_hot(top_idx, E, dtype=x.dtype) * top_gates[..., None]).sum(axis=1)
        y = jnp.zeros_like(xt)
        for e in range(E):
            h = xt @ w_in[e].T
            y = y + gates[:, e:e + 1] * (h @ w_out[e].T)
        return y.reshape(B, S, D)
    x = x + _L0_xattn_ref(_layernorm(x, axis=-1), ctx_1024, ctx_1024, L0_xattn_Wq, L0_xattn_bq, L0_xattn_Wk, L0_xattn_bk, L0_xattn_Wv, L0_xattn_bv, L0_xattn_Wo, L0_xattn_bo)
    x = x + _L0_attn_ref(_layernorm(x, axis=-1), L0_attn_ln1_w, L0_attn_ln1_b, L0_attn_wq, L0_attn_wk, L0_attn_wv, L0_attn_wo, L0_attn_bo, L0_attn_ln2_w, L0_attn_ln2_b, L0_attn_w1, L0_attn_w2)
    x = x + _L0_ffn_ref(_layernorm(x, axis=-1), L0_ffn_Wr, L0_ffn_W1, L0_ffn_W2)
    x = x + _L1_xattn_ref(_layernorm(x, axis=-1), ctx_1024, L1_xattn_Wq, L1_xattn_bq, L1_xattn_Wk, L1_xattn_bk, L1_xattn_Wv, L1_xattn_bv, L1_xattn_Wo, L1_xattn_bo)
    x = x + _L1_attn_ref(_layernorm(x, axis=-1), L1_attn_Wqkv, L1_attn_bqkv, L1_attn_Wout, L1_attn_bout, L1_attn_gamma, L1_attn_beta)
    x = x + _L1_ffn_ref(_layernorm(x, axis=-1), L1_ffn_w_gate, L1_ffn_w_in, L1_ffn_w_out)
    return x

_drawn_inputs = setup_inputs


def setup_inputs(seed=0):
    import zlib

    import numpy as np

    out = dict(_drawn_inputs(seed))
    spreads = {'L0_xattn_bq': (0.0, 0.1),
     'L0_xattn_bk': (0.0, 0.308),
     'L0_xattn_bv': (0.0, 0.1),
     'L0_xattn_bo': (0.0, 0.1),
     'L0_attn_ln1_w': (1.0, 0.6),
     'L0_attn_ln1_b': (0.0, 0.323),
     'L0_attn_bo': (0.0, 0.1),
     'L0_attn_ln2_w': (1.0, 0.567),
     'L0_attn_ln2_b': (0.0, 0.435),
     'L1_xattn_bq': (0.0, 0.8),
     'L1_xattn_bk': (0.0, 0.8),
     'L1_xattn_bv': (0.0, 0.1),
     'L1_xattn_bo': (0.0, 0.1),
     'L1_attn_bqkv': (0.0, 0.1),
     'L1_attn_bout': (0.0, 0.1),
     'L1_attn_gamma': (1.0, 0.2),
     'L1_attn_beta': (0.0, 0.1)}
    factors = {'L0_attn_wq': 8.0,
     'L0_attn_wk': 8.0,
     'L0_ffn_W1': 8.0,
     'L0_ffn_W2': 8.0,
     'L1_ffn_w_gate': 8.0,
     'L1_ffn_w_in': 8.0,
     'L1_ffn_w_out': 8.0}
    for name, (base, spread) in spreads.items():
        noise = np.random.default_rng([zlib.crc32(name.encode()), seed]).standard_normal(out[name].shape)
        drawn = base * np.exp(spread * noise) if base else spread * noise
        out[name] = jnp.asarray(drawn.astype(out[name].dtype))
    for name, factor in factors.items():
        out[name] = (out[name] * factor).astype(out[name].dtype)
    return out
```

```python
from contextlib import ExitStack

import numpy as np

import concourse.bass as bass
from concourse import mybir

F32 = mybir.dt.float32
BF16 = mybir.dt.bfloat16
ALU = mybir.AluOpType
ACT = mybir.ActivationFunctionType
AX = mybir.AxisListType

P = 128
B, S, D, CTX = 16, 64, 128, 128
NT = B * S // P
H = 16
DH = D // H
DEPTH = 6
LH = 8
LD = D // LH
E = 8
FF = 512
FC = FF // P
CAP = int(1.25 * B * S / E)
LN_EPS = 1e-5
FEAT_EPS = 1e-4
NEG = -1e30
VA = DH + 1
CA = D + LH

CONST = {}


def _layout():
    at = 0
    for name, width in (
        ("ident", P), ("cos2", 4 * S), ("sin2", 4 * S), ("qmask", 4), ("mask01", S), ("headblock", P),
        ("headsel", LH), ("tokhalf", 2), ("iota", E), ("causal", 2 * S), ("qsel", P), ("ksel", 4 * P),
        ("tri", P), ("ones", P),
    ):
        CONST[name] = (at, at + width)
        at += width
    return at


NCONST = _layout()


def const_table():
    c = np.zeros((P, NCONST), np.float32)

    def put(name, a):
        lo, hi = CONST[name]
        c[:a.shape[0], lo:hi] = a.reshape(a.shape[0], hi - lo)

    p = np.arange(P)
    pos = np.arange(S, dtype=np.float32)
    half = DH // 2
    inv = (1.0 / 10000.0 ** (np.arange(half, dtype=np.float32) / half)).astype(np.float32)
    ang = pos[None, :] * inv[p % half][:, None]
    put("ident", np.eye(P))
    put("cos2", np.tile(np.cos(ang), (1, 4)))
    put("sin2", np.tile(np.sin(ang), (1, 4)))
    put("qmask", ((p // DH)[:, None] % 4 == np.arange(4)) * np.float32(DH ** -0.5))
    put("mask01", (np.arange(S)[None, :] >= (p % S)[:, None]).astype(np.float32))
    put("headblock", (p[:, None] // LD == p[None, :] // LD).astype(np.float32))
    put("headsel", (p[:, None] // LD == np.arange(LH)).astype(np.float32))
    put("tokhalf", (p[:, None] // S == np.arange(2)).astype(np.float32))
    put("iota", np.tile(np.arange(E, dtype=np.float32), (P, 1)))
    put("causal", np.tile(np.where(np.arange(S)[None, :] > (p % S)[:, None], NEG, 0.0), (1, 2)))
    put("qsel", (np.arange(LH)[:, None] == p[None, :] // LD).astype(np.float32))
    put("ksel", (np.arange(8)[:, None] == (np.arange(4 * P) // S)[None, :]).astype(np.float32))
    put("tri", (p[:, None] <= p[None, :]).astype(np.float32))
    put("ones", np.ones((P, P)))
    return c


class Sems(dict):

    def __init__(self, sem, stage):
        self.sem, self.stage = sem, stage

    def __missing__(self, name):
        self[name] = self.sem(f"s{self.stage}_{name}")
        return self[name]


def perceiver_kernel(nc, a, out, stages=6):
    with ExitStack() as ctx:
        def sb(name, shape, dt=F32):
            return ctx.enter_context(nc.sbuf_tensor(name, shape, dt))

        def sem(name):
            return ctx.enter_context(nc.semaphore(name))

        C = sb("C", [P, NCONST])
        CB = sb("CB", [P, NCONST], BF16)

        def const(name, dt=F32):
            lo, hi = CONST[name]
            return (C if dt == F32 else CB)[:, lo:hi]

        ident, identb = const("ident"), const("ident", BF16)
        X = sb("X", [P, NT, D])
        Y = sb("Y", [P, NT, D])
        wraw = sb("wraw", [P, 12, D])
        wT = sb("wT", [P, 9, D])
        wrot = sb("wrot", [P, 2, D])
        woraw = sb("woraw", [P, 3, 2, 2, 8, DH])
        woP = sb("woP", [P, 3, 2, D])
        vrow = sb("vrow", [32, D])
        vcol = sb("vcol", [P, 32])
        brow = sb("brow", [1, 2, D])
        brot = sb("brot", [1, 2, D])
        vbc = sb("vbc", [P, 14, D])
        BQK = sb("BQK", [P, 4, S])
        bqm = sb("bqm", [P, 4])
        spacer = sb("spacer", [P, 1])
        eps = sb("eps", [P, 8])
        power = sb("power", [P, 8])

        ctxbuf = sb("ctxbuf", [P, 2, D])
        stats = sb("stats", [P, 8, 6])
        meanvar = sb("meanvar", [P, 8, 2])
        veps = sb("veps", [P, 8])
        rstd = sb("rstd", [P, 8])
        xn = sb("xn", [P, D])
        xcT = sb("xcT", [P, 3, D])
        qkx = sb("qkx", [P, 2, 4 * S])
        qk = sb("qk", [P, 4 * S])
        qexp = sb("qexp", [P, 2, 4, S])
        kT = sb("kT", [P, 2 * P])
        vaug = sb("vaug", [P, 2, H, VA])
        xb = sb("xb", [P, D])
        sc = [sb(f"sc{p}", [P, 8, P]) for p in range(2)]
        nmax = [sb(f"nmax{p}", [P, 8]) for p in range(2)]
        pT = [sb(f"pT{p}", [P, 8, P]) for p in range(2)]
        rsum = sb("rsum", [P, 2, 8])
        att = sb("att", [P, 2, 4, 2, DH])
        attT = sb("attT", [P, D])
        fm = sb("fm", [P, 2 * P])
        fr = sb("fr", [P, 2 * P])
        ls = sb("ls", [P, D])
        ls2 = sb("ls2", [P, D])

        wq = sb("wq", [P, D])
        wk = sb("wk", [P, D])
        wv = sb("wv", [P, D])
        wo = sb("wo", [P, D])
        w1 = sb("w1", [P, FF])
        w2 = sb("w2", [P, FC, D])
        bo = sb("bo", [P, D])
        lnp = sb("lnp", [P, 4])
        st2 = [sb(f"st2{h}", [P, 4, 6]) for h in range(2)]
        mv2 = [sb(f"mv2{h}", [P, 4, 2]) for h in range(2)]
        ve2 = [sb(f"ve2{h}", [P, 4]) for h in range(2)]
        rs2 = [sb(f"rs2{h}", [P, 4]) for h in range(2)]
        xn2 = [sb(f"xn2{h}", [P, 4, D]) for h in range(2)]
        xT2 = [sb(f"xT2{h}", [P, 4 * P]) for h in range(2)]
        nqm = [sb(f"nqm{h}", [P, 4, LH]) for h in range(2)]
        nkm = [sb(f"nkm{h}", [P, 8]) for h in range(2)]
        nqT = [sb(f"nqT{h}", [8, 4 * P], BF16) for h in range(2)]
        nkT = [sb(f"nkT{h}", [8, D], BF16) for h in range(2)]
        eqT = [sb(f"eqT{h}", [P, 4 * P]) for h in range(2)]
        ek = [sb(f"ek{h}", [P, 4, D]) for h in range(2)]
        vs = [sb(f"vs{h}", [P, 4, D]) for h in range(2)]
        rk = [sb(f"rk{h}", [P, 8]) for h in range(2)]
        ctxa = [sb(f"ctxa{h}", [P, 8, CA]) for h in range(2)]
        rq = [sb(f"rq{h}", [P, 4, LH]) for h in range(2)]
        aq = [sb(f"aq{h}", [P, 4, D]) for h in range(2)]
        aT = [sb(f"aT{h}", [P, 4 * P]) for h in range(2)]
        hs = [sb(f"hs{h}", [P, FC, 4 * P]) for h in range(2)]
        hT = [sb(f"hT{h}", [P, FC, 4 * P]) for h in range(2)]

        tT = sb("tT", [P, NT * P])
        wr = sb("wr", [P, 2, E])
        wgraw = sb("wgraw", [E, D])
        we1 = sb("we1", [P, FF])
        we2 = sb("we2", [P, FC, D])
        acc = sb("acc", [P, NT, D])
        lg = sb("lg", [P, NT, E])
        r1 = sb("r1", [P, NT, E])
        r2 = sb("r2", [P, NT, E])
        oh = sb("oh", [P, NT, E])
        oh2 = sb("oh2", [P, NT, E])
        ohb = sb("ohb", [P, NT, E], BF16)
        gate = sb("gate", [P, E, NT])
        m1 = sb("m1", [P, NT])
        m2 = sb("m2", [P, NT])
        m3 = sb("m3", [P, NT])
        m4 = sb("m4", [P, NT])
        keep = sb("keep", [P, NT])
        woutT = sb("woutT", [P, FC, D])
        wc = sb("wc", [P, E, D])

        Z = ctx.enter_context(nc.psum_tensor("Z", [P, 8, 512], F32))

        s_const = sem("s_const")
        s_tab = sem("s_tab")
        s_x = sem("s_x")
        s_out = sem("s_out")
        s_vec = sem("s_vec")
        s_setd = sem("s_setd")
        s_set = sem("s_set")
        s_setp = sem("s_setp")
        s_sett = sem("s_sett")

        def sems(stage, names):
            names = names.split()
            return Sems(sem, stage)

        A = Sems(sem, "a")
        N = Sems(sem, "n")
        C5 = sems(5, "st mv rv rs xn T xT qk fm fe ff qx va s pm av den rec att attT aTe y bo st2 mv2 rv2 rs2 n g b out xb")
        L = sems(2, "w wv wo w1 w2 bo in st mv rv rs xn yb T xT qt kt nq nk nT nTe adq adk v eq ek vs cx sum rk ca o rq aq aqT "
                    "aqTe wo_ y st_ mv_ rv_ rs_ xn_ T_ xT_ h hT w2_ out")
        M3 = sems(3, "w1 w2 ln t t2 T tT lg r p cum wx h hT o acc")
        M6 = sems(6, "w f T wT m wc ln T2 tT lg r p o acc out")

        x_d = a["x"].rearrange("(t b) n d -> (b n) t d", b=2)
        out_d = out.rearrange("(t b) n d -> (b n) t d", b=2)
        ctx_d = a["ctx_1024"].rearrange("b n d -> n b d")

        block = ctx.enter_context(nc.Block())

        def nth(i, k=1):
            return (i + 1) * k

        def peeled(eng, count, body):
            body(0, True)
            with eng.Fori(1, count) as i:
                body(i, False)

        def KEYS(st):
            return S if st == 1 else CTX

        def scores(st, p):
            return Z[:, 3 + 2 * p:5 + 2 * p, 0:4 * KEYS(st)].rearrange("p g (r k) -> p g r k", k=KEYS(st))

        def bulk(t, st):
            return t[:].rearrange("p r k -> p (r k)")[:, 0:8 * KEYS(st)].rearrange("p (g r k) -> p g r k", g=2, k=KEYS(st))

        def attention_act(act, st):
            s = A
            base = 0 if st == 1 else NT
            with act.Fori(0, NT) as i:
                act.wait_ge(s["ctxT"], nth(i + base))
                act.activation(xcT[:].rearrange("p a n -> p (a n)"), Z[:, 0, 0:3 * D], ACT.Identity).then_inc(s["xcT"], 1)
                if st == 4:
                    act.wait_ge(s["qk"], nth(i + base))
                    for j in range(4):
                        t = act.activation(qexp[:, :, j, :], Z[:, 1, 0:P].rearrange("p (b q) -> p b q", b=2), ACT.Identity,
                                           scale=const("qmask")[:, j:j + 1], bias=bqm[:, j:j + 1])
                    t.then_inc(s["qx"], 1)
                    act.activation(kT[:], Z[:, 1, P:3 * P], ACT.Identity, bias=vcol[:, 25:26]).then_inc(s["kT"], 1)
                for p in range(2):
                    act.wait_ge(s["sub"], 2 * (i + base) + p + 1)
                    act.activation(bulk(sc[p], st), bulk(sc[p], st), ACT.Exp).then_inc(s["exp"], 1)
                for p in range(2):
                    act.wait_ge(s["pT"], 2 * (i + base) + p + 1)
                    if st == 1:
                        act.activation(pT[p][:, 0:4, :], Z[:, 3 + 2 * p, :].rearrange("p (r q) -> p r q", q=P), ACT.Identity).then_inc(s["pTe"], 1)
                    else:
                        act.activation(pT[p][:].rearrange("p r k -> p (r k)"), Z[:, 3 + 2 * p:5 + 2 * p, :].rearrange("p a b -> p (a b)"),
                                       ACT.Identity).then_inc(s["pTe"], 1)
                act.wait_ge(s["attT"], nth(i + base))
                act.activation(attT[:], Z[:, 0, 0:P], ACT.Identity).then_inc(s["aTe"], 1)

        def attention_pe(pe, st):
            s, K = A, KEYS(st)
            base = 0 if st == 1 else NT
            w0 = 0 if st == 1 else 3
            with pe.Fori(0, NT) as i:
                pe.wait_ge(s["xn"], nth(i + base))
                pe.transpose(Z[:, 0, 0:P], xn[:], ident)
                pe.wait_ge(s["ctx"], nth(i + base, 16))
                for b in range(2):
                    t = pe.transpose(Z[:, 0, (1 + b) * P:(2 + b) * P], ctxbuf[:, b, :], ident)
                t.then_inc(s["ctxT"], 1)
                pe.wait_ge(s["xcT"], nth(i + base))
                if st == 1:
                    for k, w in enumerate((wT, wrot)):
                        pe.matmul(Z[:, 1, 4 * S * k:4 * S * k + 2 * S], w[:, 0, :], xcT[:, 0, :], start=True, stop=True)
                        t = pe.matmul(Z[:, 1, 4 * S * k + 2 * S:4 * S * k + 4 * S], w[:, 1, :], xcT[:, 1:3, 0:S], start=True, stop=True)
                    t.then_inc(s["qk"], 1)
                    for b in range(2):
                        for hf in range(2):
                            t = pe.matmul(Z[hf * S:(hf + 1) * S, 2, b * D:(b + 1) * D], xcT[:, 1 + b, 0:S], wT[:, w0 + 2, :],
                                          start=True, stop=True)
                    t.then_inc(s["v"], 1)
                else:
                    pe.matmul(Z[:, 1, 0:P], wT[:, w0, :], xcT[:, 0, :], start=True, stop=True)
                    pe.matmul(Z[:, 1, P:3 * P], wT[:, w0 + 1, :], xcT[:, 1:3, :], start=True, stop=True).then_inc(s["qk"], 1)
                    for b in range(2):
                        t = pe.matmul(Z[:, 2, b * D:(b + 1) * D], xcT[:, 1 + b, :], wT[:, w0 + 2, :], start=True, stop=True)
                    t.then_inc(s["v"], 1)
                if st == 1:
                    for gg in range(4):
                        pe.matmul(Z[:, 3 + gg, 0:4 * K], identb, const("causal", BF16).unsqueeze(1).broadcast_to([P, 2, 2 * S]),
                                  start=True, stop=False, skip_group_check=True)
                pe.wait_ge(s["kT"], nth(i + base))
                pe.wait_ge(s["qx"], nth(i + base))
                for b in range(2):
                    for jj in range(2):
                        for gg in range(4):
                            rows = slice(32 * gg, 32 * gg + 32)
                            t = pe.matmul(Z[:, 3 + gg, (2 * b + jj) * K:(2 * b + jj + 1) * K],
                                          qexp[rows, b, 2 * jj:2 * jj + 2, :].rearrange("p j q -> p (j q)"),
                                          kT[rows, b * K:(b + 1) * K], start=(st == 4), stop=True, skip_group_check=True)
                t.then_inc(s["s"], 1)
                for p in range(2):
                    pe.wait_ge(s["exp"], 2 * (i + base) + p + 1)
                    if st == 1:
                        for r in range(4):
                            t = pe.transpose(Z[:, 3 + 2 * p, r * P:(r + 1) * P],
                                             sc[p][:].rearrange("p r k -> p (r k)")[:, r * P:(r + 1) * P], ident)
                    else:
                        for r in range(8):
                            t = pe.transpose(Z[:, 3 + 2 * p + r // 4, (r % 4) * P:(r % 4 + 1) * P], sc[p][:, r, :], ident)
                    t.then_inc(s["pT"], 1)
                pe.wait_ge(s["va"], nth(i + base))
                for p in range(2):
                    pe.wait_ge(s["pTe"], 2 * (i + base) + p + 1)
                    for jj in range(2):
                        for g2 in range(2):
                            for b in range(2):
                                gg = 2 * p + g2
                                c = 2 * gg + jj
                                if st == 1:
                                    rows = slice(jj * S, (jj + 1) * S)
                                    w = pT[p][rows, 2 * g2 + b, :]
                                else:
                                    rows = slice(0, P)
                                    w = pT[p][:, 4 * g2 + 2 * b + jj, :]
                                at = (b * 4 + gg) * 2 * VA
                                t = pe.matmul(Z[:, (2, 7)[jj], at:at + 2 * VA], w,
                                              vaug[rows, b, 2 * c:2 * c + 2, :].rearrange("p h d -> p (h d)"),
                                              start=True, stop=True, skip_group_check=True)
                t.then_inc(s["av"], 1)
                pe.wait_ge(s["att"], nth(i + base))
                pe.transpose(Z[:, 0, 0:P], att[:].rearrange("p b g j d -> p (b g j d)"), ident).then_inc(s["attT"], 1)
                pe.wait_ge(s_set, 4)
                pe.wait_ge(s["aTe"], nth(i + base))
                out_projection(pe, 0 if st == 1 else 1).then_inc(s["y"], 1)

        def out_projection(pe, w):
            for j in range(2):
                for b in range(2):
                    rows = slice(b * S, (b + 1) * S)
                    t = pe.matmul(Z[rows, b, 0:D], attT[rows, j * S:(j + 1) * S], woP[rows, w, j, :],
                                  start=(j == 0), stop=(j == 1), skip_group_check=True)
            return t

        def norm_dve(v, s, i, src, dst):
            v.bn_stats(stats[:, 0, :], src).then_inc(s["st"], 1)
            v.wait_ge(s["st"], nth(i))
            v.memset(spacer[:], 0.0)
            v.bn_aggr(meanvar[:, 0, :], stats[:, 0, :]).then_inc(s["mv"], 1)
            v.wait_ge(s["rs"], nth(i))
            v.tensor_scalar(dst, src, meanvar[:, 0, 0:1], rstd[:, 0:1], ALU.subtract, ALU.mult).then_inc(s["xn"], 1)

        def norm_pool(g, s, i):
            g.wait_ge(s["mv"], nth(i))
            g.tensor_tensor(veps[:, 0:1], meanvar[:, 0, 1:2], eps[:, 0:1], ALU.add).then_inc(s["rv"], 1)
            g.wait_ge(s["rv"], nth(i))
            g.tensor_tensor(rstd[:, 0:1], veps[:, 0:1], power[:, 0:1], ALU.pow).then_inc(s["rs"], 1)

        def attention_dve(v, st):
            s, K = A, KEYS(st)
            base = 0 if st == 1 else NT
            bv = 0 if st == 1 else 2
            if st == 4:
                v.wait_ge(M3["out"], 1)
            with v.Fori(0, NT) as i:
                xi = X[:, bass.ds(i, 1), :].rearrange("p a d -> p (a d)")
                norm_dve(v, s, i + base, xi, xn[:])
                if st == 1:
                    v.wait_ge(s["qk"], nth(i + base))
                    v.tensor_tensor(qkx[:, 0, :], Z[:, 1, 0:4 * S], const("cos2"), ALU.mult)
                    v.tensor_tensor(qkx[:, 1, :], Z[:, 1, 4 * S:8 * S], const("sin2"), ALU.mult).then_inc(s["qr"], 1)
                    v.wait_ge(s["qr"], nth(i + base))
                    v.tensor_tensor(qk[:], qkx[:, 0, :], qkx[:, 1, :], ALU.add).then_inc(s["qa"], 1)
                    v.wait_ge(s["qa"], nth(i + base))
                    v.tensor_tensor(qk[:, 0:P], qk[:, 0:P], BQK[:, 0:2, :].rearrange("p a s -> p (a s)"), ALU.add).then_inc(s["qb"], 1)
                    v.tensor_tensor(kT[:, 0:P], qk[:, P:2 * P], BQK[:, 2:4, :].rearrange("p a s -> p (a s)"), ALU.add).then_inc(s["kT"], 1)
                v.wait_ge(s["v"], nth(i + base))
                v.tensor_tensor(vaug[:, :, :, 0:DH], Z[:, 2, 0:2 * D].rearrange("p (b h d) -> p b h d", b=2, d=DH),
                                vbc[:, bv, :].rearrange("p (h d) -> p h d", d=DH).unsqueeze(1).broadcast_to([P, 2, H, DH]),
                                ALU.add).then_inc(s["va"], 1)
                for p in range(2):
                    if p == 0:
                        v.wait_ge(s["s"], nth(i + base))
                    v.tensor_reduce(nmax[p][:].rearrange("p (g r) -> p g r", g=2), scores(st, p), AX.X, ALU.max, negate=True).then_inc(s["max"], 1)
                    v.wait_ge(s["max"], 2 * (i + base) + p + 1)
                    v.tensor_tensor(bulk(sc[p], st), scores(st, p),
                                    nmax[p][:].rearrange("p (g r) -> p g r", g=2).unsqueeze(3).broadcast_to([P, 2, 4, K]), ALU.add).then_inc(s["sub"], 1)
                v.wait_ge(s["av"], nth(i + base))
                attention_norm(v, s, i + base, None)
                v.wait_ge(s["xb"], nth(i + base))
                v.wait_ge(s["y"], nth(i + base))
                residual_in(v, s, i)

        def attention_norm(v, s, i, eps):
            for jj in range(2):
                for j in range(2):
                    rows = slice(j * S, (j + 1) * S)
                    o = Z[rows, (2, 7)[jj], 0:16 * VA].rearrange("p (r t d) -> p r t d", t=2, d=VA)
                    t = v.reciprocal(rsum[rows, jj, :], o[:, :, j, DH])
            t.then_inc(s["rec"], 1)
            v.wait_ge(s["rec"], nth(i))
            for jj in range(2):
                for j in range(2):
                    rows = slice(j * S, (j + 1) * S)
                    o = Z[rows, (2, 7)[jj], 0:16 * VA].rearrange("p (r t d) -> p r t d", t=2, d=VA)
                    t = v.tensor_tensor(att[rows].rearrange("p b g j d -> p (b g) j d")[:, :, jj, :], o[:, :, j, 0:DH],
                                        rsum[rows, jj, :].unsqueeze(2).broadcast_to([S, 8, DH]), ALU.mult)
            t.then_inc(s["att"], 1)

        def residual_in(v, s, i):
            for b in range(2):
                rows = slice(b * S, (b + 1) * S)
                t = v.tensor_tensor(X[rows, bass.ds(i, 1), :].rearrange("p a d -> p (a d)"), Z[rows, b, 0:D], xb[rows, :], ALU.add)
            t.then_inc(s["out"], 1)

        def attention_pool(g, st):
            s = A
            base = 0 if st == 1 else NT
            with g.Fori(0, NT) as i:
                norm_pool(g, s, i + base)
                g.tensor_tensor(xb[:], X[:, bass.ds(i, 1), :].rearrange("p a d -> p (a d)"), vbc[:, 1 if st == 1 else 3, :], ALU.add)\
                    .then_inc(s["xb"], 1)
                if st == 1:
                    g.wait_ge(s["qb"], nth(i + base))
                    g.tensor_tensor(qexp[:], qk[:, 0:P].rearrange("p (b q) -> p b q", b=2).unsqueeze(2).broadcast_to([P, 2, 4, S]),
                                    const("qmask").unsqueeze(1).unsqueeze(3).broadcast_to([P, 2, 4, S]), ALU.mult).then_inc(s["qx"], 1)

        def zb(h, k):
            return Z[:, 4 * h + k, :]

        def tiles(bank):
            return bank.rearrange("p (t n) -> p t n", n=P)

        def stats_all(v, s, key, src):
            for t in range(NT):
                u = v.bn_stats(stats[:, t, :], src[:, t, :])
            u.then_inc(s["ast"], 1)
            v.wait_ge(s["ast"], key)
            for t in range(NT):
                u = v.bn_aggr(meanvar[:, t, :], stats[:, t, :])
            u.then_inc(s["amv"], 1)

        def norm_all(v, s, key, src, dst):
            stats_all(v, s, key, src)
            v.wait_ge(s["ars"], key)
            for t in range(NT):
                u = v.tensor_scalar(dst[:, t, :], src[:, t, :], meanvar[:, t, 0:1], rstd[:, t:t + 1], ALU.subtract, ALU.mult)
            u.then_inc(s["axn"], 1)
            v.wait_ge(s["axn"], key)

        def norm_all_pool(g, s, key):
            g.wait_ge(s["amv"], key)
            g.tensor_tensor(veps[:], meanvar[:, :, 1], eps[:], ALU.add).then_inc(s["arv"], 1)
            g.wait_ge(s["arv"], key)
            g.tensor_tensor(rstd[:], veps[:], power[:], ALU.pow).then_inc(s["ars"], 1)

        def half_norm_dve(v, h, n, x):
            y = Y[:, 4 * h:4 * h + 4, :]
            for t in range(4):
                u = v.bn_stats(st2[h][:, t, :], y[:, t, :])
            u.then_inc(L["st" + x], 1)
            v.wait_ge(L["st" + x], n)
            v.memset(spacer[:], 0.0)
            for t in range(4):
                u = v.bn_aggr(mv2[h][:, t, :], st2[h][:, t, :])
            u.then_inc(L["mv" + x], 1)

        def half_scale_dve(v, h, n, x):
            y = Y[:, 4 * h:4 * h + 4, :]
            v.wait_ge(L["rs" + x], n)
            for t in range(4):
                u = v.tensor_scalar(xn2[h][:, t, :], y[:, t, :], mv2[h][:, t, 0:1], rs2[h][:, t:t + 1], ALU.subtract, ALU.mult)
            u.then_inc(L["xn" + x], 1)

        def half_norm_pool(g, h, n, x):
            g.wait_ge(L["mv" + x], n)
            g.tensor_tensor(ve2[h][:], mv2[h][:, :, 1], eps[:, 0:4], ALU.add).then_inc(L["rv" + x], 1)
            g.wait_ge(L["rv" + x], n)
            g.tensor_tensor(rs2[h][:], ve2[h][:], power[:, 0:4], ALU.pow).then_inc(L["rs" + x], 1)

        def layers_pool(g):
            norm_all_pool(g, N, 1)
            with g.Fori(0, DEPTH) as l:
                n = [2 * l + 1, 2 * l + 2]
                for h in range(2):
                    half_norm_pool(g, h, n[h], "")
                g.wait_ge(L["bo"], 16 * l + 16)
                for h in range(2):
                    y = Y[:, 4 * h:4 * h + 4, :]
                    g.wait_ge(L["xn"], n[h])
                    g.tensor_tensor(y, y, bo[:].unsqueeze(1).broadcast_to([P, 4, D]), ALU.add).then_inc(L["yb"], 1)
                for h in range(2):
                    half_norm_pool(g, h, n[h], "_")

        def nextnorm(l):
            return vcol[:, bass.ds(l + 1, 4, DEPTH)]

        def layers_dve(v):
            v.wait_ge(A["out"], NT)
            norm_all(v, N, 1, X, Y)
            norms = vcol[:, 0:4 * DEPTH].rearrange("p (k l) -> p k l", l=DEPTH)
            v.tensor_copy(lnp[:], norms[:, :, 0]).then_inc(L["lnp"], 1)
            with v.Fori(0, DEPTH) as l:
                n = [2 * l + 1, 2 * l + 2]
                for h in range(2):
                    half_norm_dve(v, h, n[h], "")
                for h in range(2):
                    half_scale_dve(v, h, n[h], "")
                for h in range(2):
                    v.wait_ge(L["qt"], n[h])
                    v.tensor_reduce(nqm[h][:].rearrange("p t h -> p (t h)"), zb(h, 1).rearrange("p (t d) -> p t d", d=LD), AX.X, ALU.max, negate=True)\
                        .then_inc(L["nq"], 1)
                    v.wait_ge(L["kt"], n[h])
                    v.tensor_reduce(nkm[h][:], zb(h, 3).rearrange("p (b s) -> p b s", s=S), AX.X, ALU.max, negate=True).then_inc(L["nk"], 1)
                for h in range(2):
                    v.wait_ge(L["nT"], n[h])
                    v.tensor_copy(nqT[h][:], zb(h, 1)[0:8, :])
                    v.tensor_copy(nkT[h][:], zb(h, 3)[0:8, 0:D]).then_inc(L["nTe"], 1)
                for h in range(2):
                    v.wait_ge(L["v"], n[h])
                    v.tensor_copy(vs[h][:].rearrange("p t n -> p (t n)"), zb(h, 1)).then_inc(L["vs"], 1)
                for h in range(2):
                    v.wait_ge(L["cx"], n[h])
                    v.reciprocal(rk[h][:], zb(h, 2)[:, 0:8]).then_inc(L["rk"], 1)
                    v.wait_ge(L["rk"], n[h])
                    for t in range(4):
                        for u in range(2):
                            w = v.scalar_tensor_tensor(out=ctxa[h][:, 2 * t + u, 0:D], in0=tiles(zb(h, (3, 1)[u]))[:, t, :],
                                                       scalar=rk[h][:, 2 * t + u:2 * t + u + 1], in1=const("headblock"),
                                                       op0=ALU.mult, op1=ALU.mult)
                    w.then_inc(L["ca"], 1)
                for h in range(2):
                    v.wait_ge(L["o"], n[h])
                    for k in range(2):
                        o = zb(h, 2 * k)[:, 0:2 * CA].rearrange("p (t c) -> p t c", c=CA)
                        w = v.reciprocal(rq[h][:, 2 * k:2 * k + 2, :], o[:, :, D:CA])
                    w.then_inc(L["rq"], 1)
                    v.wait_ge(L["rq"], n[h])
                    for k in range(2):
                        o = zb(h, 2 * k)[:, 0:2 * CA].rearrange("p (t c) -> p t c", c=CA)
                        w = v.tensor_tensor(aq[h][:, 2 * k:2 * k + 2, :].rearrange("p t (h d) -> p t h d", d=LD),
                                            o[:, :, 0:D].rearrange("p t (h d) -> p t h d", d=LD),
                                            rq[h][:, 2 * k:2 * k + 2, :].unsqueeze(3).broadcast_to([P, 2, LH, LD]), ALU.mult)
                    w.then_inc(L["aq"], 1)
                for h in range(2):
                    y = Y[:, 4 * h:4 * h + 4, :].rearrange("p t n -> p (t n)")
                    v.wait_ge(L["yb"], n[h])
                    v.wait_ge(L["wo_"], n[h])
                    v.tensor_tensor(y, zb(h, 3), y, ALU.add).then_inc(L["y"], 1)
                    v.wait_ge(L["y"], n[h])
                    half_norm_dve(v, h, n[h], "_")
                for h in range(2):
                    half_scale_dve(v, h, n[h], "_")
                for h in range(2):
                    for c in range(FC):
                        v.wait_ge(L["hs"], 8 * l + 4 * h + c + 1)
                        v.tensor_tensor(hT[h][:, c, :], zb(h, (c + 1) % 4), hs[h][:, c, :], ALU.max).then_inc(L["hT"], 1)
                for h in range(2):
                    y = Y[:, 4 * h:4 * h + 4, :].rearrange("p t n -> p (t n)")
                    v.wait_ge(L["w2_"], n[h])
                    v.tensor_tensor(y, zb(h, 1), y, ALU.add).then_inc(L["y2"], 1)
                    v.wait_ge(L["y2"], n[h])
                v.tensor_copy(lnp[:], nextnorm(l)).then_inc(L["lnp"], 1)
            v.tensor_tensor(X[:], X[:], Y[:], ALU.add).then_inc(L["out"], 1)
            v.wait_ge(L["out"], 1)

        def layers_act(act):
            with act.Fori(0, DEPTH) as l:
                n = [2 * l + 1, 2 * l + 2]
                act.wait_ge(L["lnp"], nth(l))
                for h in range(2):
                    act.wait_ge(L["T"], n[h])
                    act.activation(xT2[h][:], zb(h, 0), ACT.Identity, scale=lnp[:, 0:1], bias=lnp[:, 1:2]).then_inc(L["xT"], 1)
                for h in range(2):
                    act.wait_ge(L["v"], n[h])
                    act.activation(eqT[h][:], zb(h, 2), ACT.Exp).then_inc(L["eq"], 1)
                    act.activation(ek[h][:].rearrange("p t n -> p (t n)"), zb(h, 0), ACT.Exp).then_inc(L["ek"], 1)
                for h in range(2):
                    act.wait_ge(L["aqT"], n[h])
                    act.activation(aT[h][:], zb(h, 1), ACT.Identity).then_inc(L["aqTe"], 1)
                for h in range(2):
                    act.wait_ge(L["T_"], n[h])
                    act.activation(xT2[h][:], zb(h, 0), ACT.Identity, scale=lnp[:, 2:3], bias=lnp[:, 3:4]).then_inc(L["xT_"], 1)
                for h in range(2):
                    for c in range(FC):
                        act.wait_ge(L["h1"], 8 * l + 4 * h + c + 1)
                        act.activation(hs[h][:, c, :], zb(h, (c + 1) % 4), ACT.Identity, scale=0.01).then_inc(L["hs"], 1)

        def layers_pe(pe):
            def transposes(h, src, bank):
                for t in range(4):
                    w = pe.transpose(tiles(zb(h, bank))[:, t, :], src[h][:, t, :], ident)
                return w

            def xtile(h, t):
                return xT2[h][:, t * P:(t + 1) * P]

            with pe.Fori(0, DEPTH) as l:
                n = [2 * l + 1, 2 * l + 2]
                for h in range(2):
                    pe.wait_ge(L["xn"], n[h])
                    transposes(h, xn2, 0).then_inc(L["T"], 1)
                pe.wait_ge(L["w"], 32 * l + 32)
                for h in range(2):
                    pe.wait_ge(L["xT"], n[h])
                    for t in range(4):
                        w = pe.matmul(tiles(zb(h, 1))[:, t, :], xtile(h, t), wq[:], start=True, stop=True)
                    w.then_inc(L["qt"], 1)
                    pe.matmul(zb(h, 3), wk[:], xT2[h][:], start=True, stop=True).then_inc(L["kt"], 1)
                    pe.matmul(zb(h, 2), wq[:], xT2[h][:], start=True, stop=False, skip_group_check=True)
                    for t in range(4):
                        w = pe.matmul(tiles(zb(h, 0))[:, t, :], xtile(h, t), wk[:], start=(t == 0), stop=False, skip_group_check=True)
                    w.then_inc(L["qk"], 1)
                for h in range(2):
                    pe.wait_ge(L["nq"], n[h])
                    for t in range(4):
                        pe.transpose(tiles(zb(h, 1))[0:8, t, :], nqm[h][:, t, :], ident)
                    pe.wait_ge(L["nk"], n[h])
                    pe.transpose(zb(h, 3)[0:8, 0:P], nkm[h][:], ident).then_inc(L["nT"], 1)
                pe.wait_ge(L["wv"], 16 * l + 16)
                for h in range(2):
                    pe.wait_ge(L["nTe"], n[h])
                    pe.matmul(zb(h, 2), const("qsel", BF16)[0:8, :], nqT[h][:], start=False, stop=True, skip_group_check=True)
                    for t in range(4):
                        pe.matmul(tiles(zb(h, 0))[:, t, :], const("ksel", BF16)[0:8, t * P:(t + 1) * P], nkT[h][:],
                                  start=False, stop=True, skip_group_check=True)
                    for t in range(4):
                        w = pe.matmul(tiles(zb(h, 1))[:, t, :], xtile(h, t), wv[:], start=True, stop=True)
                    w.then_inc(L["v"], 1)
                for h in range(2):
                    pe.wait_ge(L["ek"], n[h])
                    pe.wait_ge(L["vs"], n[h])
                    for t in range(4):
                        for u in range(2):
                            rows = slice(u * S, (u + 1) * S)
                            pe.matmul(tiles(zb(h, (3, 1)[u]))[:, t, :], ek[h][rows, t, :], vs[h][rows, t, :], start=True, stop=True)
                    for t in range(4):
                        w = pe.matmul(zb(h, 2)[:, 2 * t:2 * t + 2], ek[h][:, t, :], const("tokhalf"), start=True, stop=True)
                    w.then_inc(L["cx"], 1)
                for h in range(2):
                    pe.wait_ge(L["ca"], n[h])
                    for t in range(4):
                        for u in range(2):
                            w = pe.matmul(zb(h, 2 * (t // 2))[u * S:(u + 1) * S, (t % 2) * CA:(t % 2 + 1) * CA],
                                          eqT[h][:, (2 * t + u) * S:(2 * t + u + 1) * S], ctxa[h][:, 2 * t + u, :], start=True, stop=True)
                    w.then_inc(L["o"], 1)
                for h in range(2):
                    pe.wait_ge(L["aq"], n[h])
                    transposes(h, aq, 1).then_inc(L["aqT"], 1)
                pe.wait_ge(L["wo"], 16 * l + 16)
                for h in range(2):
                    pe.wait_ge(L["aqTe"], n[h])
                    for t in range(4):
                        w = pe.matmul(tiles(zb(h, 3))[:, t, :], aT[h][:, t * P:(t + 1) * P], wo[:], start=True, stop=True)
                    w.then_inc(L["wo_"], 1)
                for h in range(2):
                    pe.wait_ge(L["xn_"], n[h])
                    transposes(h, xn2, 0).then_inc(L["T_"], 1)
                pe.wait_ge(L["w1"], 16 * l + 16)
                for h in range(2):
                    pe.wait_ge(L["xT_"], n[h])
                    for c in range(FC):
                        w = pe.matmul(zb(h, (c + 1) % 4), w1[:, c * P:(c + 1) * P], xT2[h][:], start=True, stop=True).then_inc(L["h1"], 1)
                pe.wait_ge(L["w2"], 16 * l + 16)
                for h in range(2):
                    pe.wait_ge(L["hT"], 8 * l + 4 * h + 4)
                    for t in range(4):
                        for c in range(FC):
                            w = pe.matmul(tiles(zb(h, 1))[:, t, :], hT[h][:, c, t * P:(t + 1) * P], w2[:, c, :],
                                          start=(c == 0), stop=(c == FC - 1))
                    w.then_inc(L["w2_"], 1)

        def chain(v, sem_):
            count = [0]

            def link(ins):
                count[0] += 1
                ins.then_inc(sem_, 1)
                v.wait_ge(sem_, count[0])

            return link

        def per_token(t):
            return t[:].unsqueeze(2).broadcast_to([P, NT, E])

        iota = const("iota").unsqueeze(1).broadcast_to([P, NT, E])

        def first_of(v, link, onehot, values, top):
            link(v.tensor_tensor(r1[:], values[:], per_token(top), ALU.is_equal))
            link(v.tensor_scalar(r1[:], r1[:], -float(E), None, ALU.mult))
            link(v.tensor_tensor(r1[:], r1[:], iota, ALU.add))
            link(v.tensor_reduce(m4[:], r1[:], AX.X, ALU.min))
            link(v.tensor_scalar(m4[:], m4[:], float(E), None, ALU.add))
            link(v.tensor_tensor(onehot[:], iota, per_token(m4), ALU.is_equal))

        def router_pe(pe, s, which):
            pe.wait_ge(N["axn"], 2 + which)
            for t in range(NT):
                w = pe.transpose(Z[:, t // 4, (t % 4) * P:(t % 4 + 1) * P], Y[:, t, :], ident)
            w.then_inc(s["T"], 1)
            pe.wait_ge(s["tT"], 1)
            for t in range(NT):
                w = pe.matmul(Z[:, 2, t * E:(t + 1) * E], tT[:, t * P:(t + 1) * P], wr[:, which, :], start=True, stop=True)
            w.then_inc(s["lg"], 1)

        def router_act(act, s):
            act.wait_ge(s["T"], 1)
            act.activation(tT[:], Z[:, 0:2, :].rearrange("p a b -> p (a b)"), ACT.Identity).then_inc(s["tT"], 1)
            act.wait_ge(s["d"], 1)
            if s is M3:
                act.activation(r2[:], r1[:], ACT.Exp).then_inc(s["ex"], 1)
            else:
                act.activation(m3[:], m3[:], ACT.Exp).then_inc(s["ex"], 1)

        def moe_dve(v):
            v.wait_ge(L["out"], 1)
            norm_all(v, N, 2, X, Y)
            link = chain(v, M3["r"])
            v.wait_ge(M3["lg"], 1)
            link(v.tensor_copy(lg[:].rearrange("p t e -> p (t e)"), Z[:, 2, 0:NT * E]))
            link(v.tensor_reduce(m1[:], lg[:], AX.X, ALU.max))
            v.tensor_tensor(r1[:], lg[:], per_token(m1), ALU.subtract).then_inc(M3["d"], 1)
            v.wait_ge(M3["ex"], 1)
            link(v.tensor_reduce(m1[:], r2[:], AX.X, ALU.add))
            link(v.reciprocal(m2[:], m1[:]))
            link(v.tensor_tensor(r2[:], r2[:], per_token(m2), ALU.mult))
            link(v.tensor_reduce(m3[:], r2[:], AX.X, ALU.max))
            first_of(v, link, oh, r2, m3)
            v.tensor_copy(ohb[:], oh[:]).then_inc(M3["p"], 1)
            v.wait_ge(M3["cum"], 1)
            link(v.tensor_tensor(r1[:], Z[:, 3, 0:NT * E].rearrange("p (t e) -> p t e", e=E), oh[:], ALU.mult))
            link(v.tensor_reduce(m4[:], r1[:], AX.X, ALU.add))
            link(v.tensor_scalar(keep[:], m4[:], float(CAP), None, ALU.is_le))
            link(v.tensor_tensor(m1[:], m3[:], keep[:], ALU.mult))
            link(v.tensor_tensor(gate[:].rearrange("p e t -> p t e"), oh[:], per_token(m1), ALU.mult))
            link(v.tensor_scalar(m2[:], keep[:], -1.0, 1.0, ALU.mult, ALU.add))
            link(v.tensor_tensor(acc[:], Y[:], m2[:].unsqueeze(2).broadcast_to([P, NT, D]), ALU.mult))

            def expert(e, first):
                for h in range(2):
                    if not first:
                        v.wait_ge(M3["acc"], 2 * e + h - 1)
                    v.wait_ge(M3["o"], 2 * e + h + 1)
                    for t in range(4):
                        at = acc[:, 4 * h + t, :]
                        w = v.scalar_tensor_tensor(out=at, in0=tiles(zb(h, 0))[:, t, :], scalar=gate[:, bass.ds(e, 1), 4 * h + t],
                                                   in1=at, op0=ALU.mult, op1=ALU.add)
                    w.then_inc(M3["acc"], 1)

            peeled(v, E, expert)
            v.wait_ge(M3["acc"], 2 * E)
            v.tensor_tensor(X[:], X[:], acc[:], ALU.add).then_inc(M3["out"], 1)
            v.wait_ge(M3["out"], 1)

        def moe_act(act):
            router_act(act, M3)
            with act.Fori(0, E) as e:
                for h in range(2):
                    for c in range(FC):
                        act.wait_ge(M3["h"], 8 * e + 4 * h + c + 1)
                        act.activation(hT[h][:, c, :], zb(h, c), ACT.Relu).then_inc(M3["hT"], 1)

        def moe_pool(g):
            norm_all_pool(g, N, 2)

        def moe_pe(pe):
            router_pe(pe, M3, 0)
            pe.wait_ge(M3["p"], 1)
            flat = ohb[:].rearrange("p t e -> p (t e)")
            pe.matmul(Z[:, 3, 0:NT * E], const("tri", BF16), flat, start=True, stop=False, skip_group_check=True)
            for t in range(NT - 1):
                w = pe.matmul(Z[:, 3, (t + 1) * E:NT * E].rearrange("p (t e) -> p t e", e=E), const("ones", BF16),
                              ohb[:, t:t + 1, :].broadcast_to([P, NT - 1 - t, E]), start=False, stop=(t == NT - 2), skip_group_check=True)
            w.then_inc(M3["cum"], 1)
            pe.wait_ge(M3["r"], 13)

            def expert(e, first):
                pe.wait_ge(M3["w1"], 16 * e + 16)
                for h in range(2):
                    if not first:
                        pe.wait_ge(M3["acc"], 2 * e + h - 1)
                    for c in range(FC):
                        pe.matmul(zb(h, c), we1[:, c * P:(c + 1) * P], tT[:, 4 * h * P:4 * (h + 1) * P], start=True, stop=True)\
                            .then_inc(M3["h"], 1)
                pe.wait_ge(M3["w2"], 16 * e + 16)
                for h in range(2):
                    pe.wait_ge(M3["hT"], 8 * e + 4 * h + 4)
                    for t in range(4):
                        for c in range(FC):
                            w = pe.matmul(tiles(zb(h, 0))[:, t, :], hT[h][:, c, t * P:(t + 1) * P], we2[:, c, :],
                                          start=(c == 0), stop=(c == FC - 1))
                    w.then_inc(M3["o"], 1)

            peeled(pe, E, expert)

        def linear_act(act):
            s = C5
            with act.Fori(0, NT) as i:
                act.wait_ge(s["T"], nth(i))
                act.activation(xcT[:, 0, :], Z[:, 0, 0:P], ACT.Identity).then_inc(s["xT"], 1)
                act.wait_ge(s["fm"], nth(i))
                act.activation(fm[:], fm[:], ACT.Exp).then_inc(s["fe"], 1)
                act.wait_ge(s["attT"], nth(i))
                act.activation(attT[:], Z[:, 0, 0:P], ACT.Identity).then_inc(s["aTe"], 1)

        def linear_pe(pe):
            s = C5
            with pe.Fori(0, NT) as i:
                pe.wait_ge(s["xn"], nth(i))
                pe.transpose(Z[:, 0, 0:P], xn[:], ident).then_inc(s["T"], 1)
                pe.wait_ge(s["xT"], nth(i))
                for k in range(2):
                    w = pe.matmul(Z[:, 1, k * P:(k + 1) * P], wT[:, 6 + k, :], xcT[:, 0, :], start=True, stop=True)
                w.then_inc(s["qk"], 1)
                pe.matmul(Z[:, 2, 0:D], xcT[:, 0, :], wT[:, 8, :], start=True, stop=True).then_inc(s["v"], 1)
                pe.wait_ge(s["qx"], nth(i))
                for b in range(2):
                    for gg in range(4):
                        rows = slice(32 * gg, 32 * gg + 32)
                        w = pe.matmul(Z[b * S:(b + 1) * S, 3 + gg, 0:4 * S], qk[rows, P + b * S:P + (b + 1) * S],
                                      qexp[rows, b], start=True, stop=True, skip_group_check=True)
                w.then_inc(s["s"], 1)
                pe.wait_ge(s["va"], nth(i))
                for p in range(2):
                    pe.wait_ge(s["pm"], 2 * i + p + 1)
                    for g2 in range(2):
                        for jj in range(2):
                            for b in range(2):
                                rows = slice(b * S, (b + 1) * S)
                                c = 2 * (2 * p + g2) + jj
                                w = pe.matmul(Z[:, (2, 7)[b], c * 2 * VA:(c + 1) * 2 * VA],
                                              sc[p][rows, 2 * g2 + jj, :],
                                              vaug[rows, 0, 2 * c:2 * c + 2, :].rearrange("p h d -> p (h d)"),
                                              start=True, stop=True, skip_group_check=True)
                w.then_inc(s["av"], 1)
                pe.wait_ge(s["att"], nth(i))
                pe.transpose(Z[:, 0, 0:P], att[:].rearrange("p b g j d -> p (b g j d)"), ident).then_inc(s["attT"], 1)
                pe.wait_ge(s_set, 4)
                pe.wait_ge(s["aTe"], nth(i))
                out_projection(pe, 2).then_inc(s["y"], 1)

        def linear_dve(v):
            s = C5
            v.wait_ge(A["out"], 2 * NT)
            with v.Fori(0, NT) as i:
                xi = X[:, bass.ds(i, 1), :].rearrange("p a d -> p (a d)")
                norm_dve(v, s, i, xi, xn[:])
                v.wait_ge(s["qk"], nth(i))
                for k in range(2):
                    bias = vcol[:, 26 + k:27 + k]
                    v.tensor_scalar(fr[:, k * P:(k + 1) * P], Z[:, 1, k * P:(k + 1) * P], bias, 0.0, ALU.add, ALU.max)
                    w = v.tensor_scalar(fm[:, k * P:(k + 1) * P], Z[:, 1, k * P:(k + 1) * P], bias, 0.0, ALU.add, ALU.min)
                w.then_inc(s["fm"], 1)
                v.wait_ge(s["v"], nth(i))
                v.tensor_tensor(vaug[:, 0, :, 0:DH], Z[:, 2, 0:D].rearrange("p (h d) -> p h d", d=DH),
                                vbc[:, 4, :].rearrange("p (h d) -> p h d", d=DH), ALU.add).then_inc(s["va"], 1)
                v.wait_ge(s["fe"], nth(i))
                v.scalar_tensor_tensor(out=qk[:], in0=fm[:], scalar=FEAT_EPS, in1=fr[:], op0=ALU.add, op1=ALU.add).then_inc(s["ff"], 1)
                v.wait_ge(s["s"], nth(i))
                for p in range(2):
                    v.tensor_tensor(sc[p][:].rearrange("p r k -> p (r k)")[:, 0:8 * S].rearrange("p (g j q) -> p g j q", g=2, j=4),
                                    Z[:, 3 + 2 * p:5 + 2 * p, 0:4 * S].rearrange("p g (j q) -> p g j q", j=4),
                                    const("mask01").unsqueeze(1).unsqueeze(1).broadcast_to([P, 2, 4, S]), ALU.mult).then_inc(s["pm"], 1)
                v.wait_ge(s["av"], nth(i))

                def outputs():
                    for b in range(2):
                        for j in range(2):
                            rows = slice(j * S, (j + 1) * S)
                            yield b, j, rows, Z[rows, (2, 7)[b], 0:16 * VA].rearrange("p (r t d) -> p r t d", t=2, d=VA)

                for b, j, rows, o in outputs():
                    w = v.tensor_scalar(rsum[rows, b, :], o[:, :, j, DH], FEAT_EPS, None, ALU.add)
                w.then_inc(s["den"], 1)
                v.wait_ge(s["den"], nth(i))
                v.reciprocal(rsum[:], rsum[:]).then_inc(s["rec"], 1)
                v.wait_ge(s["rec"], nth(i))
                for b, j, rows, o in outputs():
                    w = v.tensor_tensor(att[rows, b].rearrange("p g j d -> p (g j) d"), o[:, :, j, 0:DH],
                                        rsum[rows, b, :].unsqueeze(2).broadcast_to([S, 8, DH]), ALU.mult)
                w.then_inc(s["att"], 1)
                v.wait_ge(s["y"], nth(i))
                for b in range(2):
                    rows = slice(b * S, (b + 1) * S)
                    w = v.tensor_tensor(ls[rows, :], Z[rows, b, 0:D], vbc[rows, 5, :], ALU.add)
                w.then_inc(s["bo"], 1)
                v.wait_ge(s["bo"], nth(i))
                v.bn_stats(stats[:, 1, :], ls[:]).then_inc(s["st2"], 1)
                v.wait_ge(s["st2"], nth(i))
                v.memset(spacer[:], 0.0)
                v.bn_aggr(meanvar[:, 1, :], stats[:, 1, :]).then_inc(s["mv2"], 1)
                v.wait_ge(s["rs2"], nth(i))
                v.tensor_scalar(ls2[:], ls[:], meanvar[:, 1, 0:1], rstd[:, 1:2], ALU.subtract, ALU.mult).then_inc(s["n"], 1)
                v.wait_ge(s["n"], nth(i))
                v.tensor_tensor(ls2[:], ls2[:], vbc[:, 6, :], ALU.mult).then_inc(s["g"], 1)
                v.wait_ge(s["xb"], nth(i))
                v.wait_ge(s["g"], nth(i))
                v.tensor_tensor(xi, ls2[:], xb[:], ALU.add).then_inc(s["out"], 1)

        def linear_pool(g):
            s = C5
            with g.Fori(0, NT) as i:
                norm_pool(g, s, i)
                g.tensor_tensor(xb[:], X[:, bass.ds(i, 1), :].rearrange("p a d -> p (a d)"), vbc[:, 7, :], ALU.add).then_inc(s["xb"], 1)
                g.wait_ge(s["ff"], nth(i))
                g.tensor_tensor(qexp[:], qk[:, 0:P].rearrange("p (b q) -> p b q", b=2).unsqueeze(2).broadcast_to([P, 2, 4, S]),
                                const("qmask").unsqueeze(1).unsqueeze(3).broadcast_to([P, 2, 4, S]), ALU.mult).then_inc(s["qx"], 1)
                g.wait_ge(s["mv2"], nth(i))
                g.tensor_tensor(veps[:, 1:2], meanvar[:, 1, 1:2], eps[:, 0:1], ALU.add).then_inc(s["rv2"], 1)
                g.wait_ge(s["rv2"], nth(i))
                g.tensor_tensor(rstd[:, 1:2], veps[:, 1:2], power[:, 0:1], ALU.pow).then_inc(s["rs2"], 1)

        def moe6_pe(pe):
            def product(e, first):
                pe.wait_ge(M6["w"], 32 * e + 32)
                for c in range(FC):
                    w = pe.transpose(Z[:, 0, c * P:(c + 1) * P], we2[:].rearrange("p c n -> p (c n)")[:, c * P:(c + 1) * P], ident)
                w.then_inc(M6["wt"], 1)
                if not first:
                    pe.wait_ge(M6["wc"], e)
                pe.wait_ge(M6["wT"], e + 1)
                for c in range(FC):
                    w = pe.matmul(Z[:, 1, 0:D], we1[:, c * P:(c + 1) * P], woutT[:, c, :], start=(c == 0), stop=(c == FC - 1))
                w.then_inc(M6["m"], 1)

            pe.wait_ge(C5["out"], NT)
            peeled(pe, E, product)
            pe.wait_ge(M6["wc"], E)
            router_pe(pe, M6, 1)
            for t in range(NT):
                if t == 1:
                    pe.wait_ge(M6["r"], 1)
                if t >= 4:
                    pe.wait_ge(M6["acc"], E * (t - 3))
                for k in range(2):
                    w = pe.matmul(Z[:, 2 * (t % 4) + k, :], tT[:, t * P:(t + 1) * P],
                                  wc[:, 4 * k:4 * k + 4, :], start=True, stop=True)
                w.then_inc(M6["o"], 1)

        def moe6_act(act):
            with act.Fori(0, E) as e:
                act.wait_ge(M6["wt"], nth(e))
                act.activation(woutT[:].rearrange("p c n -> p (c n)"), Z[:, 0, :], ACT.Identity).then_inc(M6["wT"], 1)
            router_act(act, M6)

        def moe6_pool(g):
            norm_all_pool(g, N, 3)

        def moe6_dve(v):
            with v.Fori(0, E) as e:
                v.wait_ge(M6["m"], nth(e))
                v.tensor_scalar(wc[:, bass.ds(e, 1), :].rearrange("p a n -> p (a n)"), Z[:, 1, 0:D], 1.0, None, ALU.mult)\
                    .then_inc(M6["wc"], 1)
            v.wait_ge(C5["out"], NT)
            norm_all(v, N, 3, X, Y)
            link = chain(v, M6["r"])
            v.wait_ge(M6["lg"], 1)
            link(v.tensor_copy(lg[:].rearrange("p t e -> p (t e)"), Z[:, 2, 0:NT * E]))
            link(v.tensor_reduce(m1[:], lg[:], AX.X, ALU.max))
            first_of(v, link, oh, lg, m1)
            link(v.tensor_scalar(r2[:], oh[:], NEG, None, ALU.mult))
            link(v.tensor_tensor(lg[:], lg[:], r2[:], ALU.add))
            link(v.tensor_reduce(m2[:], lg[:], AX.X, ALU.max))
            first_of(v, link, oh2, lg, m2)
            v.tensor_tensor(m3[:], m2[:], m1[:], ALU.subtract).then_inc(M6["d"], 1)
            v.wait_ge(M6["ex"], 1)
            link(v.tensor_scalar(m1[:], m3[:], 1.0, None, ALU.add))
            link(v.reciprocal(m1[:], m1[:]))
            link(v.tensor_tensor(m2[:], m3[:], m1[:], ALU.mult))
            link(v.tensor_tensor(oh[:], oh[:], per_token(m1), ALU.mult))
            link(v.tensor_tensor(oh2[:], oh2[:], per_token(m2), ALU.mult))
            link(v.tensor_tensor(gate[:].rearrange("p e t -> p t e"), oh[:], oh2[:], ALU.add))
            done = 0
            for t in range(NT):
                v.wait_ge(M6["o"], t + 1)
                for e in range(E):
                    v.scalar_tensor_tensor(out=X[:, t, :], in0=Z[:, 2 * (t % 4) + e // 4, (e % 4) * P:(e % 4 + 1) * P],
                                           scalar=gate[:, e, t:t + 1], in1=X[:, t, :], op0=ALU.mult, op1=ALU.add).then_inc(M6["acc"], 1)
                    done += 1
                    v.wait_ge(M6["acc"], done)
            v.memset(spacer[:], 0.0).then_inc(M6["out"], 1)

        def layers_load(sp):
            def load(l, first):
                def of(name):
                    return a[name][bass.ds(l, 1)].rearrange("l p n -> (l p) n")

                def read(name, each=2):
                    if not first:
                        sp.wait_ge(L[name], each * l)

                read("qk")
                sp.dma_start(wq[:], of("L0_attn_wq")).then_inc(L["w"], 16)
                sp.dma_start(wk[:], of("L0_attn_wk")).then_inc(L["w"], 16)
                read("v")
                sp.dma_start(wv[:], of("L0_attn_wv")).then_inc(L["wv"], 16)
                read("yb")
                sp.dma_start(bo[:], a["L0_attn_bo"][bass.ds(l, 1)].rearrange("l n -> (l n)").partition_broadcast(P)).then_inc(L["bo"], 16)
                read("wo_")
                sp.dma_start(wo[:], of("L0_attn_wo")).then_inc(L["wo"], 16)
                read("h1", 8)
                sp.dma_start(w1[:], of("L0_attn_w1")).then_inc(L["w1"], 16)
                read("w2_")
                sp.dma_start(w2[:], a["L0_attn_w2"].rearrange("l (c p) n -> l p c n", p=P)[bass.ds(l, 1)]
                             .rearrange("l p c n -> (l p) c n")).then_inc(L["w2"], 16)

            peeled(sp, DEPTH, load)

        def experts_load(sp):
            def load(e, first):
                if not first:
                    sp.wait_ge(M3["h"], 8 * e)
                sp.dma_start(we1[:], a["L0_ffn_W1"][bass.ds(e, 1)].rearrange("l p n -> (l p) n")).then_inc(M3["w1"], 16)
                if not first:
                    sp.wait_ge(M3["o"], 2 * e)
                sp.dma_start(we2[:], a["L0_ffn_W2"].rearrange("l (c p) n -> l p c n", p=P)[bass.ds(e, 1)]
                             .rearrange("l p c n -> (l p) c n")).then_inc(M3["w2"], 16)

            peeled(sp, E, load)

        @block.sync
        def _(sp):
            sp.dma_start(C[:], a["const"]).then_inc(s_tab, 16)
            sp.dma_start(X[:], x_d).then_inc(s_x, 16)
            n = 0
            for name in ("L0_xattn_Wq", "L0_xattn_Wk", "L0_xattn_Wv", "L1_xattn_Wq", "L1_xattn_Wk", "L1_xattn_Wv"):
                sp.dma_start(wraw[:, n, :], a[name]).then_inc(s_const, 16)
                n += 1
            sp.dma_start(wraw[:, 6:9, :], a["L1_attn_Wqkv"].rearrange("(c p) n -> p c n", p=P)).then_inc(s_const, 16)
            for k, name in enumerate(("L0_xattn_Wo", "L1_xattn_Wo", "L1_attn_Wout")):
                sp.dma_start(wraw[:, 9 + k, :], a[name]).then_inc(s_const, 16)
            for st in (1, 4):
                if st == 4 and stages >= 3:
                    experts_load(sp)
                if stages < st:
                    continue
                def load(i, first):
                    if not first or st == 4:
                        sp.wait_ge(A["ctxT"], i if st == 1 else i + NT)
                    sp.dma_start(ctxbuf[:], ctx_d[:, bass.ds(2 * i, 2), :]).then_inc(A["ctx"], 16)

                peeled(sp, NT, load)
                if st == 1 and stages >= 2:
                    layers_load(sp)
            if stages >= 6:
                def load(e, first):
                    if not first:
                        sp.wait_ge(M6["m"], e)
                    sp.dma_start(we1[:].rearrange("p (c n) -> p c n", c=FC), a["L1_ffn_w_in"].rearrange("e (c p) n -> e p c n", p=P)
                                 [bass.ds(e, 1)].rearrange("e p c n -> (e p) c n")).then_inc(M6["w"], 16)
                    sp.dma_start(we2[:].rearrange("p c n -> p (c n)"), a["L1_ffn_w_out"][bass.ds(e, 1)]
                                 .rearrange("e p n -> (e p) n")).then_inc(M6["w"], 16)

                peeled(sp, E, load)
            last = {1: (A["out"], NT), 2: (L["out"], 1), 3: (M3["out"], 1), 4: (A["out"], 2 * NT),
                    5: (C5["out"], NT), 6: (M6["out"], 1)}[stages]
            sp.wait_ge(*last)
            sp.dma_start(out_d, X[:]).then_inc(s_out, 16)
            sp.wait_ge(s_out, 16)

        @block.scalar
        def _(act):
            for k, name in enumerate(("L0_attn_ln1_w", "L0_attn_ln1_b", "L0_attn_ln2_w", "L0_attn_ln2_b")):
                act.dma_start(vrow[6 * k:6 * k + 6, :], a[name]).then_inc(s_vec, 16)
            act.dma_start(vrow[24:25, :], a["L1_xattn_bq"].unsqueeze(0)).then_inc(s_vec, 16)
            act.dma_start(vrow[25:26, :], a["L1_xattn_bk"].unsqueeze(0)).then_inc(s_vec, 16)
            act.dma_start(vrow[26:29, :], a["L1_attn_bqkv"].rearrange("(c n) -> c n", n=P)).then_inc(s_vec, 16)
            act.dma_start(vrow[29:32, :], a["L1_attn_bqkv"].rearrange("(c n) -> c n", n=P)).then_inc(s_vec, 16)
            act.dma_start(brow[:, 0, :], a["L0_xattn_bq"].unsqueeze(0)).then_inc(s_vec, 16)
            act.dma_start(brow[:, 1, :], a["L0_xattn_bk"].unsqueeze(0)).then_inc(s_vec, 16)
            for k, v in enumerate((a["L0_xattn_bv"], a["L0_xattn_bo"], a["L1_xattn_bv"], a["L1_xattn_bo"],
                                   a["L1_attn_bqkv"][2 * D:3 * D], a["L1_attn_bout"], a["L1_attn_gamma"], a["L1_attn_beta"])):
                act.dma_start(vbc[:, k, :], v.partition_broadcast(P)).then_inc(s_vec, 16)
            act.dma_start(wr[:, 0, :], a["L0_ffn_Wr"]).then_inc(s_vec, 16)
            act.dma_start(wgraw[:], a["L1_ffn_w_gate"]).then_inc(s_vec, 16)
            attention_act(act, 1)
            if stages >= 2:
                layers_act(act)
            if stages >= 3:
                moe_act(act)
            if stages >= 4:
                attention_act(act, 4)
            if stages >= 5:
                linear_act(act)
            if stages >= 6:
                moe6_act(act)

        NVEC = 16 * 20

        @block.tensor
        def _(pe):
            pe.wait_ge(s_tab, 16)
            pe.wait_ge(s_const, 16 * 10)
            for k in range(9):
                t = pe.transpose(Z[:, k // 4, (k % 4) * P:(k % 4 + 1) * P], wraw[:, k, :], ident)
            t.then_inc(s_sett, 1)
            pe.wait_ge(s_vec, NVEC)
            pe.transpose(Z[:, 3, 0:32], vrow[:], ident[0:32, 0:32])
            pe.transpose(Z[:, 3, 32:40], wgraw[:], ident[0:8, 0:8]).then_inc(s_sett, 1)
            pe.wait_ge(s_setp, 2)
            for w in range(3):
                for j in range(2):
                    k = 2 * w + j
                    t = pe.transpose(Z[:, 4 + k // 4, (k % 4) * P:(k % 4 + 1) * P],
                                     woraw[:, w, j].rearrange("p b c d -> p (b c d)"), ident)
            t.then_inc(s_sett, 1)
            for k, row in enumerate((brow, brot)):
                for j in range(2):
                    t = pe.matmul(Z[:, 6, (2 * k + j) * 2 * S:(2 * k + j + 1) * 2 * S], row[:, j, :],
                                  const("ones")[0:1, :], start=True, stop=True)
            t.then_inc(s_sett, 1)
            pe.wait_ge(s_set, 4)
            attention_pe(pe, 1)
            if stages >= 2:
                layers_pe(pe)
            if stages >= 3:
                moe_pe(pe)
            if stages >= 4:
                attention_pe(pe, 4)
            if stages >= 5:
                linear_pe(pe)
            if stages >= 6:
                moe6_pe(pe)

        @block.vector
        def _(v):
            v.memset(eps[:], LN_EPS)
            v.memset(power[:], -0.5).then_inc(s_set, 1)
            v.wait_ge(s_tab, 16)
            v.tensor_copy(CB[:], C[:])
            for h in range(2):
                for b in range(8):
                    v.tensor_copy(ctxa[h][:, b, D:CA], const("headsel"))
            v.memset(vaug[:], 1.0).then_inc(s_set, 1)
            v.wait_ge(s_sett, 1)
            v.tensor_copy(wT[:], Z[:, 0:3, :].rearrange("p a b -> p (a b)")[:, 0:9 * D].rearrange("p (k n) -> p k n", n=D)).then_inc(s_set, 1)
            v.wait_ge(s_set, 3)
            for k in range(2):
                w = wT[:, k, :].rearrange("p (h t d) -> p h t d", t=2, d=DH // 2)
                r = wrot[:, k, :].rearrange("p (h t d) -> p h t d", t=2, d=DH // 2)
                v.tensor_scalar(r[:, :, 0, :], w[:, :, 1, :], -1.0, None, ALU.mult)
                v.tensor_copy(r[:, :, 1, :], w[:, :, 0, :])
            v.wait_ge(s_sett, 2)
            v.tensor_copy(vcol[:], Z[:, 3, 0:32])
            v.tensor_copy(wr[:, 1, :], Z[:, 3, 32:40]).then_inc(s_setd, 1)
            v.wait_ge(s_setd, 1)
            v.tensor_scalar(bqm[:], const("qmask"), vcol[:, 24:25], None, ALU.mult)
            v.wait_ge(s_sett, 3)
            v.tensor_copy(woP[:].rearrange("p a b n -> p (a b n)"), Z[:, 4:6, :].rearrange("p a b -> p (a b)")[:, 0:6 * D])
            v.wait_ge(s_sett, 4)
            v.tensor_tensor(qkx[:, 0, :], Z[:, 6, 0:4 * S], const("cos2"), ALU.mult)
            v.tensor_tensor(qkx[:, 1, :], Z[:, 6, 4 * S:8 * S], const("sin2"), ALU.mult).then_inc(s_setd, 1)
            v.wait_ge(s_setd, 2)
            v.tensor_tensor(BQK[:].rearrange("p a s -> p (a s)"), qkx[:, 0, :], qkx[:, 1, :], ALU.add).then_inc(s_set, 1)
            v.wait_ge(s_x, 16)
            attention_dve(v, 1)
            if stages >= 2:
                layers_dve(v)
            if stages >= 3:
                moe_dve(v)
            if stages >= 4:
                attention_dve(v, 4)
            if stages >= 5:
                linear_dve(v)
            if stages >= 6:
                moe6_dve(v)

        @block.gpsimd
        def _(g):
            g.wait_ge(s_vec, NVEC)
            for j in range(2):
                w = brow[:, j, :].rearrange("p (h t d) -> p h t d", t=2, d=DH // 2)
                r = brot[:, j, :].rearrange("p (h t d) -> p h t d", t=2, d=DH // 2)
                g.tensor_scalar(r[:, :, 0, :], w[:, :, 1, :], -1.0, None, ALU.mult)
                t = g.tensor_copy(r[:, :, 1, :], w[:, :, 0, :])
            t.then_inc(s_setp, 1)
            g.wait_ge(s_const, 16 * 10)
            for w in range(3):
                src = wraw[:, 9 + w, :].rearrange("p (c j d) -> p c j d", j=2, d=DH)
                for j in range(2):
                    for b in range(2):
                        t = g.tensor_copy(woraw[:, w, j, b], src[:, :, j, :])
            t.then_inc(s_setp, 1)
            g.wait_ge(s_set, 4)
            attention_pool(g, 1)
            if stages >= 2:
                layers_pool(g)
            if stages >= 3:
                moe_pool(g)
            if stages >= 4:
                attention_pool(g, 4)
            if stages >= 5:
                linear_pool(g)
            if stages >= 6:
                moe6_pool(g)



def kernel(**inputs):
    import concourse.bacc as bacc
    from concourse.bass_utils import run_bass_kernel_spmd as run

    nc = bacc.Bacc("TRN2", target_bir_lowering=False, num_devices=1)
    arrays, args = {}, {}
    for name, array in [("const", const_table())] + list(inputs.items()):
        arrays[f"in_{name}"] = np.ascontiguousarray(array)
        args[name] = nc.dram_tensor(f"in_{name}", arrays[f"in_{name}"].shape, F32, kind="ExternalInput").ap()
    out = nc.dram_tensor("out", (B, S, D), F32, kind="ExternalOutput").ap()
    perceiver_kernel(nc, args, out, STAGES)
    return run(nc, [arrays], core_ids=[0]).results[0]["out"]


STAGES = 6
```

```python
from contextlib import ExitStack

import numpy as np

import concourse.bass as bass
from concourse import mybir

F32 = mybir.dt.float32
BF16 = mybir.dt.bfloat16
ALU = mybir.AluOpType
ACT = mybir.ActivationFunctionType
AX = mybir.AxisListType

P = 128
B, S, D, CTX = 16, 64, 128, 128
NT = B * S // P
H = 16
DH = D // H
DEPTH = 6
LH = 8
LD = D // LH
E = 8
FF = 512
FC = FF // P
CAP = int(1.25 * B * S / E)
SLOTS = E * CAP // P
QE = 4
LN_EPS = 1e-5
FEAT_EPS = 1e-4
NEG = -1e30
CA = D + LH

CONST = {}


def _layout():
    at = 0
    for name, width in (
        ("ident", P), ("cos2", 4 * S), ("sin2", 4 * S), ("qpar", 2), ("kpair", 2), ("hpar", 2), ("mask01", S), ("headblock", P),
        ("headsel", LH), ("tokhalf", 2), ("iota", E), ("causal", 2 * S), ("qsel", P), ("ksel", 4 * P),
        ("tri", P), ("ones", P), ("past", NT),
    ):
        CONST[name] = (at, at + width)
        at += width
    return at


NCONST = _layout()


def const_table():
    c = np.zeros((P, NCONST), np.float32)

    def put(name, a):
        lo, hi = CONST[name]
        c[:a.shape[0], lo:hi] = a.reshape(a.shape[0], hi - lo)

    p = np.arange(P)
    pos = np.arange(S, dtype=np.float32)
    half = DH // 2
    inv = (1.0 / 10000.0 ** (np.arange(half, dtype=np.float32) / half)).astype(np.float32)
    ang = pos[None, :] * inv[p % half][:, None]
    put("ident", np.eye(P))
    put("cos2", np.tile(np.cos(ang), (1, 4)))
    put("sin2", np.tile(np.sin(ang), (1, 4)))
    put("qpar", ((p // DH)[:, None] % 2 == np.arange(2)) * np.float32(DH ** -0.5))
    put("kpair", (((p // DH) % 4 // 2)[:, None] == np.arange(2)).astype(np.float32))
    put("hpar", ((p // DH)[:, None] % 2 == np.arange(2)).astype(np.float32))
    put("mask01", (np.arange(S)[None, :] >= (p % S)[:, None]).astype(np.float32))
    put("headblock", (p[:, None] // LD == p[None, :] // LD).astype(np.float32))
    put("headsel", (p[:, None] // LD == np.arange(LH)).astype(np.float32))
    put("tokhalf", (p[:, None] // S == np.arange(2)).astype(np.float32))
    put("iota", np.tile(np.arange(E, dtype=np.float32), (P, 1)))
    put("causal", np.tile(np.where(np.arange(S)[None, :] > (p % S)[:, None], NEG, 0.0), (1, 2)))
    put("qsel", (np.arange(LH)[:, None] == p[None, :] // LD).astype(np.float32))
    put("ksel", (np.arange(8)[:, None] == (np.arange(4 * P) // S)[None, :]).astype(np.float32))
    put("tri", (p[:, None] <= p[None, :]).astype(np.float32))
    put("ones", np.ones((P, P)))
    put("past", E * CAP + np.arange(NT)[None, :] * P + p[:, None])
    return c


class Sems(dict):

    def __init__(self, sem, stage):
        self.sem, self.stage = sem, stage

    def __missing__(self, name):
        self[name] = self.sem(f"s{self.stage}_{name}")
        return self[name]


def perceiver_kernel(nc, a, out, stages=6):
    with ExitStack() as ctx:
        def sb(name, shape, dt=F32):
            return ctx.enter_context(nc.sbuf_tensor(name, shape, dt))

        def sem(name):
            return ctx.enter_context(nc.semaphore(name))

        C = sb("C", [P, NCONST])
        CB = sb("CB", [P, NCONST], BF16)

        def const(name, dt=F32):
            lo, hi = CONST[name]
            return (C if dt == F32 else CB)[:, lo:hi]

        ident, identb = const("ident"), const("ident", BF16)
        X = sb("X", [P, NT, D])
        Y = sb("Y", [P, NT, D])
        wraw = sb("wraw", [P, 12, D])
        wT = sb("wT", [P, 9, D])
        wrot = sb("wrot", [P, 2, D])
        woM = sb("woM", [P, 3, 2, D])
        vrow = sb("vrow", [32, D])
        vcol = sb("vcol", [P, 32])
        brow = sb("brow", [1, 2, D])
        brot = sb("brot", [1, 2, D])
        vbc = sb("vbc", [P, 5, D])
        vbd = sb("vbd", [P, 3, 2 * D])
        BQK = sb("BQK", [P, 4, S])
        BM = sb("BM", [P, 4, 2, S])
        bqm = sb("bqm", [P, 2])
        bkm = sb("bkm", [P, 2])
        spacer = sb("spacer", [P, 1])
        eps = sb("eps", [P, 8])
        power = sb("power", [P, 8])

        ctxbuf = sb("ctxbuf", [P, 2, D])
        stats = sb("stats", [P, 8, 6])
        meanvar = sb("meanvar", [P, 8, 2])
        veps = sb("veps", [P, 8])
        rstd = sb("rstd", [P, 8])
        xn = sb("xn", [P, D])
        xcT = sb("xcT", [P, 3, D])
        qkx = sb("qkx", [P, 2, 4 * S])
        qk = sb("qk", [P, 4 * S])
        qe = sb("qe", [P, 2, 2, S])
        ke = sb("ke", [P, 4 * CTX])
        vx = sb("vx", [P, 4, 320])
        vx4 = sb("vx4", [P, 4, 576])
        sc = [sb(f"sc{p}", [P, 8, P]) for p in range(2)]
        nmax = [sb(f"nmax{p}", [P, 8]) for p in range(2)]
        pT = [sb(f"pT{p}", [P, 8, P]) for p in range(2)]
        den0 = sb("den0", [P, P])
        den = sb("den", [P, P])
        rden = sb("rden", [P, P])
        denb = sb("denb", [P, 2])
        att = sb("att", [P, 2, 2, S])
        fm = sb("fm", [P, 2 * P])
        fr = sb("fr", [P, 2 * P])

        wq = sb("wq", [P, D])
        wk = sb("wk", [P, D])
        wv = sb("wv", [P, D])
        wo = sb("wo", [P, D])
        w1 = sb("w1", [P, FF])
        w2 = sb("w2", [P, FC, D])
        bo = sb("bo", [P, D])
        lnp = sb("lnp", [P, 4])
        st2 = [sb(f"st2{h}", [P, 4, 6]) for h in range(2)]
        mv2 = [sb(f"mv2{h}", [P, 4, 2]) for h in range(2)]
        ve2 = [sb(f"ve2{h}", [P, 4]) for h in range(2)]
        rs2 = [sb(f"rs2{h}", [P, 4]) for h in range(2)]
        xn2 = [sb(f"xn2{h}", [P, 4, D]) for h in range(2)]
        xT2 = [sb(f"xT2{h}", [P, 4 * P]) for h in range(2)]
        nqm = [sb(f"nqm{h}", [P, 4, LH]) for h in range(2)]
        nkm = [sb(f"nkm{h}", [P, 8]) for h in range(2)]
        nqT = [sb(f"nqT{h}", [8, 4 * P], BF16) for h in range(2)]
        nkT = [sb(f"nkT{h}", [8, D], BF16) for h in range(2)]
        eqT = [sb(f"eqT{h}", [P, 4 * P]) for h in range(2)]
        ek = [sb(f"ek{h}", [P, 4, D]) for h in range(2)]
        vs = [sb(f"vs{h}", [P, 4, D]) for h in range(2)]
        rk = [sb(f"rk{h}", [P, 8]) for h in range(2)]
        ctxa = [sb(f"ctxa{h}", [P, 8, CA]) for h in range(2)]
        rq = [sb(f"rq{h}", [P, 4, LH]) for h in range(2)]
        aq = [sb(f"aq{h}", [P, 4, D]) for h in range(2)]
        aT = [sb(f"aT{h}", [P, 4 * P]) for h in range(2)]
        hs = [sb(f"hs{h}", [P, FC, 4 * P]) for h in range(2)]
        hT = [sb(f"hT{h}", [P, FC, 4 * P]) for h in range(2)]

        tT = sb("tT", [P, NT * P])
        wr = sb("wr", [P, 2, E])
        wgraw = sb("wgraw", [E, D])
        we1 = sb("we1", [P, FF])
        we2 = sb("we2", [P, FC, D])
        acc = sb("acc", [P, NT, D])
        xw1 = [sb(f"xw1{k}", [P, FF]) for k in range(QE)]
        xw2 = [sb(f"xw2{k}", [P, FC, D]) for k in range(QE)]
        slot = sb("slot", [P, SLOTS, D])
        slotT, resT = (hs[h][:].rearrange("p c n -> p (c n)")[:, 0:SLOTS * P] for h in range(2))
        place = sb("place", [P, NT])
        placei = sb("placei", [P, NT], mybir.dt.uint32)
        factor = sb("factor", [P, NT])
        lg = sb("lg", [P, NT, E])
        r1 = sb("r1", [P, NT, E])
        r2 = sb("r2", [P, NT, E])
        oh = sb("oh", [P, NT, E])
        oh2 = sb("oh2", [P, NT, E])
        ohb = sb("ohb", [P, NT, E], BF16)
        gate = sb("gate", [P, E, NT])
        m1 = sb("m1", [P, NT])
        m2 = sb("m2", [P, NT])
        m3 = sb("m3", [P, NT])
        m4 = sb("m4", [P, NT])
        keep = sb("keep", [P, NT])
        woutT = hs[1][:, :, 0:D]
        wc = hs[0][:].rearrange("p c n -> p (c n)")[:, 0:E * D].rearrange("p (e n) -> p e n", e=E)

        Z = ctx.enter_context(nc.psum_tensor("Z", [P, 8, 512], F32))

        s_const = sem("s_const")
        s_tab = sem("s_tab")
        s_x = sem("s_x")
        s_out = sem("s_out")
        s_vec = sem("s_vec")
        s_setd = sem("s_setd")
        s_set = sem("s_set")
        s_setp = sem("s_setp")
        s_zero = sem("s_zero")
        s_clear = sem("s_clear")
        s_sett = sem("s_sett")

        def sems(stage, names):
            names = names.split()
            return Sems(sem, stage)

        A = Sems(sem, "a")
        N = Sems(sem, "n")
        C5 = sems(5, "st mv rv rs xn T xT qk fm fe ff qx va s pm av den rec att attT aTe y bo st2 mv2 rv2 rs2 n g b out xb")
        L = sems(2, "w wv wo w1 w2 bo in st mv rv rs xn yb T xT qt kt nq nk nT nTe adq adk v eq ek vs cx sum rk ca o rq aq aqT "
                    "aqTe wo_ y st_ mv_ rv_ rs_ xn_ T_ xT_ h hT w2_ out")
        M3 = sems(3, "w1 w2 ln t t2 T tT lg r p cum wx h hT o acc")
        M6 = sems(6, "w f T wT m wc ln T2 tT lg r p o acc out")

        x_d = a["x"].rearrange("(t b) n d -> (b n) t d", b=2)
        out_d = out.rearrange("(t b) n d -> (b n) t d", b=2)
        slots_d = a["slots"][0:E * CAP].rearrange("(s p) n -> p s n", p=P)
        ctx_d = a["ctx_1024"].rearrange("b n d -> n b d")

        block = ctx.enter_context(nc.Block())

        def nth(i, k=1):
            return (i + 1) * k

        def peeled(eng, count, body):
            body(0, True)
            with eng.Fori(1, count) as i:
                body(i, False)

        def pipelined(eng, front, body):
            front(0)
            body(0, True, False)
            with eng.Fori(1, NT - 1) as i:
                body(i, False, False)
            body(NT - 1, False, True)

        def tile_of(t, i):
            return t[:, bass.ds(i, 1), :].rearrange("p a d -> p (a d)")

        def KEYS(st):
            return S if st == 1 else CTX

        def scores(st, p):
            return Z[:, 3 + 2 * p:5 + 2 * p, 0:4 * KEYS(st)].rearrange("p g (r k) -> p g r k", k=KEYS(st))

        def bulk(t, st):
            return t[:].rearrange("p r k -> p (r k)")[:, 0:8 * KEYS(st)].rearrange("p (g r k) -> p g r k", g=2, k=KEYS(st))

        def kview(st):
            return ke[:, 0:4 * KEYS(st)].rearrange("p (b k) -> p b k", b=2)

        def value_cols(st, jj, at):
            if st == 4:
                return vx4[:].rearrange("p q (c m) -> p q c m", m=144)[:, :, :, at:at + 16]
            rows = slice(jj * S, (jj + 1) * S)
            return vx[rows].rearrange("p q (c m) -> p q c m", m=160)[:, :, :, at + 16 * jj:at + 16 * jj + 16]

        def values_dve(v, s, st, i, n):
            v.wait_ge(s["v"], nth(n))
            k = {1: 0, 4: 1, 5: 2}[st]
            if st == 4:
                w = v.tensor_tensor(value_cols(4, 0, 0), Z[:, 0, 0:2 * D].rearrange("p (q c d) -> p q c d", q=4, d=16),
                                    vbd[:, k, :].rearrange("p (q c d) -> p q c d", q=4, d=16), ALU.add)
            else:
                for jj in range(2):
                    rows = slice(jj * S, (jj + 1) * S)
                    w = v.tensor_tensor(value_cols(st, jj, 0), Z[rows, 0, 0:2 * D].rearrange("p (q c d) -> p q c d", q=4, d=32)[:, :, :, 16 * jj:16 * jj + 16],
                                        vbd[rows, k, :].rearrange("p (q c d) -> p q c d", q=4, d=32)[:, :, :, 16 * jj:16 * jj + 16], ALU.add)
            w.then_inc(s["va"], 1)

        def sums_pe(pe, st, p, weights):
            for b in range(2):
                blocks = [(u, jj) for u in range(2) for jj in range(2)] if st == 4 else [(u, 0) for u in range(2)]
                for c, (u, jj) in enumerate(blocks):
                    w = (vx4 if st == 4 else vx)[:, 2 * b + p, c * P:(c + 1) * P]
                    m = weights[:, 4 * u + 2 * b + jj, :] if st == 4 else weights[:, 2 * u + b, :]
                    t = pe.matmul(Z[:, (2, 7)[p], b * P:(b + 1) * P], w, m, start=(c == 0), stop=(c == len(blocks) - 1), skip_group_check=True)
            return t

        def sums_of(p, j2):
            return Z[P // 2:P, (2, 7)[p], 0:4 * S].rearrange("p (b j q) -> p b j q", b=2, j=2)[:, :, j2, :]

        def sums_act(act, s, st, n):
            for p in range(2):
                act.wait_ge(s["av"], 2 * n + p + 1)
                act.activation(den0[p * 64:(p + 1) * 64].rearrange("p (b q) -> p b q", b=2), sums_of(p, 0), ACT.Identity,
                               scale=const("hpar")[64:P, 0:1], bias=denb[64:P, (0, 1)[st == 5]:(0, 1)[st == 5] + 1]).then_inc(s["d0"], 1)

        def divide_dve(v, s, st, n):
            for p in range(2):
                rows = slice(p * 64, (p + 1) * 64)
                v.wait_ge(s["d0"], 2 * n + p + 1)
                v.scalar_tensor_tensor(out=den[rows].rearrange("p (b q) -> p b q", b=2), in0=sums_of(p, 1), scalar=const("hpar")[rows, 1:2],
                                       in1=den0[rows].rearrange("p (b q) -> p b q", b=2), op0=ALU.mult, op1=ALU.add).then_inc(s["den"], 1)
            v.wait_ge(s["den"], 2 * n + 2)
            v.reciprocal(rden[:], den[:]).then_inc(s["rec"], 1)
            v.wait_ge(s["rec"], n + 1)
            for p in range(2):
                rows = slice(p * 64, (p + 1) * 64)
                t = v.tensor_tensor(att[rows].rearrange("p j b q -> p b j q"),
                                    Z[0:P // 2, (2, 7)[p], 0:4 * S].rearrange("p (b j q) -> p b j q", b=2, j=2),
                                    rden[rows].rearrange("p (b q) -> p b q", b=2).unsqueeze(2).broadcast_to([64, 2, 2, S]), ALU.mult)
            t.then_inc(s["att"], 1)

        def out_projection(pe, w):
            for j in range(2):
                t = pe.matmul(Z[:, 7, 0:D], att[:, j].rearrange("p b q -> p (b q)"), woM[:, w, j, :],
                              start=(j == 0), stop=(j == 1), skip_group_check=True)
            return t

        def attention_act(act, st):
            s = A
            base = 0 if st == 1 else NT

            def front(i):
                act.wait_ge(s["ctxT"], nth(i + base))
                act.activation(xcT[:].rearrange("p a n -> p (a n)"), Z[:, 0, 0:3 * D], ACT.Identity).then_inc(s["xcT"], 1)

            def front_qk(i):
                if st == 4:
                    act.wait_ge(s["qk"], nth(i + base))
                    for j in range(2):
                        act.activation(qe[:, :, j, :], Z[:, 1, 0:P].rearrange("p (b q) -> p b q", b=2), ACT.Identity,
                                       scale=const("qpar")[:, j:j + 1], bias=bqm[:, j:j + 1])
                    for j in range(2):
                        t = act.activation(kview(4).rearrange("p b (j k) -> p b j k", j=2)[:, :, j, :],
                                           Z[:, 1, P:3 * P].rearrange("p (b k) -> p b k", b=2), ACT.Identity,
                                           scale=const("kpair")[:, j:j + 1], bias=bkm[:, j:j + 1])
                    t.then_inc(s["qe"], 1)

            def body(i, first, last):
                if not last:
                    front(i + 1)
                for p in range(2):
                    act.wait_ge(s["sub"], 2 * (i + base) + p + 1)
                    act.activation(bulk(sc[p], st), bulk(sc[p], st), ACT.Exp).then_inc(s["exp"], 1)
                for p in range(2):
                    act.wait_ge(s["pT"], 2 * (i + base) + p + 1)
                    if st == 1:
                        act.activation(pT[p][:, 0:4, :], Z[:, 3 + 2 * p, :].rearrange("p (r q) -> p r q", q=P), ACT.Identity).then_inc(s["pTe"], 1)
                    else:
                        act.activation(pT[p][:].rearrange("p r k -> p (r k)"), Z[:, 3 + 2 * p:5 + 2 * p, :].rearrange("p a b -> p (a b)"),
                                       ACT.Identity).then_inc(s["pTe"], 1)
                if not last:
                    front_qk(i + 1)
                sums_act(act, s, st, i + base)

            def ahead(i):
                front(i)
                front_qk(i)

            pipelined(act, ahead, body)

        def attention_pe(pe, st):
            s, K = A, KEYS(st)
            base = 0 if st == 1 else NT
            w0 = 0 if st == 1 else 3

            def front_T(i):
                if not isinstance(i, int) or i > 0:
                    pe.wait_ge(s["va"], i + base)
                pe.wait_ge(s["xn"], nth(i + base))
                pe.transpose(Z[:, 0, 0:P], xn[:], ident)
                pe.wait_ge(s["ctx" if st == 1 else "ctx4"], nth(i, 32 if st == 1 else 16))
                for b in range(2):
                    t = pe.transpose(Z[:, 0, (1 + b) * P:(2 + b) * P], ctxbuf[:, b, :], ident)
                t.then_inc(s["ctxT"], 1)

            def front_qkv(i):
                pe.wait_ge(s["xcT"], nth(i + base))
                if st == 1:
                    for k, w in enumerate((wT, wrot)):
                        pe.matmul(Z[:, 1, 4 * S * k:4 * S * k + 2 * S], w[:, 0, :], xcT[:, 0, :], start=True, stop=True)
                        t = pe.matmul(Z[:, 1, 4 * S * k + 2 * S:4 * S * k + 4 * S], w[:, 1, :], xcT[:, 1:3, 0:S], start=True, stop=True)
                else:
                    pe.matmul(Z[:, 1, 0:P], wT[:, w0, :], xcT[:, 0, :], start=True, stop=True)
                    t = pe.matmul(Z[:, 1, P:3 * P], wT[:, w0 + 1, :], xcT[:, 1:3, :], start=True, stop=True)
                t.then_inc(s["qk"], 1)
                for b in range(2):
                    t = pe.matmul(Z[:, 0, b * D:(b + 1) * D], xcT[:, 1 + b, :], wT[:, w0 + 2, :], start=True, stop=True)
                t.then_inc(s["v"], 1)

            def tail_y(i):
                pe.wait_ge(s["att"], nth(i + base))
                out_projection(pe, 0 if st == 1 else 1).then_inc(s["y"], 1)

            def body(i, first, last):
                if st == 1:
                    for gg in range(4):
                        pe.matmul(Z[:, 3 + gg, 0:4 * K], identb, const("causal", BF16).unsqueeze(1).broadcast_to([P, 2, 2 * S]),
                                  start=True, stop=False, skip_group_check=True)
                pe.wait_ge(s["qe"], nth(i + base))
                for gg in range(4):
                    rows = slice(32 * gg, 32 * gg + 32)
                    for b in range(2):
                        t = pe.matmul(Z[:, 3 + gg, b * 2 * K:(b + 1) * 2 * K], qe[rows, b].rearrange("p j q -> p (j q)"),
                                      kview(st)[rows, b, :], start=(st == 4), stop=True, skip_group_check=True)
                    if gg % 2:
                        t.then_inc(s["s"], 1)
                if not last:
                    front_T(i + 1)
                if not last:
                    front_qkv(i + 1)
                if not first:
                    tail_y(i - 1)
                for p in range(2):
                    pe.wait_ge(s["exp"], 2 * (i + base) + p + 1)
                    if st == 1:
                        for r in range(4):
                            t = pe.transpose(Z[:, 3 + 2 * p, r * P:(r + 1) * P],
                                             sc[p][:].rearrange("p r k -> p (r k)")[:, r * P:(r + 1) * P], ident)
                    else:
                        for r in range(8):
                            t = pe.transpose(Z[:, 3 + 2 * p + r // 4, (r % 4) * P:(r % 4 + 1) * P], sc[p][:, r, :], ident)
                    t.then_inc(s["pT"], 1)
                pe.wait_ge(s["va"], nth(i + base))
                for p in range(2):
                    if p == 1 and (not first or st == 4):
                        pe.wait_ge(s["out"], i + base)
                    pe.wait_ge(s["pTe"], 2 * (i + base) + p + 1)
                    sums_pe(pe, st, p, pT[p]).then_inc(s["av"], 1)

            def ahead(i):
                front_T(i)
                front_qkv(i)

            pipelined(pe, ahead, body)
            tail_y(NT - 1)

        def scale_tile(v, s, i, step):
            v.tensor_scalar(xn[:], tile_of(X, i), meanvar[:, bass.ds(i, 1), 0], rstd[:, bass.ds(i, 1)],
                            ALU.subtract, ALU.mult).then_inc(s["xn"], 1)

        def attention_dve(v, st):
            s, K = A, KEYS(st)
            base = 0 if st == 1 else NT
            stats_all(v, N, 1 if st == 1 else 4, X)
            v.wait_ge(N["ars"], 1 if st == 1 else 4)

            def front(i):
                if not isinstance(i, int) or i > 0:
                    v.wait_ge(s["ctxT"], i + base)
                scale_tile(v, s, i, i + base)

            def front_rope(i):
                if st == 1:
                    v.wait_ge(s["qk"], nth(i + base))
                    v.tensor_tensor(qkx[:, 0, :], Z[:, 1, 0:4 * S], const("cos2"), ALU.mult)
                    v.tensor_tensor(qkx[:, 1, :], Z[:, 1, 4 * S:8 * S], const("sin2"), ALU.mult).then_inc(s["qr"], 1)
                    v.wait_ge(s["qr"], nth(i + base))
                    v.tensor_tensor(qk[:], qkx[:, 0, :], qkx[:, 1, :], ALU.add).then_inc(s["qa"], 1)
                    v.wait_ge(s["qa"], nth(i + base))
                    for k, (mask, out_) in enumerate((("qpar", qe[:]), ("kpair", kview(1).rearrange("p b (j k) -> p b j k", j=2)))):
                        for j in range(2):
                            t = v.scalar_tensor_tensor(out=out_[:, :, j, :], in0=qk[:, k * P:(k + 1) * P].rearrange("p (b s) -> p b s", b=2),
                                                       scalar=const(mask)[:, j:j + 1], in1=BM[:, 2 * k:2 * k + 2, j, :],
                                                       op0=ALU.mult, op1=ALU.add)
                    t.then_inc(s["qe"], 1)

            def tail(i):
                v.wait_ge(s["y"], nth(i + base))
                v.tensor_tensor(tile_of(X, i), Z[:, 7, 0:D], tile_of(Y, i), ALU.add).then_inc(s["out"], 1)

            def body(i, first, last):
                if not last:
                    front(i + 1)
                for p in range(2):
                    v.wait_ge(s["s"], 2 * (i + base) + p + 1)
                    v.tensor_reduce(nmax[p][:].rearrange("p (g r) -> p g r", g=2), scores(st, p), AX.X, ALU.max, negate=True).then_inc(s["max"], 1)
                    v.wait_ge(s["max"], 2 * (i + base) + p + 1)
                    v.tensor_tensor(bulk(sc[p], st), scores(st, p),
                                    nmax[p][:].rearrange("p (g r) -> p g r", g=2).unsqueeze(3).broadcast_to([P, 2, 4, K]), ALU.add).then_inc(s["sub"], 1)
                    if p == 0 and not first:
                        divide_dve(v, s, st, i - 1 + base)
                if not first:
                    tail(i - 1)
                if not last:
                    front_rope(i + 1)
                if not last:
                    v.wait_ge(s["av"], 2 * (i + base) + 2)
                    values_dve(v, s, st, i + 1, i + 1 + base)

            def ahead(i):
                front(i)
                front_rope(i)
                values_dve(v, s, st, i, i + base)

            v.wait_ge(N["xb"], 1 if st == 1 else 2)
            pipelined(v, ahead, body)
            divide_dve(v, s, st, NT - 1 + base)
            tail(NT - 1)

        def with_bias_pool(g, bias, step):
            g.tensor_tensor(Y[:], X[:], vbc[:, bias, :].unsqueeze(1).broadcast_to([P, NT, D]), ALU.add).then_inc(N["xb"], 1)

        def attention_pool(g, st):
            if st == 1:
                g.wait_ge(s_x, 16)
            norm_all_pool(g, N, 1 if st == 1 else 4)
            with_bias_pool(g, 0 if st == 1 else 1, 1)

        def zb(h, k):
            return Z[:, 4 * h + k, :]

        def tiles(bank):
            return bank.rearrange("p (t n) -> p t n", n=P)

        def stats_all(v, s, key, src):
            for t in range(NT):
                u = v.bn_stats(stats[:, t, :], src[:, t, :])
            u.then_inc(s["ast"], 1)
            v.wait_ge(s["ast"], key)
            for t in range(NT):
                u = v.bn_aggr(meanvar[:, t, :], stats[:, t, :])
            u.then_inc(s["amv"], 1)

        def norm_all(v, s, key, src, dst):
            stats_all(v, s, key, src)
            v.wait_ge(s["ars"], key)
            for t in range(NT):
                u = v.tensor_scalar(dst[:, t, :], src[:, t, :], meanvar[:, t, 0:1], rstd[:, t:t + 1], ALU.subtract, ALU.mult)
            u.then_inc(s["axn"], 1)
            v.wait_ge(s["axn"], {2: 1, 3: 2, 6: 3, 7: 4}[key])

        def norm_all_pool(g, s, key):
            g.wait_ge(s["amv"], key)
            g.tensor_tensor(veps[:], meanvar[:, :, 1], eps[:], ALU.add).then_inc(s["arv"], 1)
            g.wait_ge(s["arv"], key)
            g.tensor_tensor(rstd[:], veps[:], power[:], ALU.pow).then_inc(s["ars"], 1)

        def half_norm_dve(v, h, n, x):
            y = Y[:, 4 * h:4 * h + 4, :]
            for t in range(4):
                u = v.bn_stats(st2[h][:, t, :], y[:, t, :])
            u.then_inc(L["st" + x], 1)
            v.wait_ge(L["st" + x], n)
            v.memset(spacer[:], 0.0)
            for t in range(4):
                u = v.bn_aggr(mv2[h][:, t, :], st2[h][:, t, :])
            u.then_inc(L["mv" + x], 1)

        def half_scale_dve(v, h, n, x):
            y = Y[:, 4 * h:4 * h + 4, :]
            v.wait_ge(L["rs" + x], n)
            for t in range(4):
                u = v.tensor_scalar(xn2[h][:, t, :], y[:, t, :], mv2[h][:, t, 0:1], rs2[h][:, t:t + 1], ALU.subtract, ALU.mult)
            u.then_inc(L["xn" + x], 1)

        def half_norm_pool(g, h, n, x):
            g.wait_ge(L["mv" + x], n)
            g.tensor_tensor(ve2[h][:], mv2[h][:, :, 1], eps[:, 0:4], ALU.add).then_inc(L["rv" + x], 1)
            g.wait_ge(L["rv" + x], n)
            g.tensor_tensor(rs2[h][:], ve2[h][:], power[:, 0:4], ALU.pow).then_inc(L["rs" + x], 1)

        def layers_pool(g):
            norm_all_pool(g, N, 2)
            with g.Fori(0, DEPTH) as l:
                n = [2 * l + 1, 2 * l + 2]
                for h in range(2):
                    half_norm_pool(g, h, n[h], "")
                g.wait_ge(L["bo"], 16 * l + 16)
                for h in range(2):
                    y = Y[:, 4 * h:4 * h + 4, :]
                    g.wait_ge(L["xn"], n[h])
                    g.tensor_tensor(y, y, bo[:].unsqueeze(1).broadcast_to([P, 4, D]), ALU.add).then_inc(L["yb"], 1)
                for h in range(2):
                    half_norm_pool(g, h, n[h], "_")

        def nextnorm(l):
            return vcol[:, bass.ds(l + 1, 4, DEPTH)]

        def layers_dve(v):
            v.wait_ge(A["out"], NT)
            norm_all(v, N, 2, X, Y)
            norms = vcol[:, 0:4 * DEPTH].rearrange("p (k l) -> p k l", l=DEPTH)
            v.tensor_copy(lnp[:], norms[:, :, 0]).then_inc(L["lnp"], 1)
            with v.Fori(0, DEPTH) as l:
                n = [2 * l + 1, 2 * l + 2]
                for h in range(2):
                    half_norm_dve(v, h, n[h], "")
                for h in range(2):
                    half_scale_dve(v, h, n[h], "")
                for h in range(2):
                    v.wait_ge(L["qt"], n[h])
                    v.tensor_reduce(nqm[h][:].rearrange("p t h -> p (t h)"), zb(h, 1).rearrange("p (t d) -> p t d", d=LD), AX.X, ALU.max, negate=True)\
                        .then_inc(L["nq"], 1)
                    v.wait_ge(L["kt"], n[h])
                    v.tensor_reduce(nkm[h][:], zb(h, 3).rearrange("p (b s) -> p b s", s=S), AX.X, ALU.max, negate=True).then_inc(L["nk"], 1)
                for h in range(2):
                    v.wait_ge(L["nT"], n[h])
                    v.tensor_copy(nqT[h][:], zb(h, 1)[0:8, :])
                    v.tensor_copy(nkT[h][:], zb(h, 3)[0:8, 0:D]).then_inc(L["nTe"], 1)
                for h in range(2):
                    v.wait_ge(L["v"], n[h])
                    v.tensor_copy(vs[h][:].rearrange("p t n -> p (t n)"), zb(h, 1)).then_inc(L["vs"], 1)
                for h in range(2):
                    v.wait_ge(L["cx"], n[h])
                    v.reciprocal(rk[h][:], zb(h, 2)[:, 0:8]).then_inc(L["rk"], 1)
                    v.wait_ge(L["rk"], n[h])
                    for t in range(4):
                        for u in range(2):
                            w = v.scalar_tensor_tensor(out=ctxa[h][:, 2 * t + u, 0:D], in0=tiles(zb(h, (3, 1)[u]))[:, t, :],
                                                       scalar=rk[h][:, 2 * t + u:2 * t + u + 1], in1=const("headblock"),
                                                       op0=ALU.mult, op1=ALU.mult)
                    w.then_inc(L["ca"], 1)
                for h in range(2):
                    v.wait_ge(L["o"], n[h])
                    for k in range(2):
                        o = zb(h, 2 * k)[:, 0:2 * CA].rearrange("p (t c) -> p t c", c=CA)
                        w = v.reciprocal(rq[h][:, 2 * k:2 * k + 2, :], o[:, :, D:CA])
                    w.then_inc(L["rq"], 1)
                    v.wait_ge(L["rq"], n[h])
                    for k in range(2):
                        o = zb(h, 2 * k)[:, 0:2 * CA].rearrange("p (t c) -> p t c", c=CA)
                        w = v.tensor_tensor(aq[h][:, 2 * k:2 * k + 2, :].rearrange("p t (h d) -> p t h d", d=LD),
                                            o[:, :, 0:D].rearrange("p t (h d) -> p t h d", d=LD),
                                            rq[h][:, 2 * k:2 * k + 2, :].unsqueeze(3).broadcast_to([P, 2, LH, LD]), ALU.mult)
                    w.then_inc(L["aq"], 1)
                for h in range(2):
                    y = Y[:, 4 * h:4 * h + 4, :].rearrange("p t n -> p (t n)")
                    v.wait_ge(L["yb"], n[h])
                    v.wait_ge(L["wo_"], n[h])
                    v.tensor_tensor(y, zb(h, 3), y, ALU.add).then_inc(L["y"], 1)
                    v.wait_ge(L["y"], n[h])
                    half_norm_dve(v, h, n[h], "_")
                for h in range(2):
                    half_scale_dve(v, h, n[h], "_")
                for h in range(2):
                    for c in range(FC):
                        v.wait_ge(L["hs"], 8 * l + 4 * h + c + 1)
                        v.tensor_tensor(hT[h][:, c, :], zb(h, (c + 1) % 4), hs[h][:, c, :], ALU.max).then_inc(L["hT"], 1)
                for h in range(2):
                    y = Y[:, 4 * h:4 * h + 4, :].rearrange("p t n -> p (t n)")
                    v.wait_ge(L["w2_"], n[h])
                    v.tensor_tensor(y, zb(h, 1), y, ALU.add).then_inc(L["y2"], 1)
                    v.wait_ge(L["y2"], n[h])
                v.tensor_copy(lnp[:], nextnorm(l)).then_inc(L["lnp"], 1)
            v.tensor_tensor(X[:], X[:], Y[:], ALU.add).then_inc(L["out"], 1)
            v.wait_ge(L["out"], 1)

        def layers_act(act):
            with act.Fori(0, DEPTH) as l:
                n = [2 * l + 1, 2 * l + 2]
                act.wait_ge(L["lnp"], nth(l))
                for h in range(2):
                    act.wait_ge(L["T"], n[h])
                    act.activation(xT2[h][:], zb(h, 0), ACT.Identity, scale=lnp[:, 0:1], bias=lnp[:, 1:2]).then_inc(L["xT"], 1)
                for h in range(2):
                    act.wait_ge(L["v"], n[h])
                    act.activation(eqT[h][:], zb(h, 2), ACT.Exp).then_inc(L["eq"], 1)
                    act.activation(ek[h][:].rearrange("p t n -> p (t n)"), zb(h, 0), ACT.Exp).then_inc(L["ek"], 1)
                for h in range(2):
                    act.wait_ge(L["aqT"], n[h])
                    act.activation(aT[h][:], zb(h, 1), ACT.Identity).then_inc(L["aqTe"], 1)
                for h in range(2):
                    act.wait_ge(L["T_"], n[h])
                    act.activation(xT2[h][:], zb(h, 0), ACT.Identity, scale=lnp[:, 2:3], bias=lnp[:, 3:4]).then_inc(L["xT_"], 1)
                for h in range(2):
                    for c in range(FC):
                        act.wait_ge(L["h1"], 8 * l + 4 * h + c + 1)
                        act.activation(hs[h][:, c, :], zb(h, (c + 1) % 4), ACT.Identity, scale=0.01).then_inc(L["hs"], 1)

        def layers_pe(pe):
            def transposes(h, src, bank):
                for t in range(4):
                    w = pe.transpose(tiles(zb(h, bank))[:, t, :], src[h][:, t, :], ident)
                return w

            def xtile(h, t):
                return xT2[h][:, t * P:(t + 1) * P]

            with pe.Fori(0, DEPTH) as l:
                n = [2 * l + 1, 2 * l + 2]
                for h in range(2):
                    pe.wait_ge(L["xn"], n[h])
                    transposes(h, xn2, 0).then_inc(L["T"], 1)
                pe.wait_ge(L["w"], 32 * l + 32)
                for h in range(2):
                    pe.wait_ge(L["xT"], n[h])
                    for t in range(4):
                        w = pe.matmul(tiles(zb(h, 1))[:, t, :], xtile(h, t), wq[:], start=True, stop=True)
                    w.then_inc(L["qt"], 1)
                    pe.matmul(zb(h, 3), wk[:], xT2[h][:], start=True, stop=True).then_inc(L["kt"], 1)
                    pe.matmul(zb(h, 2), wq[:], xT2[h][:], start=True, stop=False, skip_group_check=True)
                    for t in range(4):
                        w = pe.matmul(tiles(zb(h, 0))[:, t, :], xtile(h, t), wk[:], start=(t == 0), stop=False, skip_group_check=True)
                    w.then_inc(L["qk"], 1)
                for h in range(2):
                    pe.wait_ge(L["nq"], n[h])
                    for t in range(4):
                        pe.transpose(tiles(zb(h, 1))[0:8, t, :], nqm[h][:, t, :], ident)
                    pe.wait_ge(L["nk"], n[h])
                    pe.transpose(zb(h, 3)[0:8, 0:P], nkm[h][:], ident).then_inc(L["nT"], 1)
                pe.wait_ge(L["wv"], 16 * l + 16)
                for h in range(2):
                    pe.wait_ge(L["nTe"], n[h])
                    pe.matmul(zb(h, 2), const("qsel", BF16)[0:8, :], nqT[h][:], start=False, stop=True, skip_group_check=True)
                    for t in range(4):
                        pe.matmul(tiles(zb(h, 0))[:, t, :], const("ksel", BF16)[0:8, t * P:(t + 1) * P], nkT[h][:],
                                  start=False, stop=True, skip_group_check=True)
                    for t in range(4):
                        w = pe.matmul(tiles(zb(h, 1))[:, t, :], xtile(h, t), wv[:], start=True, stop=True)
                    w.then_inc(L["v"], 1)
                for h in range(2):
                    pe.wait_ge(L["ek"], n[h])
                    pe.wait_ge(L["vs"], n[h])
                    for t in range(4):
                        for u in range(2):
                            rows = slice(u * S, (u + 1) * S)
                            pe.matmul(tiles(zb(h, (3, 1)[u]))[:, t, :], ek[h][rows, t, :], vs[h][rows, t, :], start=True, stop=True)
                    for t in range(4):
                        w = pe.matmul(zb(h, 2)[:, 2 * t:2 * t + 2], ek[h][:, t, :], const("tokhalf"), start=True, stop=True)
                    w.then_inc(L["cx"], 1)
                for h in range(2):
                    pe.wait_ge(L["ca"], n[h])
                    for t in range(4):
                        for u in range(2):
                            w = pe.matmul(zb(h, 2 * (t // 2))[u * S:(u + 1) * S, (t % 2) * CA:(t % 2 + 1) * CA],
                                          eqT[h][:, (2 * t + u) * S:(2 * t + u + 1) * S], ctxa[h][:, 2 * t + u, :], start=True, stop=True)
                    w.then_inc(L["o"], 1)
                for h in range(2):
                    pe.wait_ge(L["aq"], n[h])
                    transposes(h, aq, 1).then_inc(L["aqT"], 1)
                pe.wait_ge(L["wo"], 16 * l + 16)
                for h in range(2):
                    pe.wait_ge(L["aqTe"], n[h])
                    for t in range(4):
                        w = pe.matmul(tiles(zb(h, 3))[:, t, :], aT[h][:, t * P:(t + 1) * P], wo[:], start=True, stop=True)
                    w.then_inc(L["wo_"], 1)
                for h in range(2):
                    pe.wait_ge(L["xn_"], n[h])
                    transposes(h, xn2, 0).then_inc(L["T_"], 1)
                pe.wait_ge(L["w1"], 16 * l + 16)
                for h in range(2):
                    pe.wait_ge(L["xT_"], n[h])
                    for c in range(FC):
                        w = pe.matmul(zb(h, (c + 1) % 4), w1[:, c * P:(c + 1) * P], xT2[h][:], start=True, stop=True).then_inc(L["h1"], 1)
                pe.wait_ge(L["w2"], 16 * l + 16)
                for h in range(2):
                    pe.wait_ge(L["hT"], 8 * l + 4 * h + 4)
                    for t in range(4):
                        for c in range(FC):
                            w = pe.matmul(tiles(zb(h, 1))[:, t, :], hT[h][:, c, t * P:(t + 1) * P], w2[:, c, :],
                                          start=(c == 0), stop=(c == FC - 1))
                    w.then_inc(L["w2_"], 1)

        def chain(v, sem_):
            count = [0]

            def link(ins):
                count[0] += 1
                ins.then_inc(sem_, 1)
                v.wait_ge(sem_, count[0])

            return link

        def per_token(t):
            return t[:].unsqueeze(2).broadcast_to([P, NT, E])

        iota = const("iota").unsqueeze(1).broadcast_to([P, NT, E])

        def first_of(v, link, onehot, values, top):
            link(v.tensor_tensor(r1[:], values[:], per_token(top), ALU.is_equal))
            link(v.tensor_scalar(r1[:], r1[:], -float(E), None, ALU.mult))
            link(v.tensor_tensor(r1[:], r1[:], iota, ALU.add))
            link(v.tensor_reduce(m4[:], r1[:], AX.X, ALU.min))
            link(v.tensor_scalar(m4[:], m4[:], float(E), None, ALU.add))
            link(v.tensor_tensor(onehot[:], iota, per_token(m4), ALU.is_equal))

        def router_pe(pe, s, which):
            pe.wait_ge(N["axn"], (2, 4)[which])
            for t in range(NT):
                w = pe.transpose(Z[:, t // 4, (t % 4) * P:(t % 4 + 1) * P], Y[:, t, :], ident)
            w.then_inc(s["T"], 1)
            pe.wait_ge(s["tT"], 1)
            for t in range(NT):
                w = pe.matmul(Z[:, 2, t * E:(t + 1) * E], tT[:, t * P:(t + 1) * P], wr[:, which, :], start=True, stop=True)
            w.then_inc(s["lg"], 1)

        def router_act(act, s):
            act.wait_ge(s["T"], 1)
            act.activation(tT[:], Z[:, 0:2, :].rearrange("p a b -> p (a b)"), ACT.Identity).then_inc(s["tT"], 1)
            act.wait_ge(s["d"], 1)
            if s is M3:
                act.activation(r2[:], r1[:], ACT.Exp).then_inc(s["ex"], 1)
            else:
                act.activation(m3[:], m3[:], ACT.Exp).then_inc(s["ex"], 1)

        def moe_dve(v):
            v.wait_ge(L["out"], 1)
            norm_all(v, N, 3, X, Y)
            link = chain(v, M3["r"])
            v.wait_ge(M3["lg"], 1)
            link(v.tensor_copy(lg[:].rearrange("p t e -> p (t e)"), Z[:, 2, 0:NT * E]))
            link(v.tensor_reduce(m1[:], lg[:], AX.X, ALU.max))
            v.tensor_tensor(r1[:], lg[:], per_token(m1), ALU.subtract).then_inc(M3["d"], 1)
            v.wait_ge(M3["ex"], 1)
            link(v.tensor_reduce(m1[:], r2[:], AX.X, ALU.add))
            link(v.reciprocal(m2[:], m1[:]))
            link(v.tensor_tensor(r2[:], r2[:], per_token(m2), ALU.mult))
            link(v.tensor_reduce(m3[:], r2[:], AX.X, ALU.max))
            first_of(v, link, oh, r2, m3)
            v.tensor_copy(ohb[:], oh[:]).then_inc(M3["p"], 1)
            link(v.tensor_scalar(m4[:], m4[:], float(CAP), -1.0, ALU.mult, ALU.add))
            v.wait_ge(M3["cum"], 1)
            link(v.tensor_tensor(r1[:], Z[:, 3, 0:NT * E].rearrange("p (t e) -> p t e", e=E), oh[:], ALU.mult))
            link(v.tensor_reduce(m1[:], r1[:], AX.X, ALU.add))
            link(v.tensor_scalar(keep[:], m1[:], float(CAP), None, ALU.is_le))
            link(v.tensor_tensor(m1[:], m1[:], m4[:], ALU.add))
            link(v.tensor_tensor(m1[:], m1[:], const("past"), ALU.subtract))
            link(v.tensor_tensor(m1[:], m1[:], keep[:], ALU.mult))
            link(v.tensor_tensor(place[:], m1[:], const("past"), ALU.add))
            v.tensor_copy(placei[:], place[:]).then_inc(M3["place"], 1)
            link(v.tensor_scalar(m2[:], keep[:], -1.0, 1.0, ALU.mult, ALU.add))
            link(v.tensor_tensor(m1[:], m3[:], keep[:], ALU.mult))
            link(v.tensor_tensor(factor[:], m1[:], m2[:], ALU.add))

            with v.Fori(0, E // QE) as q:
                for k in range(QE):
                    v.wait_ge(M3["o"], q * QE + k + 1)
                    v.tensor_scalar(resT[:, bass.ds(q * (QE * CAP) + k * CAP, CAP)], Z[:, 4 + k % 2, 0:CAP], 1.0, None, ALU.mult)\
                        .then_inc(M3["res"], 1)
            v.wait_ge(M3["rT"], 2)
            v.tensor_copy(slot[:, 5:SLOTS, :].rearrange("p s n -> p (s n)")[:, 0:4 * P], Z[:, 6, :])
            v.tensor_copy(slot[:, 9:SLOTS, :].rearrange("p s n -> p (s n)"), Z[:, 7, 0:P]).then_inc(M3["rTe"], 1)
            v.wait_ge(M3["back"], 16 * NT)
            for t in range(NT):
                w = v.scalar_tensor_tensor(out=X[:, t, :], in0=acc[:, t, :], scalar=factor[:, t:t + 1], in1=X[:, t, :],
                                           op0=ALU.mult, op1=ALU.add)
            w.then_inc(M3["out"], 1)
            v.wait_ge(M3["out"], 1)

        def moe_act(act):
            router_act(act, M3)
            act.wait_ge(M3["sT"], 1)
            act.activation(slotT[:, 0:8 * P], Z[:, 0:2, :].rearrange("p a b -> p (a b)"), ACT.Identity).then_inc(M3["slotT"], 1)
            act.activation(slotT[:, 8 * P:SLOTS * P], Z[:, 2, 0:(SLOTS - 8) * P], ACT.Identity).then_inc(M3["slotT"], 1)
            with act.Fori(0, E // QE) as q:
                for k in range(QE):
                    act.wait_ge(M3["h"], q * QE + k + 1)
                    act.activation(hT[k % 2][:, :, 0:CAP].rearrange("p (a b) n -> p a b n", a=2),
                                   Z[:, 2 * (k % 2):2 * (k % 2) + 2, 0:2 * CAP].rearrange("p a (b n) -> p a b n", b=2), ACT.Relu)\
                        .then_inc(M3["hT"], 1)
            act.wait_ge(M3["rT"], 1)
            act.activation(slot[:, 0:4, :].rearrange("p s n -> p (s n)"), Z[:, 0, :], ACT.Identity)
            act.activation(slot[:, 4, :], Z[:, 1, 0:P], ACT.Identity).then_inc(M3["rTe"], 1)

        def moe_pool(g):
            norm_all_pool(g, N, 3)
            g.wait_ge(s_clear, 48)
            g.wait_ge(M3["place"], 1)
            for t in range(NT):
                g.indirect_dma_start(a["slots"], bass.IndirectOffsetOnAxis(placei[:, t:t + 1], 0), Y[:, t, :], None).then_inc(M3["there"], 16)
            g.wait_ge(M3["stored"], 16)
            for t in range(NT):
                g.indirect_dma_start(acc[:, t, :], None, a["slots"], bass.IndirectOffsetOnAxis(placei[:, t:t + 1], 0)).then_inc(M3["back"], 16)

        def moe_pe(pe):
            router_pe(pe, M3, 0)
            pe.wait_ge(M3["p"], 1)
            flat = ohb[:].rearrange("p t e -> p (t e)")
            pe.matmul(Z[:, 3, 0:NT * E], const("tri", BF16), flat, start=True, stop=False, skip_group_check=True)
            for t in range(NT - 1):
                w = pe.matmul(Z[:, 3, (t + 1) * E:NT * E].rearrange("p (t e) -> p t e", e=E), const("ones", BF16),
                              ohb[:, t:t + 1, :].broadcast_to([P, NT - 1 - t, E]), start=False, stop=(t == NT - 2), skip_group_check=True)
            w.then_inc(M3["cum"], 1)
            pe.wait_ge(M3["slots"], 16)
            for k in range(SLOTS):
                w = pe.transpose(Z[:, k // 4, (k % 4) * P:(k % 4 + 1) * P], slot[:, k, :], ident)
            w.then_inc(M3["sT"], 1)
            pe.wait_ge(M3["slotT"], 2)

            def hidden(q, k):
                if k % 2 == 0:
                    pe.wait_ge(M3["w1" + "ab"[k // 2]], q * 32 + 32)
                for c in range(FC):
                    w = pe.matmul(Z[:, 2 * (k % 2) + c // 2, (c % 2) * CAP:(c % 2 + 1) * CAP], xw1[k][:, c * P:(c + 1) * P],
                                  slotT[:, bass.ds(q * (QE * CAP) + k * CAP, CAP)], start=True, stop=True, skip_group_check=True)
                w.then_inc(M3["h"], 1)

            def result(q, k, first):
                if k % 2 == 0:
                    pe.wait_ge(M3["w2" + "ab"[k // 2]], q * 32 + 32)
                if not first or k >= 2:
                    pe.wait_ge(M3["res"], q * QE + k - 1)
                pe.wait_ge(M3["hT"], q * QE + k + 1)
                for c in range(FC):
                    w = pe.matmul(Z[:, 4 + k % 2, 0:CAP], xw2[k][:, c, :], hT[k % 2][:, c, 0:CAP], start=(c == 0), stop=(c == FC - 1))
                w.then_inc(M3["o"], 1)

            def four(q, first):
                hidden(q, 0)
                for k in range(QE):
                    if k + 1 < QE:
                        hidden(q, k + 1)
                    result(q, k, first)

            peeled(pe, E // QE, four)
            pe.wait_ge(M3["res"], E)
            for half, banks in enumerate(((0, 1), (6, 7))):
                for k in range(5):
                    w = pe.transpose(Z[:, banks[k // 4], (k % 4) * P:(k % 4 + 1) * P], resT[:, (5 * half + k) * P:(5 * half + k + 1) * P], ident)
                w.then_inc(M3["rT"], 1)

        def linear_act(act):
            s = C5

            def front_T(i):
                act.wait_ge(s["T"], nth(i))
                act.activation(xcT[:, 0:2, :].rearrange("p b (r s) -> p b r s", r=2),
                               Z[:, 0, 0:P].rearrange("p (b s) -> p b s", b=2).unsqueeze(2).broadcast_to([P, 2, 2, S]), ACT.Identity).then_inc(s["xT"], 1)

            def front_exp(i):
                act.wait_ge(s["fm"], nth(i))
                act.activation(fm[:], fm[:], ACT.Exp).then_inc(s["fe"], 1)

            def front_k(i):
                act.wait_ge(s["ff"], nth(i))
                for j in range(2):
                    t = act.activation(kview(1).rearrange("p b (j k) -> p b j k", j=2)[:, :, j, :],
                                       qk[:, P:2 * P].rearrange("p (b s) -> p b s", b=2), ACT.Identity, scale=const("kpair")[:, j:j + 1])
                t.then_inc(s["ke"], 1)

            def ahead(i):
                front_T(i)
                front_exp(i)
                front_k(i)

            def body(i, first, last):
                if not last:
                    ahead(i + 1)
                act.wait_ge(M6["wt"], nth(i))
                act.activation(woutT, Z[:, 3, :].rearrange("p (c n) -> p c n", n=D), ACT.Identity).then_inc(M6["wT"], 1)
                sums_act(act, s, 5, i)

            pipelined(act, ahead, body)

        def linear_pe(pe):
            s = C5

            def front_T(i):
                if not isinstance(i, int) or i > 0:
                    pe.wait_ge(s["va"], i)
                pe.wait_ge(s["xn"], nth(i))
                pe.transpose(Z[:, 0, 0:P], xn[:], ident).then_inc(s["T"], 1)

            def front_qkv(i):
                pe.wait_ge(s["xT"], nth(i))
                for k in range(2):
                    w = pe.matmul(Z[:, 1, k * P:(k + 1) * P], wT[:, 6 + k, :], xcT[:, 0:2, 0:S], start=True, stop=True)
                w.then_inc(s["qk"], 1)
                for b in range(2):
                    w = pe.matmul(Z[:, 0, b * D:(b + 1) * D], xcT[:, b, :], wT[:, 8, :], start=True, stop=True)
                w.then_inc(s["v"], 1)

            def tail_y(i):
                pe.wait_ge(s["att"], nth(i))
                out_projection(pe, 2).then_inc(s["y"], 1)

            def body(i, first, last):
                pe.wait_ge(s["ke"], nth(i))
                if not first:
                    pe.wait_ge(M6["wT"], i)
                pe.wait_ge(s["qx"], nth(i))
                for gg in range(4):
                    rows = slice(32 * gg, 32 * gg + 32)
                    for b in range(2):
                        w = pe.matmul(Z[:, 3 + gg, b * P:(b + 1) * P], kview(1)[rows, b, :], qe[rows, b].rearrange("p j q -> p (j q)"),
                                      start=True, stop=True, skip_group_check=True)
                    if gg % 2:
                        w.then_inc(s["s"], 1)
                if not last:
                    front_T(i + 1)
                if not last:
                    front_qkv(i + 1)
                if not first:
                    tail_y(i - 1)
                pe.wait_ge(s["pm"], 2 * i + 2)
                if not first:
                    expert_product(pe, i - 1)
                expert_transposes(pe, i)
                pe.wait_ge(s["va"], nth(i))
                for p in range(2):
                    if p == 1 and not first:
                        pe.wait_ge(s["bo"], i)
                    pe.wait_ge(s["pm"], 2 * i + p + 1)
                    sums_pe(pe, 5, p, sc[p]).then_inc(s["av"], 1)

            def ahead(i):
                front_T(i)
                front_qkv(i)

            pipelined(pe, ahead, body)
            tail_y(NT - 1)
            expert_product(pe, E - 1)

        def expert_transposes(pe, e):
            pe.wait_ge(M6["wout"], nth(e, 16))
            for c in range(FC):
                w = pe.transpose(Z[:, 3, c * P:(c + 1) * P], we2[:].rearrange("p c n -> p (c n)")[:, c * P:(c + 1) * P], ident)
            w.then_inc(M6["wt"], 1)

        def expert_product(pe, e):
            pe.wait_ge(M6["win"], nth(e, 16))
            pe.wait_ge(M6["wT"], nth(e))
            for c in range(FC):
                w = pe.matmul(Z[:, 5, 0:D], we1[:, c * P:(c + 1) * P], woutT[:, c, :], start=(c == 0), stop=(c == FC - 1))
            w.then_inc(M6["m"], 1)

        def linear_dve(v):
            s = C5
            v.wait_ge(A["out"], 2 * NT)
            stats_all(v, N, 5, X)
            v.wait_ge(N["ars"], 5)

            def front(i):
                if not isinstance(i, int) or i > 0:
                    v.wait_ge(s["T"], i)
                scale_tile(v, s, i, i)

            def front_qk(i):
                v.wait_ge(s["qk"], nth(i))
                for k in range(2):
                    bias = vcol[:, 26 + k:27 + k]
                    w = v.tensor_scalar(fm[:, k * P:(k + 1) * P], Z[:, 1, k * P:(k + 1) * P], bias, 0.0, ALU.add, ALU.min)
                w.then_inc(s["fm"], 1)
                for k in range(2):
                    bias = vcol[:, 26 + k:27 + k]
                    w = v.tensor_scalar(fr[:, k * P:(k + 1) * P], Z[:, 1, k * P:(k + 1) * P], bias, 0.0, ALU.add, ALU.max)
                w.then_inc(s["fr"], 1)

            def take_product(e):
                v.wait_ge(M6["m"], nth(e))
                v.tensor_scalar(wc[:, bass.ds(e, 1), :].rearrange("p a n -> p (a n)"), Z[:, 5, 0:D], 1.0, None, ALU.mult)\
                    .then_inc(M6["wc"], 1)

            def front_features(i):
                v.wait_ge(s["fr"], nth(i))
                v.wait_ge(s["fe"], nth(i))
                v.scalar_tensor_tensor(out=qk[:], in0=fm[:], scalar=FEAT_EPS, in1=fr[:], op0=ALU.add, op1=ALU.add).then_inc(s["ff"], 1)

            def tail(i):
                v.wait_ge(s["y"], nth(i))
                v.tensor_tensor(tile_of(acc, i), Z[:, 7, 0:D], vbc[:, 2, :], ALU.add).then_inc(s["bo"], 1)

            def body(i, first, last):
                if not last:
                    front(i + 1)
                for p in range(2):
                    v.wait_ge(s["s"], 2 * i + p + 1)
                    v.tensor_tensor(sc[p][:].rearrange("p r k -> p (r k)")[:, 0:8 * S].rearrange("p (g j q) -> p g j q", g=2, j=4),
                                    Z[:, 3 + 2 * p:5 + 2 * p, 0:4 * S].rearrange("p g (j q) -> p g j q", j=4),
                                    const("mask01").unsqueeze(1).unsqueeze(1).broadcast_to([P, 2, 4, S]), ALU.mult).then_inc(s["pm"], 1)
                    if p == 0 and not first:
                        divide_dve(v, s, 5, i - 1)
                if not first:
                    tail(i - 1)
                if not last:
                    front_qk(i + 1)
                if not first:
                    take_product(i - 1)
                if not last:
                    front_features(i + 1)
                if not last:
                    v.wait_ge(s["av"], 2 * i + 2)
                    values_dve(v, s, 5, i + 1, i + 1)

            def ahead(i):
                front(i)
                front_qk(i)
                front_features(i)
                values_dve(v, s, 5, i, i)

            pipelined(v, ahead, body)
            divide_dve(v, s, 5, NT - 1)
            tail(NT - 1)
            take_product(E - 1)
            v.wait_ge(s["bo"], NT)
            norm_all(v, N, 6, acc, Y)
            v.tensor_tensor(Y[:], Y[:], vbc[:, 3, :].unsqueeze(1).broadcast_to([P, NT, D]), ALU.mult).then_inc(s["g"], 1)
            v.wait_ge(s["xb"], 1)
            v.wait_ge(s["g"], 1)
            v.tensor_tensor(X[:], Y[:], X[:], ALU.add).then_inc(s["out"], 1)
            v.wait_ge(s["out"], 1)

        def linear_pool(g):
            s = C5
            norm_all_pool(g, N, 5)
            with g.Fori(0, NT) as i:
                g.wait_ge(s["ff"], nth(i))
                g.tensor_tensor(qe[:], qk[:, 0:P].rearrange("p (b q) -> p b q", b=2).unsqueeze(2).broadcast_to([P, 2, 2, S]),
                                const("qpar").unsqueeze(1).unsqueeze(3).broadcast_to([P, 2, 2, S]), ALU.mult).then_inc(s["qx"], 1)
            g.wait_ge(s["xn"], NT)
            g.tensor_tensor(X[:], X[:], vbc[:, 4, :].unsqueeze(1).broadcast_to([P, NT, D]), ALU.add).then_inc(s["xb"], 1)
            norm_all_pool(g, N, 6)

        def moe6_pe(pe):
            pe.wait_ge(C5["out"], 1)
            pe.wait_ge(M6["wc"], E)
            router_pe(pe, M6, 1)
            for t in range(NT):
                if t == 1:
                    pe.wait_ge(M6["r"], 1)
                if t >= 4:
                    pe.wait_ge(M6["acc"], E * (t - 3))
                for k in range(2):
                    w = pe.matmul(Z[:, 2 * (t % 4) + k, :], tT[:, t * P:(t + 1) * P],
                                  wc[:, 4 * k:4 * k + 4, :], start=True, stop=True)
                w.then_inc(M6["o"], 1)

        def moe6_act(act):
            router_act(act, M6)

        def moe6_pool(g):
            norm_all_pool(g, N, 7)

        def moe6_dve(v):
            v.wait_ge(C5["out"], 1)
            norm_all(v, N, 7, X, Y)
            link = chain(v, M6["r"])
            v.wait_ge(M6["lg"], 1)
            link(v.tensor_copy(lg[:].rearrange("p t e -> p (t e)"), Z[:, 2, 0:NT * E]))
            link(v.tensor_reduce(m1[:], lg[:], AX.X, ALU.max))
            first_of(v, link, oh, lg, m1)
            link(v.tensor_scalar(r2[:], oh[:], NEG, None, ALU.mult))
            link(v.tensor_tensor(lg[:], lg[:], r2[:], ALU.add))
            link(v.tensor_reduce(m2[:], lg[:], AX.X, ALU.max))
            first_of(v, link, oh2, lg, m2)
            v.tensor_tensor(m3[:], m2[:], m1[:], ALU.subtract).then_inc(M6["d"], 1)
            v.wait_ge(M6["ex"], 1)
            link(v.tensor_scalar(m1[:], m3[:], 1.0, None, ALU.add))
            link(v.reciprocal(m1[:], m1[:]))
            link(v.tensor_tensor(m2[:], m3[:], m1[:], ALU.mult))
            link(v.tensor_tensor(oh[:], oh[:], per_token(m1), ALU.mult))
            link(v.tensor_tensor(oh2[:], oh2[:], per_token(m2), ALU.mult))
            link(v.tensor_tensor(gate[:].rearrange("p e t -> p t e"), oh[:], oh2[:], ALU.add))
            done = 0
            for t in range(NT):
                v.wait_ge(M6["o"], t + 1)
                for e in range(E):
                    v.scalar_tensor_tensor(out=X[:, t, :], in0=Z[:, 2 * (t % 4) + e // 4, (e % 4) * P:(e % 4 + 1) * P],
                                           scalar=gate[:, e, t:t + 1], in1=X[:, t, :], op0=ALU.mult, op1=ALU.add).then_inc(M6["acc"], 1)
                    done += 1
                    v.wait_ge(M6["acc"], done)
            v.memset(spacer[:], 0.0).then_inc(M6["out"], 1)

        def layers_load(sp):
            def load(l, first):
                def of(name):
                    return a[name][bass.ds(l, 1)].rearrange("l p n -> (l p) n")

                def read(name, each=2):
                    if not first:
                        sp.wait_ge(L[name], each * l)

                read("qk")
                sp.dma_start(wq[:], of("L0_attn_wq")).then_inc(L["w"], 16)
                sp.dma_start(wk[:], of("L0_attn_wk")).then_inc(L["w"], 16)
                read("v")
                sp.dma_start(wv[:], of("L0_attn_wv")).then_inc(L["wv"], 16)
                read("yb")
                sp.dma_start(bo[:], a["L0_attn_bo"][bass.ds(l, 1)].rearrange("l n -> (l n)").partition_broadcast(P)).then_inc(L["bo"], 16)
                read("wo_")
                sp.dma_start(wo[:], of("L0_attn_wo")).then_inc(L["wo"], 16)
                read("h1", 8)
                sp.dma_start(w1[:], of("L0_attn_w1")).then_inc(L["w1"], 16)
                read("w2_")
                sp.dma_start(w2[:], a["L0_attn_w2"].rearrange("l (c p) n -> l p c n", p=P)[bass.ds(l, 1)]
                             .rearrange("l p c n -> (l p) c n")).then_inc(L["w2"], 16)

            peeled(sp, DEPTH, load)

        def experts_load(sp, q, first):
            for k in range(QE):
                if not first:
                    sp.wait_ge(M3["h"], (q - 1) * QE + k + 1)
                sp.dma_start(xw1[k][:], a["L0_ffn_W1"][q * QE + k]).then_inc(M3["w1" + "ab"[k // 2]], 16)
                if not first:
                    sp.wait_ge(M3["o"], (q - 1) * QE + k + 1)
                sp.dma_start(xw2[k][:], a["L0_ffn_W2"][q * QE + k].rearrange("(c p) n -> p c n", p=P)).then_inc(M3["w2" + "ab"[k // 2]], 16)

        @block.sync
        def _(sp):
            sp.dma_start(C[:], a["const"]).then_inc(s_tab, 16)
            sp.dma_start(X[:], x_d).then_inc(s_x, 16)
            n = 0
            for name in ("L0_xattn_Wq", "L0_xattn_Wk", "L0_xattn_Wv", "L1_xattn_Wq", "L1_xattn_Wk", "L1_xattn_Wv"):
                sp.dma_start(wraw[:, n, :], a[name]).then_inc(s_const, 16)
                n += 1
            sp.dma_start(wraw[:, 6:9, :], a["L1_attn_Wqkv"].rearrange("(c p) n -> p c n", p=P)).then_inc(s_const, 16)
            for k, name in enumerate(("L0_xattn_Wo", "L1_xattn_Wo", "L1_attn_Wout")):
                sp.dma_start(wraw[:, 9 + k, :], a[name]).then_inc(s_const, 16)
            for st in (1, 4):
                if st == 4 and stages >= 3:
                    sp.wait_ge(M3["there"], 16 * NT)
                    sp.dma_start(slot[:], slots_d).then_inc(M3["slots"], 16)
                    experts_load(sp, 1, False)
                    sp.wait_ge(M3["rTe"], 2)
                    sp.dma_start(slots_d, slot[:]).then_inc(M3["stored"], 16)
                if stages < st:
                    continue
                def load(i, first):
                    if not first or st == 4:
                        sp.wait_ge(A["ctxT"], i if st == 1 else i + NT)
                    if st == 1:
                        for hf in range(2):
                            sp.dma_start(ctxbuf[hf * S:(hf + 1) * S], ctx_d[0:S, bass.ds(2 * i, 2), :]).then_inc(A["ctx"], 16)
                    else:
                        sp.dma_start(ctxbuf[:], ctx_d[:, bass.ds(2 * i, 2), :]).then_inc(A["ctx4"], 16)

                peeled(sp, NT, load)
                if st == 1 and stages >= 3:
                    sp.wait_ge(s_zero, 3)
                    sp.dma_start(slots_d[:, 0:NT, :], acc[:]).then_inc(s_clear, 16)
                    sp.dma_start(slots_d[:, NT:SLOTS, :], acc[:, 0:SLOTS - NT, :]).then_inc(s_clear, 16)
                    sp.dma_start(a["slots"][E * CAP:E * CAP + B * S].rearrange("(s p) n -> p s n", p=P), acc[:]).then_inc(s_clear, 16)
                    experts_load(sp, 0, True)
                if st == 1 and stages >= 2:
                    layers_load(sp)
            if stages >= 6:
                def load(e, first):
                    if not first:
                        sp.wait_ge(M6["wt"], e)
                    sp.dma_start(we2[:].rearrange("p c n -> p (c n)"), a["L1_ffn_w_out"][bass.ds(e, 1)]
                                 .rearrange("e p n -> (e p) n")).then_inc(M6["wout"], 16)
                    if not first:
                        sp.wait_ge(M6["m"], e)
                    sp.dma_start(we1[:].rearrange("p (c n) -> p c n", c=FC), a["L1_ffn_w_in"].rearrange("e (c p) n -> e p c n", p=P)
                                 [bass.ds(e, 1)].rearrange("e p c n -> (e p) c n")).then_inc(M6["win"], 16)

                peeled(sp, E, load)
            last = {1: (A["out"], NT), 2: (L["out"], 1), 3: (M3["out"], 1), 4: (A["out"], 2 * NT),
                    5: (C5["out"], 1), 6: (M6["out"], 1)}[stages]
            sp.wait_ge(*last)
            sp.dma_start(out_d, X[:]).then_inc(s_out, 16)
            sp.wait_ge(s_out, 16)

        @block.scalar
        def _(act):
            for k, name in enumerate(("L0_attn_ln1_w", "L0_attn_ln1_b", "L0_attn_ln2_w", "L0_attn_ln2_b")):
                act.dma_start(vrow[6 * k:6 * k + 6, :], a[name]).then_inc(s_vec, 16)
            act.dma_start(vrow[24:25, :], a["L1_xattn_bq"].unsqueeze(0)).then_inc(s_vec, 16)
            act.dma_start(vrow[25:26, :], a["L1_xattn_bk"].unsqueeze(0)).then_inc(s_vec, 16)
            act.dma_start(vrow[26:29, :], a["L1_attn_bqkv"].rearrange("(c n) -> c n", n=P)).then_inc(s_vec, 16)
            act.dma_start(vrow[29:32, :], a["L1_attn_bqkv"].rearrange("(c n) -> c n", n=P)).then_inc(s_vec, 16)
            act.dma_start(brow[:, 0, :], a["L0_xattn_bq"].unsqueeze(0)).then_inc(s_vec, 16)
            act.dma_start(brow[:, 1, :], a["L0_xattn_bk"].unsqueeze(0)).then_inc(s_vec, 16)
            for k, v in enumerate((a["L0_xattn_bo"], a["L1_xattn_bo"], a["L1_attn_bout"], a["L1_attn_gamma"], a["L1_attn_beta"])):
                act.dma_start(vbc[:, k, :], v.partition_broadcast(P)).then_inc(s_vec, 16)
            for k, v in enumerate((a["L0_xattn_bv"], a["L1_xattn_bv"], a["L1_attn_bqkv"][2 * D:3 * D])):
                for b in range(2):
                    act.dma_start(vbd[:, k, b * D:(b + 1) * D], v.partition_broadcast(P)).then_inc(s_vec, 16)
            act.dma_start(wr[:, 0, :], a["L0_ffn_Wr"]).then_inc(s_vec, 16)
            act.dma_start(wgraw[:], a["L1_ffn_w_gate"]).then_inc(s_vec, 16)
            attention_act(act, 1)
            if stages >= 2:
                layers_act(act)
            if stages >= 3:
                moe_act(act)
            if stages >= 4:
                attention_act(act, 4)
            if stages >= 5:
                linear_act(act)
            if stages >= 6:
                moe6_act(act)

        NVEC = 16 * 23

        @block.tensor
        def _(pe):
            pe.wait_ge(s_tab, 16)
            pe.wait_ge(s_const, 16 * 10)
            for k in range(9):
                t = pe.transpose(Z[:, k // 4, (k % 4) * P:(k % 4 + 1) * P], wraw[:, k, :], ident)
            t.then_inc(s_sett, 1)
            pe.wait_ge(s_vec, NVEC)
            pe.transpose(Z[:, 3, 0:32], vrow[:], ident[0:32, 0:32])
            pe.transpose(Z[:, 3, 32:40], wgraw[:], ident[0:8, 0:8]).then_inc(s_sett, 1)
            for w in range(3):
                t = pe.transpose(Z[:, 4, w * P:(w + 1) * P], wraw[:, 9 + w, :], ident)
            t.then_inc(s_sett, 1)
            pe.wait_ge(s_setp, 1)
            for k, row in enumerate((brow, brot)):
                for j in range(2):
                    t = pe.matmul(Z[:, 6, (2 * k + j) * 2 * S:(2 * k + j + 1) * 2 * S], row[:, j, :],
                                  const("ones")[0:1, :], start=True, stop=True)
            t.then_inc(s_sett, 1)
            pe.wait_ge(s_set, 4)
            attention_pe(pe, 1)
            if stages >= 2:
                layers_pe(pe)
            if stages >= 3:
                moe_pe(pe)
            if stages >= 4:
                attention_pe(pe, 4)
            if stages >= 5:
                linear_pe(pe)
            if stages >= 6:
                moe6_pe(pe)

        @block.vector
        def _(v):
            v.memset(eps[:], LN_EPS)
            v.memset(denb[:, 0:1], 0.0)
            v.memset(denb[:, 1:2], FEAT_EPS)
            v.memset(power[:], -0.5).then_inc(s_set, 1)
            v.memset(vx[:], 0.0)
            v.memset(vx4[:], 0.0).then_inc(s_zero, 1)
            v.wait_ge(s_zero, 1)
            for jj in range(2):
                v.memset(value_cols(1, jj, P // 2), 1.0)
            v.memset(value_cols(4, 0, P // 2), 1.0).then_inc(s_zero, 1)
            v.memset(acc[:], 0.0).then_inc(s_zero, 1)
            v.wait_ge(s_tab, 16)
            v.tensor_copy(CB[:], C[:])
            for h in range(2):
                for b in range(8):
                    v.tensor_copy(ctxa[h][:, b, D:CA], const("headsel"))
            v.memset(spacer[:], 0.0).then_inc(s_set, 1)
            v.wait_ge(s_sett, 1)
            v.tensor_copy(wT[:], Z[:, 0:3, :].rearrange("p a b -> p (a b)")[:, 0:9 * D].rearrange("p (k n) -> p k n", n=D)).then_inc(s_set, 1)
            v.wait_ge(s_set, 3)
            for k in range(2):
                w = wT[:, k, :].rearrange("p (h t d) -> p h t d", t=2, d=DH // 2)
                r = wrot[:, k, :].rearrange("p (h t d) -> p h t d", t=2, d=DH // 2)
                v.tensor_scalar(r[:, :, 0, :], w[:, :, 1, :], -1.0, None, ALU.mult)
                v.tensor_copy(r[:, :, 1, :], w[:, :, 0, :])
            v.wait_ge(s_sett, 2)
            v.tensor_copy(vcol[:], Z[:, 3, 0:32])
            v.tensor_copy(wr[:, 1, :], Z[:, 3, 32:40]).then_inc(s_setd, 1)
            v.wait_ge(s_setd, 1)
            v.tensor_scalar(bqm[:], const("qpar"), vcol[:, 24:25], None, ALU.mult)
            v.tensor_scalar(bkm[:], const("kpair"), vcol[:, 25:26], None, ALU.mult)
            v.wait_ge(s_sett, 3)
            for j in range(2):
                v.tensor_scalar(woM[:, :, j, :], Z[:, 4, 0:3 * P].rearrange("p (w n) -> p w n", n=P), const("hpar")[:, j:j + 1], None, ALU.mult)
            v.wait_ge(s_sett, 4)
            v.tensor_tensor(qkx[:, 0, :], Z[:, 6, 0:4 * S], const("cos2"), ALU.mult)
            v.tensor_tensor(qkx[:, 1, :], Z[:, 6, 4 * S:8 * S], const("sin2"), ALU.mult).then_inc(s_setd, 1)
            v.wait_ge(s_setd, 2)
            v.tensor_tensor(BQK[:].rearrange("p a s -> p (a s)"), qkx[:, 0, :], qkx[:, 1, :], ALU.add).then_inc(s_setd, 1)
            v.wait_ge(s_setd, 3)
            for k, mask in enumerate(("qpar", "kpair")):
                for j in range(2):
                    w = v.tensor_scalar(BM[:, 2 * k:2 * k + 2, j, :], BQK[:, 2 * k:2 * k + 2, :], const(mask)[:, j:j + 1], None, ALU.mult)
            w.then_inc(s_set, 1)
            v.wait_ge(s_x, 16)
            v.wait_ge(s_zero, 3)
            attention_dve(v, 1)
            if stages >= 2:
                layers_dve(v)
            if stages >= 3:
                moe_dve(v)
            if stages >= 4:
                attention_dve(v, 4)
            if stages >= 5:
                linear_dve(v)
            if stages >= 6:
                moe6_dve(v)

        @block.gpsimd
        def _(g):
            g.wait_ge(s_vec, NVEC)
            for j in range(2):
                w = brow[:, j, :].rearrange("p (h t d) -> p h t d", t=2, d=DH // 2)
                r = brot[:, j, :].rearrange("p (h t d) -> p h t d", t=2, d=DH // 2)
                g.tensor_scalar(r[:, :, 0, :], w[:, :, 1, :], -1.0, None, ALU.mult)
                t = g.tensor_copy(r[:, :, 1, :], w[:, :, 0, :])
            t.then_inc(s_setp, 1)
            g.wait_ge(s_set, 4)
            attention_pool(g, 1)
            if stages >= 2:
                layers_pool(g)
            if stages >= 3:
                moe_pool(g)
            if stages >= 4:
                attention_pool(g, 4)
            if stages >= 5:
                linear_pool(g)
            if stages >= 6:
                moe6_pool(g)



def kernel(**inputs):
    import concourse.bacc as bacc
    from concourse.bass_utils import run_bass_kernel_spmd as run

    nc = bacc.Bacc("TRN2", target_bir_lowering=False, num_devices=1)
    arrays, args = {}, {}
    for name, array in [("const", const_table())] + list(inputs.items()):
        arrays[f"in_{name}"] = np.ascontiguousarray(array)
        args[name] = nc.dram_tensor(f"in_{name}", arrays[f"in_{name}"].shape, F32, kind="ExternalInput").ap()
    args["slots"] = nc.dram_tensor("slots", (E * CAP + B * S, D), F32).ap()
    out = nc.dram_tensor("out", (B, S, D), F32, kind="ExternalOutput").ap()
    perceiver_kernel(nc, args, out, STAGES)
    return run(nc, [arrays], core_ids=[0]).results[0]["out"]


STAGES = 6
```

```python
from contextlib import ExitStack

import numpy as np

import concourse.bass as bass
from concourse import mybir

F32 = mybir.dt.float32
BF16 = mybir.dt.bfloat16
ALU = mybir.AluOpType
ACT = mybir.ActivationFunctionType
AX = mybir.AxisListType

P = 128
B, S, D, CTX = 16, 64, 128, 128
NT = B * S // P
H = 16
DH = D // H
DEPTH = 6
LH = 8
LD = D // LH
E = 8
FF = 512
FC = FF // P
CAP = int(1.25 * B * S / E)
SLOTS = E * CAP // P
QE = 4
LN_EPS = 1e-5
FEAT_EPS = 1e-4
NEG = -1e30

CONST = {}


def _layout():
    at = 0
    for name, width in (
        ("ident", P), ("cos2", 4 * S), ("sin2", 4 * S), ("qpar", 2), ("kpair", 2), ("hpar", 2), ("mask01", S), ("headblock", P),
        ("iota", E), ("causal", 2 * S),
        ("tri", P), ("ones", P), ("past", NT),
    ):
        CONST[name] = (at, at + width)
        at += width
    return at


NCONST = _layout()


def const_table():
    c = np.zeros((P, NCONST), np.float32)

    def put(name, a):
        lo, hi = CONST[name]
        c[:a.shape[0], lo:hi] = a.reshape(a.shape[0], hi - lo)

    p = np.arange(P)
    pos = np.arange(S, dtype=np.float32)
    half = DH // 2
    inv = (1.0 / 10000.0 ** (np.arange(half, dtype=np.float32) / half)).astype(np.float32)
    ang = pos[None, :] * inv[p % half][:, None]
    put("ident", np.eye(P))
    put("cos2", np.tile(np.cos(ang), (1, 4)))
    put("sin2", np.tile(np.sin(ang), (1, 4)))
    put("qpar", ((p // DH)[:, None] % 2 == np.arange(2)) * np.float32(DH ** -0.5))
    put("kpair", (((p // DH) % 4 // 2)[:, None] == np.arange(2)).astype(np.float32))
    put("hpar", ((p // DH)[:, None] % 2 == np.arange(2)).astype(np.float32))
    put("mask01", (np.arange(S)[None, :] >= (p % S)[:, None]).astype(np.float32))
    put("headblock", (p[:, None] // LD == p[None, :] // LD).astype(np.float32))
    put("iota", np.tile(np.arange(E, dtype=np.float32), (P, 1)))
    put("causal", np.tile(np.where(np.arange(S)[None, :] > (p % S)[:, None], NEG, 0.0), (1, 2)))
    put("tri", (p[:, None] <= p[None, :]).astype(np.float32))
    put("ones", np.ones((P, P)))
    put("past", E * CAP + np.arange(NT)[None, :] * P + p[:, None])
    return c


class Sems(dict):

    def __init__(self, sem, stage):
        self.sem, self.stage = sem, stage

    def __missing__(self, name):
        self[name] = self.sem(f"{self.stage}_{name}")
        return self[name]


def perceiver_kernel(nc, a, out):
    with ExitStack() as ctx:
        def sb(name, shape, dt=F32):
            return ctx.enter_context(nc.sbuf_tensor(name, shape, dt))

        def sem(name):
            return ctx.enter_context(nc.semaphore(name))

        C = sb("C", [P, NCONST])
        CB = sb("CB", [P, NCONST], BF16)

        def const(name, dt=F32):
            lo, hi = CONST[name]
            return (C if dt == F32 else CB)[:, lo:hi]

        ident, identb = const("ident"), const("ident", BF16)
        X = sb("X", [P, NT, D])
        Y = sb("Y", [P, NT, D])
        wraw = sb("wraw", [P, 12, D])
        wT = sb("wT", [P, 9, D])
        wrot = sb("wrot", [P, 2, D])
        woM = sb("woM", [P, 3, 2, D])
        vrow = sb("vrow", [32, D])
        vcol = sb("vcol", [P, 32])
        brow = sb("brow", [1, 2, D])
        brot = sb("brot", [1, 2, D])
        vbc = sb("vbc", [P, 5, D])
        vbd = sb("vbd", [P, 3, 2 * D])
        BQK = sb("BQK", [P, 4, S])
        BM = sb("BM", [P, 4, 2, S])
        bqm = sb("bqm", [P, 2])
        bkm = sb("bkm", [P, 2])
        spacer = sb("spacer", [P, 1])
        eps = sb("eps", [P, 8])
        power = sb("power", [P, 8])

        ctxbuf = sb("ctxbuf", [P, 2, D])
        stats = sb("stats", [P, 8, 6])
        meanvar = sb("meanvar", [P, 8, 2])
        veps = sb("veps", [P, 8])
        rstd = sb("rstd", [P, 8])
        xn = sb("xn", [P, D])
        xcT = sb("xcT", [P, 3, D])
        qkx = sb("qkx", [P, 2, 4 * S])
        qk = sb("qk", [P, 4 * S])
        qe = sb("qe", [P, 2, 2, S])
        ke = sb("ke", [P, 4 * CTX])
        vx = sb("vx", [P, 4, 320])
        vx4 = sb("vx4", [P, 4, 576])
        sc = [sb(f"sc{p}", [P, 8, P]) for p in range(2)]
        nmax = [sb(f"nmax{p}", [P, 8]) for p in range(2)]
        pT = [sb(f"pT{p}", [P, 8, P]) for p in range(2)]
        den2 = sb("den2", [P, 2, P])
        den = sb("den", [P, P])
        rden = sb("rden", [P, P])
        denb = sb("denb", [P, 2])
        att = sb("att", [P, 2, 2, S])
        fm = sb("fm", [P, 2 * P])
        fr = sb("fr", [P, 2 * P])

        wq = sb("wq", [P, D])
        wk = sb("wk", [P, D])
        wv = sb("wv", [P, D])
        wo = sb("wo", [P, D])
        w1 = sb("w1", [P, FF])
        w2 = sb("w2", [P, FC, D])
        bo = sb("bo", [P, D])
        lnp = [sb(f"lnp{h}", [P, 4]) for h in range(2)]
        st2 = [sb(f"st2{h}", [P, 4, 6]) for h in range(2)]
        mv2 = [sb(f"mv2{h}", [P, 4, 2]) for h in range(2)]
        ve2 = [sb(f"ve2{h}", [P, 4]) for h in range(2)]
        rs2 = [sb(f"rs2{h}", [P, 4]) for h in range(2)]
        xn2 = [sb(f"xn2{h}", [P, 4, D]) for h in range(2)]
        xT2 = [sb(f"xT2{h}", [P, 4 * P]) for h in range(2)]
        nqm = [sb(f"nqm{h}", [P, 4, LH]) for h in range(2)]
        nkm = [sb(f"nkm{h}", [P, 8]) for h in range(2)]
        eqT = [sb(f"eqT{h}", [P, 4 * P]) for h in range(2)]
        ek = [sb(f"ek{h}", [P, 4, D]) for h in range(2)]
        vs = [sb(f"vs{h}", [P, 4, D]) for h in range(2)]
        rk = [sb(f"rk{h}", [P, 8]) for h in range(2)]
        ctxa = [sb(f"ctxa{h}", [P, 8, D]) for h in range(2)]
        sk = [sb(f"sk{h}", [P, 8]) for h in range(2)]
        sq = [sb(f"sq{h}", [P, 4, LH]) for h in range(2)]
        rq = [sb(f"rq{h}", [P, 4, LH]) for h in range(2)]
        aq = [sb(f"aq{h}", [P, 4, D]) for h in range(2)]
        aT = [sb(f"aT{h}", [P, 4 * P]) for h in range(2)]
        qx2, kx2 = aq, aT
        hs = [sb(f"hs{h}", [P, FC, 4 * P]) for h in range(2)]
        hT = [sb(f"hT{h}", [P, FC, 4 * P]) for h in range(2)]

        tT = sb("tT", [P, NT * P])
        wr = sb("wr", [P, 2, E])
        wgraw = sb("wgraw", [E, D])
        we1 = sb("we1", [P, FF])
        we2 = sb("we2", [P, FC, D])
        acc = sb("acc", [P, NT, D])
        xw1 = [sb(f"xw1{k}", [P, FF]) for k in range(QE)]
        xw2 = [sb(f"xw2{k}", [P, FC, D]) for k in range(QE)]
        slot = sb("slot", [P, SLOTS, D])
        slotT, resT = (hs[h][:].rearrange("p c n -> p (c n)")[:, 0:SLOTS * P] for h in range(2))
        place = sb("place", [P, NT])
        placei = sb("placei", [P, NT], mybir.dt.uint32)
        factor = sb("factor", [P, NT])
        lg = sb("lg", [P, NT, E])
        r1 = sb("r1", [P, NT, E])
        r2 = sb("r2", [P, NT, E])
        oh = sb("oh", [P, NT, E])
        oh2 = sb("oh2", [P, NT, E])
        ohb = sb("ohb", [P, NT, E], BF16)
        gate = sb("gate", [P, E, NT])
        m1 = sb("m1", [P, NT])
        m2 = sb("m2", [P, NT])
        m3 = sb("m3", [P, NT])
        m4 = sb("m4", [P, NT])
        keep = sb("keep", [P, NT])
        woutT = hs[1][:, :, 0:D]
        wc = hs[0][:].rearrange("p c n -> p (c n)")[:, 0:E * D].rearrange("p (e n) -> p e n", e=E)

        Z = ctx.enter_context(nc.psum_tensor("Z", [P, 8, 512], F32))

        s_tab = sem("s_tab")
        s_x = sem("s_x")
        s_w1 = sem("s_w1")
        s_vec1 = sem("s_vec1")
        s_const = sem("s_const")
        s_vec = sem("s_vec")
        s_clear = sem("s_clear")
        s_out = sem("s_out")
        s_set = sem("s_set")
        s_setd = sem("s_setd")
        s_setp = sem("s_setp")
        s_sett = sem("s_sett")
        s_zero = sem("s_zero")

        N = Sems(sem, "n")
        A = Sems(sem, "a")
        C5 = Sems(sem, "s5")
        L = Sems(sem, "s2")
        R = Sems(sem, "r")
        M3 = Sems(sem, "s3")
        M6 = Sems(sem, "s6")

        x_d = a["x"].rearrange("(t b) n d -> (b n) t d", b=2)
        out_d = out.rearrange("(t b) n d -> (b n) t d", b=2)
        slots_d = a["slots"][0:E * CAP].rearrange("(s p) n -> p s n", p=P)
        ctx_d = a["ctx_1024"].rearrange("b n d -> n b d")

        block = ctx.enter_context(nc.Block())

        def nth(i, k=1):
            return (i + 1) * k

        def peeled(eng, count, body):
            body(0, True)
            with eng.Fori(1, count) as i:
                body(i, False)

        def pipelined(eng, front, body):
            front(0)
            body(0, True, False)
            with eng.Fori(1, NT - 1) as i:
                body(i, False, False)
            body(NT - 1, False, True)

        def tile_of(t, i):
            return t[:, bass.ds(i, 1), :].rearrange("p a d -> p (a d)")

        def KEYS(st):
            return S if st == 1 else CTX

        def scores(st, p):
            return Z[:, 3 + 2 * p:5 + 2 * p, 0:4 * KEYS(st)].rearrange("p g (r k) -> p g r k", k=KEYS(st))

        def bulk(t, st):
            return t[:].rearrange("p r k -> p (r k)")[:, 0:8 * KEYS(st)].rearrange("p (g r k) -> p g r k", g=2, k=KEYS(st))

        def kview(st):
            return ke[:, 0:4 * KEYS(st)].rearrange("p (b k) -> p b k", b=2)

        def value_cols(st, jj, at):
            if st == 4:
                return vx4[:].rearrange("p q (c m) -> p q c m", m=144)[:, :, :, at:at + 16]
            rows = slice(jj * S, (jj + 1) * S)
            return vx[rows].rearrange("p q (c m) -> p q c m", m=160)[:, :, :, at + 16 * jj:at + 16 * jj + 16]

        def values_dve(v, s, st, i, n):
            v.wait_ge(s["v"], nth(n))
            k = {1: 0, 4: 1, 5: 2}[st]
            if st == 4:
                w = v.tensor_tensor(value_cols(4, 0, 0), Z[:, 0, 0:2 * D].rearrange("p (q c d) -> p q c d", q=4, d=16),
                                    vbd[:, k, :].rearrange("p (q c d) -> p q c d", q=4, d=16), ALU.add)
            else:
                for jj in range(2):
                    rows = slice(jj * S, (jj + 1) * S)
                    w = v.tensor_tensor(value_cols(st, jj, 0), Z[rows, 0, 0:2 * D].rearrange("p (q c d) -> p q c d", q=4, d=32)[:, :, :, 16 * jj:16 * jj + 16],
                                        vbd[rows, k, :].rearrange("p (q c d) -> p q c d", q=4, d=32)[:, :, :, 16 * jj:16 * jj + 16], ALU.add)
            w.then_inc(s["va"], 1)

        def sums_pe(pe, st, p, weights):
            for b in range(2):
                blocks = [(u, jj) for u in range(2) for jj in range(2)] if st == 4 else [(u, 0) for u in range(2)]
                for c, (u, jj) in enumerate(blocks):
                    w = (vx4 if st == 4 else vx)[:, 2 * b + p, c * P:(c + 1) * P]
                    m = weights[:, 4 * u + 2 * b + jj, :] if st == 4 else weights[:, 2 * u + b, :]
                    t = pe.matmul(Z[:, (2, 7)[p], b * P:(b + 1) * P], w, m, start=(c == 0), stop=(c == len(blocks) - 1), skip_group_check=True)
            return t

        def sums_of(p, j2):
            return Z[P // 2:P, (2, 7)[p], 0:4 * S].rearrange("p (b j q) -> p b j q", b=2, j=2)[:, :, j2, :]

        def sums_act(act, s, st, n):
            for p in range(2):
                act.wait_ge(s["av"], 2 * n + p + 1)
                for j in range(2):
                    add = int(st == 5 and j == 0)
                    t = act.activation(den2[p * 64:(p + 1) * 64, j, :].rearrange("p (b q) -> p b q", b=2), sums_of(p, j), ACT.Identity,
                                       scale=const("hpar")[64:P, j:j + 1], bias=denb[64:P, add:add + 1])
            t.then_inc(s["d0"], 1)

        def sums_pool(g, s, n):
            g.wait_ge(s["d0"], nth(n))
            g.tensor_tensor(den[:], den2[:, 0, :], den2[:, 1, :], ALU.add).then_inc(s["den"], 1)

        def beside(g, ahead, behind):
            ahead(0)
            with g.Fori(0, NT - 1) as i:
                ahead(i + 1)
                behind(i)
            behind(NT - 1)

        def divide_dve(v, s, st, n):
            v.wait_ge(s["den"], nth(n))
            v.reciprocal(rden[:], den[:]).then_inc(s["rec"], 1)
            v.wait_ge(s["rec"], n + 1)
            for p in range(2):
                rows = slice(p * 64, (p + 1) * 64)
                t = v.tensor_tensor(att[rows].rearrange("p j b q -> p b j q"),
                                    Z[0:P // 2, (2, 7)[p], 0:4 * S].rearrange("p (b j q) -> p b j q", b=2, j=2),
                                    rden[rows].rearrange("p (b q) -> p b q", b=2).unsqueeze(2).broadcast_to([64, 2, 2, S]), ALU.mult)
            t.then_inc(s["att"], 1)

        def out_projection(pe, w):
            for j in range(2):
                t = pe.matmul(Z[:, 7, 0:D], att[:, j].rearrange("p b q -> p (b q)"), woM[:, w, j, :],
                              start=(j == 0), stop=(j == 1), skip_group_check=True)
            return t

        def attention_act(act, st):
            s = A
            base = 0 if st == 1 else NT

            def front(i):
                act.wait_ge(s["ctxT"], nth(i + base))
                act.activation(xcT[:].rearrange("p a n -> p (a n)"), Z[:, 0, 0:3 * D], ACT.Identity).then_inc(s["xcT"], 1)

            def front_qk(i):
                if st == 4:
                    act.wait_ge(s["qk"], nth(i + base))
                    for j in range(2):
                        act.activation(qe[:, :, j, :], Z[:, 1, 0:P].rearrange("p (b q) -> p b q", b=2), ACT.Identity,
                                       scale=const("qpar")[:, j:j + 1], bias=bqm[:, j:j + 1])
                    for j in range(2):
                        t = act.activation(kview(4).rearrange("p b (j k) -> p b j k", j=2)[:, :, j, :],
                                           Z[:, 1, P:3 * P].rearrange("p (b k) -> p b k", b=2), ACT.Identity,
                                           scale=const("kpair")[:, j:j + 1], bias=bkm[:, j:j + 1])
                    t.then_inc(s["qe"], 1)

            def body(i, first, last):
                if not last:
                    front(i + 1)
                for p in range(2):
                    act.wait_ge(s["sub"], 2 * (i + base) + p + 1)
                    act.activation(bulk(sc[p], st), bulk(sc[p], st), ACT.Exp).then_inc(s["exp"], 1)
                for p in range(2):
                    act.wait_ge(s["pT"], 2 * (i + base) + p + 1)
                    if st == 1:
                        act.activation(pT[p][:, 0:4, :], Z[:, 3 + 2 * p, :].rearrange("p (r q) -> p r q", q=P), ACT.Identity).then_inc(s["pTe"], 1)
                    else:
                        act.activation(pT[p][:].rearrange("p r k -> p (r k)"), Z[:, 3 + 2 * p:5 + 2 * p, :].rearrange("p a b -> p (a b)"),
                                       ACT.Identity).then_inc(s["pTe"], 1)
                if not last:
                    front_qk(i + 1)
                sums_act(act, s, st, i + base)

            def ahead(i):
                front(i)
                front_qk(i)

            pipelined(act, ahead, body)

        def attention_pe(pe, st):
            s, K = A, KEYS(st)
            base = 0 if st == 1 else NT
            w0 = 0 if st == 1 else 3

            def front_T(i):
                if not isinstance(i, int) or i > 0:
                    pe.wait_ge(s["va"], i + base)
                pe.wait_ge(s["xn"], nth(i + base))
                pe.transpose(Z[:, 0, 0:P], xn[:], ident)
                pe.wait_ge(s["ctx" if st == 1 else "ctx4"], nth(i, 32 if st == 1 else 16))
                for b in range(2):
                    t = pe.transpose(Z[:, 0, (1 + b) * P:(2 + b) * P], ctxbuf[:, b, :], ident)
                t.then_inc(s["ctxT"], 1)

            def front_qkv(i):
                pe.wait_ge(s["xcT"], nth(i + base))
                if st == 1:
                    for k, w in enumerate((wT, wrot)):
                        pe.matmul(Z[:, 1, 4 * S * k:4 * S * k + 2 * S], w[:, 0, :], xcT[:, 0, :], start=True, stop=True)
                        t = pe.matmul(Z[:, 1, 4 * S * k + 2 * S:4 * S * k + 4 * S], w[:, 1, :], xcT[:, 1:3, 0:S], start=True, stop=True)
                else:
                    pe.matmul(Z[:, 1, 0:P], wT[:, w0, :], xcT[:, 0, :], start=True, stop=True)
                    t = pe.matmul(Z[:, 1, P:3 * P], wT[:, w0 + 1, :], xcT[:, 1:3, :], start=True, stop=True)
                t.then_inc(s["qk"], 1)
                for b in range(2):
                    t = pe.matmul(Z[:, 0, b * D:(b + 1) * D], xcT[:, 1 + b, :], wT[:, w0 + 2, :], start=True, stop=True)
                t.then_inc(s["v"], 1)

            def tail_y(i):
                pe.wait_ge(s["att"], nth(i + base))
                out_projection(pe, 0 if st == 1 else 1).then_inc(s["y"], 1)

            def body(i, first, last):
                if st == 1:
                    for gg in range(4):
                        pe.matmul(Z[:, 3 + gg, 0:4 * K], identb, const("causal", BF16).unsqueeze(1).broadcast_to([P, 2, 2 * S]),
                                  start=True, stop=False, skip_group_check=True)
                if st == 1:
                    pe.wait_ge(s["ke"], nth(i))
                pe.wait_ge(s["qe"], nth(i + base))
                for gg in range(4):
                    rows = slice(32 * gg, 32 * gg + 32)
                    for b in range(2):
                        t = pe.matmul(Z[:, 3 + gg, b * 2 * K:(b + 1) * 2 * K], qe[rows, b].rearrange("p j q -> p (j q)"),
                                      kview(st)[rows, b, :], start=(st == 4), stop=True, skip_group_check=True)
                    if gg % 2:
                        t.then_inc(s["s"], 1)
                if not last:
                    front_T(i + 1)
                if not last:
                    front_qkv(i + 1)
                if not first:
                    tail_y(i - 1)
                for p in range(2):
                    pe.wait_ge(s["exp"], 2 * (i + base) + p + 1)
                    if st == 1:
                        for r in range(4):
                            t = pe.transpose(Z[:, 3 + 2 * p, r * P:(r + 1) * P],
                                             sc[p][:].rearrange("p r k -> p (r k)")[:, r * P:(r + 1) * P], ident)
                    else:
                        for r in range(8):
                            t = pe.transpose(Z[:, 3 + 2 * p + r // 4, (r % 4) * P:(r % 4 + 1) * P], sc[p][:, r, :], ident)
                    t.then_inc(s["pT"], 1)
                pe.wait_ge(s["va"], nth(i + base))
                for p in range(2):
                    if p == 1 and (not first or st == 4):
                        pe.wait_ge(s["out"], i + base)
                    pe.wait_ge(s["pTe"], 2 * (i + base) + p + 1)
                    sums_pe(pe, st, p, pT[p]).then_inc(s["av"], 1)

            def ahead(i):
                front_T(i)
                front_qkv(i)

            pipelined(pe, ahead, body)
            tail_y(NT - 1)

        def scale_tile(v, s, i, step):
            v.tensor_scalar(xn[:], tile_of(X, i), meanvar[:, bass.ds(i, 1), 0], rstd[:, bass.ds(i, 1)],
                            ALU.subtract, ALU.mult).then_inc(s["xn"], 1)

        def attention_dve(v, st):
            s, K = A, KEYS(st)
            base = 0 if st == 1 else NT
            if st == 4:
                stats_all(v, N, 4, X)
            v.wait_ge(N["ars"], 1 if st == 1 else 4)

            def front(i):
                if not isinstance(i, int) or i > 0:
                    v.wait_ge(s["ctxT"], i + base)
                scale_tile(v, s, i, i + base)

            def front_rope(i):
                if st == 1:
                    v.wait_ge(s["qk"], nth(i + base))
                    v.tensor_tensor(qkx[:, 0, :], Z[:, 1, 0:4 * S], const("cos2"), ALU.mult)
                    v.tensor_tensor(qkx[:, 1, :], Z[:, 1, 4 * S:8 * S], const("sin2"), ALU.mult).then_inc(s["qr"], 1)
                    v.wait_ge(s["qr"], nth(i + base))
                    v.tensor_tensor(qk[:], qkx[:, 0, :], qkx[:, 1, :], ALU.add).then_inc(s["qa"], 1)
                    v.wait_ge(s["qa"], nth(i + base))
                    for j in range(2):
                        t = v.scalar_tensor_tensor(out=qe[:, :, j, :], in0=qk[:, 0:P].rearrange("p (b s) -> p b s", b=2),
                                                   scalar=const("qpar")[:, j:j + 1], in1=BM[:, 0:2, j, :], op0=ALU.mult, op1=ALU.add)
                    t.then_inc(s["qe"], 1)

            def tail(i):
                v.wait_ge(s["y"], nth(i + base))
                v.tensor_tensor(tile_of(X, i), Z[:, 7, 0:D], tile_of(Y, i), ALU.add).then_inc(s["out"], 1)

            def body(i, first, last):
                if not last:
                    front(i + 1)
                for p in range(2):
                    v.wait_ge(s["s"], 2 * (i + base) + p + 1)
                    v.tensor_reduce(nmax[p][:].rearrange("p (g r) -> p g r", g=2), scores(st, p), AX.X, ALU.max, negate=True).then_inc(s["max"], 1)
                    v.wait_ge(s["max"], 2 * (i + base) + p + 1)
                    v.tensor_tensor(bulk(sc[p], st), scores(st, p),
                                    nmax[p][:].rearrange("p (g r) -> p g r", g=2).unsqueeze(3).broadcast_to([P, 2, 4, K]), ALU.add).then_inc(s["sub"], 1)
                    if p == 0 and not first:
                        divide_dve(v, s, st, i - 1 + base)
                if not first:
                    tail(i - 1)
                if not last:
                    front_rope(i + 1)
                if not last:
                    v.wait_ge(s["av"], 2 * (i + base) + 2)
                    values_dve(v, s, st, i + 1, i + 1 + base)

            def ahead(i):
                front(i)
                front_rope(i)
                values_dve(v, s, st, i, i + base)
                v.wait_ge(N["xb"], 1 if st == 1 else 2)

            pipelined(v, ahead, body)
            divide_dve(v, s, st, NT - 1 + base)
            tail(NT - 1)

        def with_bias_pool(g, bias, step):
            g.tensor_tensor(Y[:], X[:], vbc[:, bias, :].unsqueeze(1).broadcast_to([P, NT, D]), ALU.add).then_inc(N["xb"], 1)

        def attention_pool(g, st):
            if st == 1:
                g.wait_ge(s_x, 16)
            norm_all_pool(g, N, 1 if st == 1 else 4)
            with_bias_pool(g, 0 if st == 1 else 1, 1)
            base = 0 if st == 1 else NT

            def keys(i):
                if st == 1:
                    k = kview(1).rearrange("p b (j k) -> p b j k", j=2)
                    g.wait_ge(A["qa"], nth(i))
                    g.tensor_tensor(k, qk[:, P:2 * P].rearrange("p (b s) -> p b s", b=2).unsqueeze(2).broadcast_to([P, 2, 2, S]),
                                    const("kpair").unsqueeze(1).unsqueeze(3).broadcast_to([P, 2, 2, S]), ALU.mult).then_inc(A["km"], 1)
                    g.wait_ge(A["km"], nth(i))
                    g.tensor_tensor(k, k, BM[:, 2:4], ALU.add).then_inc(A["ke"], 1)

            beside(g, keys, lambda i: sums_pool(g, A, i + base))

        def zb(h, k):
            return Z[:, 4 * h + k, :]

        def tiles(bank):
            return bank.rearrange("p (t n) -> p t n", n=P)

        def stats_all(v, s, key, src):
            for t in range(NT):
                u = v.bn_stats(stats[:, t, :], src[:, t, :])
            u.then_inc(s["ast"], 1)
            v.wait_ge(s["ast"], key)
            for t in range(NT):
                u = v.bn_aggr(meanvar[:, t, :], stats[:, t, :])
            u.then_inc(s["amv"], 1)

        def norm_all(v, s, key, src, dst):
            stats_all(v, s, key, src)
            v.wait_ge(s["ars"], key)
            for t in range(NT):
                u = v.tensor_scalar(dst[:, t, :], src[:, t, :], meanvar[:, t, 0:1], rstd[:, t:t + 1], ALU.subtract, ALU.mult)
            u.then_inc(s["axn"], 1)
            v.wait_ge(s["axn"], {2: 1, 3: 2, 6: 3, 7: 4}[key])

        def norm_all_pool(g, s, key):
            g.wait_ge(s["amv"], key)
            g.tensor_tensor(veps[:], meanvar[:, :, 1], eps[:], ALU.add).then_inc(s["arv"], 1)
            g.wait_ge(s["arv"], key)
            g.tensor_tensor(rstd[:], veps[:], power[:], ALU.pow).then_inc(s["ars"], 1)

        def half_stats_dve(v, h, n, x, part):
            y = Y[:, 4 * h:4 * h + 4, :]
            for t in range(2 * part, 2 * part + 2):
                u = v.bn_stats(st2[h][:, t, :], y[:, t, :])
            if part == 1:
                u.then_inc(L["st" + x], 1)
                v.wait_ge(L["st" + x], n)
                v.memset(spacer[:], 0.0)
                for t in range(4):
                    u = v.bn_aggr(mv2[h][:, t, :], st2[h][:, t, :])
                u.then_inc(L["mv" + x], 1)

        def half_scale_dve(v, h, n, x):
            y = Y[:, 4 * h:4 * h + 4, :]
            v.wait_ge(L["rs" + x], n)
            for t in range(4):
                v.tensor_scalar(xn2[h][:, t, :], y[:, t, :], mv2[h][:, t, 0:1], rs2[h][:, t:t + 1], ALU.subtract, ALU.mult)\
                    .then_inc(L["xn" + x], 1)

        def half_norm_pool(g, h, n, x):
            g.wait_ge(L["mv" + x], n)
            g.tensor_tensor(ve2[h][:], mv2[h][:, :, 1], eps[:, 0:4], ALU.add).then_inc(L["rv" + x], 1)
            g.wait_ge(L["rv" + x], n)
            g.tensor_tensor(rs2[h][:], ve2[h][:], power[:, 0:4], ALU.pow).then_inc(L["rs" + x], 1)

        def skewed(eng, step, rest):
            step(0, 0, None, None)
            step(1, 0, 0, 0)
            with eng.Fori(1, DEPTH) as l:
                step(0, l, 1, l - 1)
                step(1, l, 0, l)
            rest(1, DEPTH - 1)

        def nof(l, h):
            return 2 * l + h + 1

        def layers_pool(g):
            norm_all_pool(g, N, 2)
            half_norm_pool(g, 0, 1, "")
            half_norm_pool(g, 1, 2, "")

            def step(a, l, b, lb):
                if b is not None:
                    half_norm_pool(g, b, nof(lb, b), "_")
                y = Y[:, 4 * a:4 * a + 4, :]
                g.wait_ge(L["bo"], 16 * l + 16)
                g.wait_ge(L["xn"], 4 * nof(l, a))
                g.tensor_tensor(y, y, bo[:].unsqueeze(1).broadcast_to([P, 4, D]), ALU.add).then_inc(L["yb"], 1)
                if b is not None:
                    half_norm_pool(g, b, nof(lb, b) + 2, "")

            skewed(g, step, lambda b, lb: half_norm_pool(g, b, nof(lb, b), "_"))

        def nextnorm(l):
            return vcol[:, bass.ds(l + 1, 4, DEPTH)]

        def layers_dve(v):
            v.wait_ge(A["out"], NT)
            norm_all(v, N, 2, X, Y)
            norms = vcol[:, 0:4 * DEPTH].rearrange("p (k l) -> p k l", l=DEPTH)
            for h in range(2):
                v.tensor_copy(lnp[h][:], norms[:, :, 0]).then_inc(L["lnp"], 1)
                half_stats_dve(v, h, h + 1, "", 0)
                half_stats_dve(v, h, h + 1, "", 1)

            def add_tiles(h, l, part, banks, product, done):
                y = Y[:, 4 * h + 2 * part:4 * h + 2 * part + 2, :].rearrange("p t n -> p (t n)")
                v.wait_ge(L[product], 2 * nof(l, h) - 1 + part)
                v.tensor_tensor(y, zb(h, banks[part])[:, 2 * P * part:2 * P * (part + 1)], y, ALU.add).then_inc(L[done], 1)
                v.wait_ge(L[done], 2 * nof(l, h) - 1 + part)

            def residual_norm(h, l):
                v.wait_ge(L["yb"], nof(l, h))
                for part in range(2):
                    add_tiles(h, l, part, (3, 1), "wo_", "y")
                    half_stats_dve(v, h, nof(l, h), "_", part)

            def shift_k(h, l):
                k = zb(h, 3).rearrange("p (b s) -> p b s", s=S)
                v.wait_ge(L["kt"], nof(l, h))
                v.tensor_reduce(nkm[h][:], k, AX.X, ALU.max, negate=True).then_inc(L["nk"], 1)
                v.wait_ge(L["nk"], nof(l, h))
                v.tensor_tensor(kx2[h][:].rearrange("p (b s) -> p b s", s=S), k, nkm[h][:].unsqueeze(2).broadcast_to([P, 8, S]), ALU.add)\
                    .then_inc(L["ks"], 1)

            def shift_q(h, l):
                q = zb(h, 1).rearrange("p (t d) -> p t d", d=LD)
                v.wait_ge(L["qt"], nof(l, h))
                v.tensor_reduce(nqm[h][:].rearrange("p t h -> p (t h)"), q, AX.X, ALU.max, negate=True).then_inc(L["nq"], 1)
                v.wait_ge(L["nq"], nof(l, h))
                v.tensor_tensor(qx2[h][:].rearrange("p t (h d) -> p (t h) d", d=LD), q,
                                nqm[h][:].rearrange("p t h -> p (t h)").unsqueeze(2).broadcast_to([P, 4 * LH, LD]), ALU.add)\
                    .then_inc(L["qs"], 1)

            def sum_k(h, l):
                v.wait_ge(L["ke"], nof(l, h))
                v.tensor_reduce(sk[h][:], kx2[h][:].rearrange("p (b s) -> p b s", s=S), AX.X, ALU.add).then_inc(L["sk"], 1)
                v.wait_ge(L["sk"], nof(l, h))
                v.reciprocal(rk[h][:], sk[h][:]).then_inc(L["rk"], 1)

            def sum_q(h, l):
                v.wait_ge(L["qe"], nof(l, h))
                v.tensor_reduce(sq[h][:].rearrange("p t h -> p (t h)"), qx2[h][:].rearrange("p t (h d) -> p (t h) d", d=LD), AX.X, ALU.add)\
                    .then_inc(L["sq"], 1)
                v.wait_ge(L["sq"], nof(l, h))
                v.reciprocal(rq[h][:], sq[h][:]).then_inc(L["rq"], 1)

            def leaky(h, l):
                for c in range(FC):
                    v.wait_ge(L["hs"], 8 * l + 4 * h + c + 1)
                    v.tensor_tensor(hT[h][:, c, :], zb(h, (c + 1) % 4), hs[h][:, c, :], ALU.max).then_inc(L["hT"], 1)
                v.tensor_copy(lnp[h][:], nextnorm(l)).then_inc(L["lnp"], 1)

            def context(h, l):
                v.wait_ge(L["cx"], nof(l, h))
                for u in range(2):
                    w = v.tensor_tensor(ctxa[h][:].rearrange("p (t u) n -> p t u n", u=2)[:, :, u, :], tiles(zb(h, (3, 1)[u])),
                                        const("headblock").unsqueeze(1).broadcast_to([P, 4, D]), ALU.mult)
                w.then_inc(L["ca"], 1)

            def take_qT(h, l):
                v.wait_ge(L["rk"], nof(l, h))
                v.wait_ge(L["qT"], nof(l, h))
                v.tensor_tensor(eqT[h][:].rearrange("p (b s) -> p b s", s=S), zb(h, 2).rearrange("p (b s) -> p b s", s=S),
                                rk[h][:].unsqueeze(2).broadcast_to([P, 8, S]), ALU.mult).then_inc(L["eq"], 1)

            def divide(h, l):
                v.wait_ge(L["rq"], nof(l, h))
                v.wait_ge(L["o"], nof(l, h))
                v.tensor_tensor(aq[h][:].rearrange("p t (h d) -> p (t h) d", d=LD), zb(h, 0).rearrange("p (t d) -> p t d", d=LD),
                                rq[h][:].rearrange("p t h -> p (t h)").unsqueeze(2).broadcast_to([P, 4 * LH, LD]), ALU.mult)\
                    .then_inc(L["aq"], 1)

            def residual(h, l, part):
                add_tiles(h, l, part, (1, 2), "w2_", "y2")

            def step(a, l, b, lb):
                half_scale_dve(v, a, nof(l, a), "")
                if b is not None:
                    residual_norm(b, lb)
                if b is not None:
                    half_scale_dve(v, b, nof(lb, b), "_")
                shift_k(a, l)
                shift_q(a, l)
                sum_k(a, l)
                if b is not None:
                    leaky(b, lb)
                sum_q(a, l)
                take_qT(a, l)
                context(a, l)
                if b is not None:
                    residual(b, lb, 0)
                    half_stats_dve(v, b, nof(lb, b) + 2, "", 0)
                divide(a, l)
                if b is not None:
                    residual(b, lb, 1)
                    half_stats_dve(v, b, nof(lb, b) + 2, "", 1)

            def rest(b, lb):
                residual_norm(b, lb)
                half_scale_dve(v, b, nof(lb, b), "_")
                leaky(b, lb)
                residual(b, lb, 0)
                residual(b, lb, 1)

            skewed(v, step, rest)
            v.tensor_tensor(X[:], X[:], Y[:], ALU.add).then_inc(L["out"], 1)
            v.wait_ge(L["out"], 1)

        def layers_act(act):
            def first_norm(h, l):
                act.wait_ge(L["lnp"], nof(l, h))
                act.wait_ge(L["T"], nof(l, h))
                act.activation(xT2[h][:], zb(h, 0), ACT.Identity, scale=lnp[h][:, 0:1], bias=lnp[h][:, 1:2]).then_inc(L["xT"], 1)

            def exp_k(h, l):
                act.wait_ge(L["ks"], nof(l, h))
                act.activation(kx2[h][:], kx2[h][:], ACT.Exp).then_inc(L["ke"], 1)

            def exp_q(h, l):
                act.wait_ge(L["qs"], nof(l, h))
                act.activation(qx2[h][:], qx2[h][:], ACT.Exp).then_inc(L["qe"], 1)

            def take_v(h, l):
                act.wait_ge(L["v"], nof(l, h))
                act.activation(vs[h][:].rearrange("p t n -> p (t n)"), zb(h, 2), ACT.Identity).then_inc(L["vs"], 1)

            def second_norm(h, l):
                act.wait_ge(L["T_"], nof(l, h))
                act.activation(xT2[h][:], zb(h, 0), ACT.Identity, scale=lnp[h][:, 2:3], bias=lnp[h][:, 3:4]).then_inc(L["xT_"], 1)

            def take_kT(h, l):
                act.wait_ge(L["kT"], nof(l, h))
                act.activation(ek[h][:].rearrange("p t n -> p (t n)"), zb(h, 0), ACT.Identity).then_inc(L["ek"], 1)

            def hidden(h, l, c):
                act.wait_ge(L["h1"], 8 * l + 4 * h + c + 1)
                act.activation(hs[h][:, c, :], zb(h, (c + 1) % 4), ACT.Identity, scale=0.01).then_inc(L["hs"], 1)

            def attention_T(h, l):
                act.wait_ge(L["aqT"], nof(l, h))
                act.activation(aT[h][:], zb(h, 1), ACT.Identity).then_inc(L["aqTe"], 1)

            def step(a, l, b, lb):
                first_norm(a, l)
                if b is not None:
                    second_norm(b, lb)
                exp_k(a, l)
                take_v(a, l)
                exp_q(a, l)
                if b is not None:
                    hidden(b, lb, 0)
                    hidden(b, lb, 1)
                take_kT(a, l)
                if b is not None:
                    hidden(b, lb, 2)
                if b is not None:
                    hidden(b, lb, 3)
                attention_T(a, l)

            def rest(b, lb):
                second_norm(b, lb)
                for c in range(FC):
                    hidden(b, lb, c)

            skewed(act, step, rest)

        def layers_pe(pe):
            def transposes(h, src, bank, scaled=None, n=None):
                for t in range(4):
                    if scaled:
                        pe.wait_ge(L[scaled], 4 * n - 3 + t)
                    w = pe.transpose(tiles(zb(h, bank))[:, t, :], src[h][:, t, :], ident)
                return w

            def xtile(h, t):
                return xT2[h][:, t * P:(t + 1) * P]

            def first_T(h, l):
                transposes(h, xn2, 0, "xn", nof(l, h)).then_inc(L["T"], 1)

            def keys_queries(h, l):
                pe.wait_ge(L["w"], 32 * l + 32)
                pe.wait_ge(L["xT"], nof(l, h))
                pe.matmul(zb(h, 3), wk[:], xT2[h][:], start=True, stop=True).then_inc(L["kt"], 1)
                for t in range(4):
                    w = pe.matmul(tiles(zb(h, 1))[:, t, :], xtile(h, t), wq[:], start=True, stop=True)
                w.then_inc(L["qt"], 1)

            def keys_T(h, l):
                pe.wait_ge(L["ke"], nof(l, h))
                for t in range(4):
                    w = pe.transpose(tiles(zb(h, 0))[:, t, :], kx2[h][:, t * P:(t + 1) * P], ident)
                w.then_inc(L["kT"], 1)

            def queries_T(h, l):
                pe.wait_ge(L["vs"], nof(l, h))
                pe.wait_ge(L["qe"], nof(l, h))
                transposes(h, qx2, 2).then_inc(L["qT"], 1)

            def second_T(h, l):
                transposes(h, xn2, 0, "xn_", nof(l, h)).then_inc(L["T_"], 1)

            def values(h, l):
                pe.wait_ge(L["wv"], 16 * l + 16)
                for t in range(4):
                    w = pe.matmul(tiles(zb(h, 2))[:, t, :], xtile(h, t), wv[:], start=True, stop=True)
                w.then_inc(L["v"], 1)

            def hidden(h, l, c):
                if c == 0:
                    pe.wait_ge(L["w1"], 16 * l + 16)
                    pe.wait_ge(L["xT_"], nof(l, h))
                pe.matmul(zb(h, (c + 1) % 4), w1[:, c * P:(c + 1) * P], xT2[h][:], start=True, stop=True).then_inc(L["h1"], 1)

            def context(h, l):
                pe.wait_ge(L["ek"], nof(l, h))
                for t in range(4):
                    for u in range(2):
                        rows = slice(u * S, (u + 1) * S)
                        w = pe.matmul(tiles(zb(h, (3, 1)[u]))[:, t, :], ek[h][rows, t, :], vs[h][rows, t, :], start=True, stop=True)
                w.then_inc(L["cx"], 1)

            def out(h, l, first, last):
                if first == 0:
                    pe.wait_ge(L["w2"], 16 * l + 16)
                    pe.wait_ge(L["hT"], 8 * l + 4 * h + 4)
                for t in range(first, last):
                    for c in range(FC):
                        w = pe.matmul(tiles(zb(h, (1, 2)[t // 2]))[:, t, :], hT[h][:, c, t * P:(t + 1) * P], w2[:, c, :],
                                      start=(c == 0), stop=(c == FC - 1))
                    if t % 2:
                        w.then_inc(L["w2_"], 1)

            def attention(h, l):
                pe.wait_ge(L["eq"], nof(l, h))
                pe.wait_ge(L["ca"], nof(l, h))
                for t in range(4):
                    for u in range(2):
                        w = pe.matmul(tiles(zb(h, 0))[u * S:(u + 1) * S, t, :], eqT[h][:, (2 * t + u) * S:(2 * t + u + 1) * S],
                                      ctxa[h][:, 2 * t + u, :], start=True, stop=True)
                w.then_inc(L["o"], 1)

            def attention_T(h, l):
                pe.wait_ge(L["aq"], nof(l, h))
                transposes(h, aq, 1).then_inc(L["aqT"], 1)

            def projection(h, l):
                pe.wait_ge(L["wo"], 16 * l + 16)
                pe.wait_ge(L["aqTe"], nof(l, h))
                for t in range(4):
                    w = pe.matmul(tiles(zb(h, (3, 1)[t // 2]))[:, t, :], aT[h][:, t * P:(t + 1) * P], wo[:], start=True, stop=True)
                    if t % 2:
                        w.then_inc(L["wo_"], 1)

            def step(a, l, b, lb):
                first_T(a, l)
                keys_queries(a, l)
                if b is not None:
                    second_T(b, lb)
                values(a, l)
                if b is not None:
                    hidden(b, lb, 0)
                    hidden(b, lb, 1)
                keys_T(a, l)
                if b is not None:
                    hidden(b, lb, 2)
                queries_T(a, l)
                if b is not None:
                    hidden(b, lb, 3)
                context(a, l)
                if b is not None:
                    out(b, lb, 0, 3)
                attention(a, l)
                if b is not None:
                    out(b, lb, 3, 4)
                attention_T(a, l)
                projection(a, l)

            def rest(b, lb):
                second_T(b, lb)
                for c in range(FC):
                    hidden(b, lb, c)
                out(b, lb, 0, 4)

            skewed(pe, step, rest)

        def chain(v, sem_):
            count = [0]

            def link(ins):
                count[0] += 1
                ins.then_inc(sem_, 1)
                v.wait_ge(sem_, count[0])

            return link

        def per_token(t):
            return t[:].unsqueeze(2).broadcast_to([P, NT, E])

        iota = const("iota").unsqueeze(1).broadcast_to([P, NT, E])

        def first_of(v, link, onehot, values, top):
            link(v.tensor_tensor(r1[:], values[:], per_token(top), ALU.is_equal))
            link(v.tensor_scalar(r1[:], r1[:], -float(E), None, ALU.mult))
            link(v.tensor_tensor(r1[:], r1[:], iota, ALU.add))
            link(v.tensor_reduce(m4[:], r1[:], AX.X, ALU.min))
            link(v.tensor_scalar(m4[:], m4[:], float(E), None, ALU.add))
            link(v.tensor_tensor(onehot[:], iota, per_token(m4), ALU.is_equal))

        def router_pe(pe, which):
            pe.wait_ge(N["axn"], (2, 4)[which])
            for t in range(NT):
                w = pe.transpose(Z[:, t // 4, (t % 4) * P:(t % 4 + 1) * P], Y[:, t, :], ident)
            w.then_inc(R["T"], 1)
            pe.wait_ge(R["tT"], which + 1)
            for t in range(NT):
                w = pe.matmul(Z[:, 2, t * E:(t + 1) * E], tT[:, t * P:(t + 1) * P], wr[:, which, :], start=True, stop=True)
            w.then_inc(R["lg"], 1)

        def router_act(act, which):
            act.wait_ge(R["T"], which + 1)
            act.activation(tT[:], Z[:, 0:2, :].rearrange("p a b -> p (a b)"), ACT.Identity).then_inc(R["tT"], 1)
            act.wait_ge(R["d"], which + 1)
            if which == 0:
                act.activation(r2[:], r1[:], ACT.Exp).then_inc(R["ex"], 1)
            else:
                act.activation(m3[:], m3[:], ACT.Exp).then_inc(R["ex"], 1)

        def moe_dve(v):
            v.wait_ge(L["out"], 1)
            norm_all(v, N, 3, X, Y)
            link = chain(v, M3["r"])
            v.wait_ge(R["lg"], 1)
            link(v.tensor_copy(lg[:].rearrange("p t e -> p (t e)"), Z[:, 2, 0:NT * E]))
            link(v.tensor_reduce(m1[:], lg[:], AX.X, ALU.max))
            v.tensor_tensor(r1[:], lg[:], per_token(m1), ALU.subtract).then_inc(R["d"], 1)
            v.wait_ge(R["ex"], 1)
            link(v.tensor_reduce(m1[:], r2[:], AX.X, ALU.add))
            link(v.reciprocal(m2[:], m1[:]))
            link(v.tensor_tensor(r2[:], r2[:], per_token(m2), ALU.mult))
            link(v.tensor_reduce(m3[:], r2[:], AX.X, ALU.max))
            first_of(v, link, oh, r2, m3)
            v.tensor_copy(ohb[:], oh[:]).then_inc(M3["p"], 1)
            link(v.tensor_scalar(m4[:], m4[:], float(CAP), -1.0, ALU.mult, ALU.add))
            v.wait_ge(M3["cum"], 1)
            link(v.tensor_tensor(r1[:], Z[:, 3, 0:NT * E].rearrange("p (t e) -> p t e", e=E), oh[:], ALU.mult))
            link(v.tensor_reduce(m1[:], r1[:], AX.X, ALU.add))
            link(v.tensor_scalar(keep[:], m1[:], float(CAP), None, ALU.is_le))
            link(v.tensor_tensor(m1[:], m1[:], m4[:], ALU.add))
            link(v.tensor_tensor(m1[:], m1[:], const("past"), ALU.subtract))
            link(v.tensor_tensor(m1[:], m1[:], keep[:], ALU.mult))
            link(v.tensor_tensor(place[:], m1[:], const("past"), ALU.add))
            v.tensor_copy(placei[:], place[:]).then_inc(M3["place"], 1)
            link(v.tensor_scalar(m2[:], keep[:], -1.0, 1.0, ALU.mult, ALU.add))
            link(v.tensor_tensor(m1[:], m3[:], keep[:], ALU.mult))
            link(v.tensor_tensor(factor[:], m1[:], m2[:], ALU.add))
            v.wait_ge(s_sett, 5)
            v.tensor_copy(wT[:, 3:7, :].rearrange("p k n -> p (k n)"), Z[:, 4, :])
            v.tensor_copy(wT[:, 7:9, :].rearrange("p k n -> p (k n)"), Z[:, 5, 0:2 * P])
            for j in range(2):
                w = v.tensor_scalar(woM[:, 1:3, j, :], Z[:, 6, 0:2 * P].rearrange("p (w n) -> p w n", n=P), const("hpar")[:, j:j + 1], None, ALU.mult)
            w.then_inc(s_set, 1)

            with v.Fori(0, E // QE) as q:
                for k in range(QE):
                    v.wait_ge(M3["o"], q * QE + k + 1)
                    v.tensor_scalar(resT[:, bass.ds(q * (QE * CAP) + k * CAP, CAP)], Z[:, 4 + k % 2, 0:CAP], 1.0, None, ALU.mult)\
                        .then_inc(M3["res"], 1)
            v.wait_ge(M3["rT"], 2)
            v.tensor_copy(slot[:, 5:SLOTS, :].rearrange("p s n -> p (s n)")[:, 0:4 * P], Z[:, 6, :])
            v.tensor_copy(slot[:, 9:SLOTS, :].rearrange("p s n -> p (s n)"), Z[:, 7, 0:P]).then_inc(M3["rTe"], 1)
            v.wait_ge(M3["back"], 16 * NT)
            for t in range(NT):
                w = v.scalar_tensor_tensor(out=X[:, t, :], in0=acc[:, t, :], scalar=factor[:, t:t + 1], in1=X[:, t, :],
                                           op0=ALU.mult, op1=ALU.add)
            w.then_inc(M3["out"], 1)
            v.wait_ge(M3["out"], 1)

        def moe_act(act):
            router_act(act, 0)
            act.wait_ge(M3["sT"], 1)
            act.activation(slotT[:, 0:8 * P], Z[:, 0:2, :].rearrange("p a b -> p (a b)"), ACT.Identity).then_inc(M3["slotT"], 1)
            act.activation(slotT[:, 8 * P:SLOTS * P], Z[:, 2, 0:(SLOTS - 8) * P], ACT.Identity).then_inc(M3["slotT"], 1)
            with act.Fori(0, E // QE) as q:
                for k in range(QE):
                    act.wait_ge(M3["h"], q * QE + k + 1)
                    act.activation(hT[k % 2][:, :, 0:CAP].rearrange("p (a b) n -> p a b n", a=2),
                                   Z[:, 2 * (k % 2):2 * (k % 2) + 2, 0:2 * CAP].rearrange("p a (b n) -> p a b n", b=2), ACT.Relu)\
                        .then_inc(M3["hT"], 1)
            act.wait_ge(M3["rT"], 1)
            act.activation(slot[:, 0:4, :].rearrange("p s n -> p (s n)"), Z[:, 0, :], ACT.Identity)
            act.activation(slot[:, 4, :], Z[:, 1, 0:P], ACT.Identity).then_inc(M3["rTe"], 1)

        def moe_pool(g):
            norm_all_pool(g, N, 3)
            g.wait_ge(s_clear, 48)
            g.wait_ge(M3["place"], 1)
            for t in range(NT):
                g.indirect_dma_start(a["slots"], bass.IndirectOffsetOnAxis(placei[:, t:t + 1], 0), Y[:, t, :], None).then_inc(M3["there"], 16)
            g.wait_ge(M3["stored"], 16)
            for t in range(NT):
                g.indirect_dma_start(acc[:, t, :], None, a["slots"], bass.IndirectOffsetOnAxis(placei[:, t:t + 1], 0)).then_inc(M3["back"], 16)

        def moe_pe(pe):
            router_pe(pe, 0)
            pe.wait_ge(M3["p"], 1)
            flat = ohb[:].rearrange("p t e -> p (t e)")
            pe.matmul(Z[:, 3, 0:NT * E], const("tri", BF16), flat, start=True, stop=False, skip_group_check=True)
            for t in range(NT - 1):
                w = pe.matmul(Z[:, 3, (t + 1) * E:NT * E].rearrange("p (t e) -> p t e", e=E), const("ones", BF16),
                              ohb[:, t:t + 1, :].broadcast_to([P, NT - 1 - t, E]), start=False, stop=(t == NT - 2), skip_group_check=True)
            w.then_inc(M3["cum"], 1)
            pe.wait_ge(s_const, 16 * 6)
            for k in range(6):
                w = pe.transpose(Z[:, 4 + k // 4, (k % 4) * P:(k % 4 + 1) * P], wraw[:, 3 + k, :], ident)
            for k in range(2):
                w = pe.transpose(Z[:, 6, k * P:(k + 1) * P], wraw[:, 10 + k, :], ident)
            w.then_inc(s_sett, 1)
            pe.wait_ge(s_set, 5)
            pe.wait_ge(M3["slots"], 16)
            for k in range(SLOTS):
                w = pe.transpose(Z[:, k // 4, (k % 4) * P:(k % 4 + 1) * P], slot[:, k, :], ident)
            w.then_inc(M3["sT"], 1)
            pe.wait_ge(M3["slotT"], 2)

            def hidden(q, k):
                if k % 2 == 0:
                    pe.wait_ge(M3["w1" + "ab"[k // 2]], q * 32 + 32)
                for c in range(FC):
                    w = pe.matmul(Z[:, 2 * (k % 2) + c // 2, (c % 2) * CAP:(c % 2 + 1) * CAP], xw1[k][:, c * P:(c + 1) * P],
                                  slotT[:, bass.ds(q * (QE * CAP) + k * CAP, CAP)], start=True, stop=True, skip_group_check=True)
                w.then_inc(M3["h"], 1)

            def result(q, k, first):
                if k % 2 == 0:
                    pe.wait_ge(M3["w2" + "ab"[k // 2]], q * 32 + 32)
                if not first or k >= 2:
                    pe.wait_ge(M3["res"], q * QE + k - 1)
                pe.wait_ge(M3["hT"], q * QE + k + 1)
                for c in range(FC):
                    w = pe.matmul(Z[:, 4 + k % 2, 0:CAP], xw2[k][:, c, :], hT[k % 2][:, c, 0:CAP], start=(c == 0), stop=(c == FC - 1))
                w.then_inc(M3["o"], 1)

            def four(q, first):
                hidden(q, 0)
                for k in range(QE):
                    if k + 1 < QE:
                        hidden(q, k + 1)
                    result(q, k, first)

            peeled(pe, E // QE, four)
            pe.wait_ge(M3["res"], E)
            for half, banks in enumerate(((0, 1), (6, 7))):
                for k in range(5):
                    w = pe.transpose(Z[:, banks[k // 4], (k % 4) * P:(k % 4 + 1) * P], resT[:, (5 * half + k) * P:(5 * half + k + 1) * P], ident)
                w.then_inc(M3["rT"], 1)

        def linear_act(act):
            s, base = C5, 2 * NT

            def front_T(i):
                act.wait_ge(s["T"], nth(i))
                act.activation(xcT[:, 0:2, :].rearrange("p b (r s) -> p b r s", r=2),
                               Z[:, 0, 0:P].rearrange("p (b s) -> p b s", b=2).unsqueeze(2).broadcast_to([P, 2, 2, S]), ACT.Identity).then_inc(s["xT"], 1)

            def front_exp(i):
                act.wait_ge(s["fm"], nth(i))
                act.activation(fm[:], fm[:], ACT.Exp).then_inc(s["fe"], 1)

            def front_k(i):
                act.wait_ge(s["ff"], nth(i))
                for j in range(2):
                    t = act.activation(kview(1).rearrange("p b (j k) -> p b j k", j=2)[:, :, j, :],
                                       qk[:, P:2 * P].rearrange("p (b s) -> p b s", b=2), ACT.Identity, scale=const("kpair")[:, j:j + 1])
                t.then_inc(s["ke"], 1)

            def ahead(i):
                front_T(i)
                front_exp(i)
                front_k(i)

            def body(i, first, last):
                if not last:
                    ahead(i + 1)
                act.wait_ge(M6["wt"], nth(i))
                act.activation(woutT, Z[:, 3, :].rearrange("p (c n) -> p c n", n=D), ACT.Identity).then_inc(M6["wT"], 1)
                sums_act(act, A, 5, i + base)

            pipelined(act, ahead, body)

        def linear_pe(pe):
            s, base = C5, 2 * NT

            def front_T(i):
                if not isinstance(i, int) or i > 0:
                    pe.wait_ge(A["va"], i + base)
                pe.wait_ge(s["xn"], nth(i))
                pe.transpose(Z[:, 0, 0:P], xn[:], ident).then_inc(s["T"], 1)

            def front_qkv(i):
                pe.wait_ge(s["xT"], nth(i))
                for k in range(2):
                    w = pe.matmul(Z[:, 1, k * P:(k + 1) * P], wT[:, 6 + k, :], xcT[:, 0:2, 0:S], start=True, stop=True)
                w.then_inc(s["qk"], 1)
                for b in range(2):
                    w = pe.matmul(Z[:, 0, b * D:(b + 1) * D], xcT[:, b, :], wT[:, 8, :], start=True, stop=True)
                w.then_inc(A["v"], 1)

            def tail_y(i):
                pe.wait_ge(A["att"], nth(i + base))
                out_projection(pe, 2).then_inc(A["y"], 1)

            def body(i, first, last):
                pe.wait_ge(s["ke"], nth(i))
                if not first:
                    pe.wait_ge(M6["wT"], i)
                pe.wait_ge(s["qx"], nth(i))
                for gg in range(4):
                    rows = slice(32 * gg, 32 * gg + 32)
                    for b in range(2):
                        w = pe.matmul(Z[:, 3 + gg, b * P:(b + 1) * P], kview(1)[rows, b, :], qe[rows, b].rearrange("p j q -> p (j q)"),
                                      start=True, stop=True, skip_group_check=True)
                    if gg % 2:
                        w.then_inc(s["s"], 1)
                if not last:
                    front_T(i + 1)
                if not last:
                    front_qkv(i + 1)
                pe.wait_ge(s["pm"], 2 * i + 2)
                if not first:
                    expert_product(pe, i - 1)
                expert_transposes(pe, i)
                if not first:
                    tail_y(i - 1)
                pe.wait_ge(A["va"], nth(i + base))
                for p in range(2):
                    if p == 1 and not first:
                        pe.wait_ge(s["bo"], i)
                    pe.wait_ge(s["pm"], 2 * i + p + 1)
                    sums_pe(pe, 5, p, sc[p]).then_inc(A["av"], 1)

            def ahead(i):
                front_T(i)
                front_qkv(i)

            pipelined(pe, ahead, body)
            tail_y(NT - 1)
            expert_product(pe, E - 1)

        def expert_transposes(pe, e):
            pe.wait_ge(M6["wout"], nth(e, 16))
            for c in range(FC):
                w = pe.transpose(Z[:, 3, c * P:(c + 1) * P], we2[:].rearrange("p c n -> p (c n)")[:, c * P:(c + 1) * P], ident)
            w.then_inc(M6["wt"], 1)

        def expert_product(pe, e):
            pe.wait_ge(M6["win"], nth(e, 16))
            pe.wait_ge(M6["wT"], nth(e))
            for c in range(FC):
                w = pe.matmul(Z[:, 5, 0:D], we1[:, c * P:(c + 1) * P], woutT[:, c, :], start=(c == 0), stop=(c == FC - 1))
            w.then_inc(M6["m"], 1)

        def linear_dve(v):
            s, base = C5, 2 * NT
            v.wait_ge(A["out"], 2 * NT)
            stats_all(v, N, 5, X)
            v.wait_ge(N["ars"], 5)

            def front(i):
                if not isinstance(i, int) or i > 0:
                    v.wait_ge(s["T"], i)
                scale_tile(v, s, i, i)

            def front_min(i):
                v.wait_ge(s["qk"], nth(i))
                for k in range(2):
                    bias = vcol[:, 26 + k:27 + k]
                    w = v.tensor_scalar(fm[:, k * P:(k + 1) * P], Z[:, 1, k * P:(k + 1) * P], bias, 0.0, ALU.add, ALU.min)
                w.then_inc(s["fm"], 1)

            def front_max(i):
                for k in range(2):
                    bias = vcol[:, 26 + k:27 + k]
                    w = v.tensor_scalar(fr[:, k * P:(k + 1) * P], Z[:, 1, k * P:(k + 1) * P], bias, 0.0, ALU.add, ALU.max)
                w.then_inc(s["fr"], 1)

            def take_product(e):
                v.wait_ge(M6["m"], nth(e))
                v.tensor_scalar(wc[:, bass.ds(e, 1), :].rearrange("p a n -> p (a n)"), Z[:, 5, 0:D], 1.0, None, ALU.mult)\
                    .then_inc(M6["wc"], 1)

            def front_features(i):
                v.wait_ge(s["fr"], nth(i))
                v.wait_ge(s["fe"], nth(i))
                v.scalar_tensor_tensor(out=qk[:], in0=fm[:], scalar=FEAT_EPS, in1=fr[:], op0=ALU.add, op1=ALU.add).then_inc(s["ff"], 1)

            def tail(i):
                v.wait_ge(A["y"], nth(i + base))
                v.tensor_tensor(tile_of(acc, i), Z[:, 7, 0:D], vbc[:, 2, :], ALU.add).then_inc(s["bo"], 1)

            def body(i, first, last):
                if not last:
                    front(i + 1)
                for p in range(2):
                    v.wait_ge(s["s"], 2 * i + p + 1)
                    v.tensor_tensor(sc[p][:].rearrange("p r k -> p (r k)")[:, 0:8 * S].rearrange("p (g j q) -> p g j q", g=2, j=4),
                                    Z[:, 3 + 2 * p:5 + 2 * p, 0:4 * S].rearrange("p g (j q) -> p g j q", j=4),
                                    const("mask01").unsqueeze(1).unsqueeze(1).broadcast_to([P, 2, 4, S]), ALU.mult).then_inc(s["pm"], 1)
                if not last:
                    front_min(i + 1)
                if not first:
                    divide_dve(v, A, 5, i - 1 + base)
                if not last:
                    front_max(i + 1)
                if not first:
                    take_product(i - 1)
                if not last:
                    front_features(i + 1)
                if not first:
                    tail(i - 1)
                if not last:
                    v.wait_ge(A["av"], 2 * (i + base) + 2)
                    values_dve(v, A, 5, i + 1, i + 1 + base)

            def ahead(i):
                front(i)
                front_min(i)
                front_max(i)
                front_features(i)
                values_dve(v, A, 5, i, i + base)

            pipelined(v, ahead, body)
            divide_dve(v, A, 5, NT - 1 + base)
            tail(NT - 1)
            take_product(E - 1)
            v.wait_ge(s["bo"], NT)
            norm_all(v, N, 6, acc, Y)
            v.tensor_tensor(Y[:], Y[:], vbc[:, 3, :].unsqueeze(1).broadcast_to([P, NT, D]), ALU.mult).then_inc(s["g"], 1)
            v.wait_ge(s["xb"], 1)
            v.wait_ge(s["g"], 1)
            v.tensor_tensor(X[:], Y[:], X[:], ALU.add).then_inc(s["out"], 1)
            v.wait_ge(s["out"], 1)

        def linear_pool(g):
            s, base = C5, 2 * NT
            norm_all_pool(g, N, 5)

            def queries(i):
                g.wait_ge(s["ff"], nth(i))
                g.tensor_tensor(qe[:], qk[:, 0:P].rearrange("p (b q) -> p b q", b=2).unsqueeze(2).broadcast_to([P, 2, 2, S]),
                                const("qpar").unsqueeze(1).unsqueeze(3).broadcast_to([P, 2, 2, S]), ALU.mult).then_inc(s["qx"], 1)

            beside(g, queries, lambda i: sums_pool(g, A, i + base))
            g.wait_ge(s["xn"], NT)
            g.tensor_tensor(X[:], X[:], vbc[:, 4, :].unsqueeze(1).broadcast_to([P, NT, D]), ALU.add).then_inc(s["xb"], 1)
            norm_all_pool(g, N, 6)

        def moe6_pe(pe):
            pe.wait_ge(C5["out"], 1)
            pe.wait_ge(M6["wc"], E)
            router_pe(pe, 1)
            for t in range(NT):
                if t == 1:
                    pe.wait_ge(M6["r"], 1)
                if t >= 4:
                    pe.wait_ge(M6["acc"], E * ((t - 4) // 2 + 1))
                    pe.wait_ge(M6["parts"], t - 3)
                for k in range(2):
                    w = pe.matmul(Z[:, 2 * (t % 4) + k, :], tT[:, t * P:(t + 1) * P],
                                  wc[:, 4 * k:4 * k + 4, :], start=True, stop=True)
                w.then_inc(M6["o"], 1)

        def parts(t):
            return hT[0][:, t % 2, :].rearrange("p (e n) -> p e n", e=4)

        def moe6_act(act):
            router_act(act, 1)
            act.wait_ge(M6["gate"], 1)
            for t in range(NT):
                act.wait_ge(M6["o"], t + 1)
                if t >= 2:
                    act.wait_ge(M6["pair"], t - 1)
                for e in range(E // 2):
                    w = act.activation(parts(t)[:, e, :], Z[:, 2 * (t % 4), e * P:(e + 1) * P], ACT.Identity, scale=gate[:, e, t:t + 1])
                w.then_inc(M6["parts"], 1)

        def moe6_pool(g):
            norm_all_pool(g, N, 7)
            for t in range(NT):
                pair = hT[1][:, t % 2, 0:2 * P].rearrange("p (a n) -> p a n", a=2)
                g.wait_ge(M6["parts"], t + 1)
                g.tensor_tensor(pair, parts(t)[:, 0:2, :], parts(t)[:, 2:4, :], ALU.add).then_inc(M6["pair"], 1)
                g.wait_ge(M6["pair"], t + 1)
                g.tensor_tensor(acc[:, t, :], pair[:, 0, :], pair[:, 1, :], ALU.add).then_inc(M6["half"], 1)

        def moe6_dve(v):
            v.wait_ge(C5["out"], 1)
            norm_all(v, N, 7, X, Y)
            link = chain(v, M6["r"])

            def take_sums(q):
                v.wait_ge(M6["half"], 2 * q + 2)
                v.tensor_tensor(X[:, 2 * q:2 * q + 2, :], X[:, 2 * q:2 * q + 2, :], acc[:, 2 * q:2 * q + 2, :], ALU.add)

            v.wait_ge(R["lg"], 2)
            link(v.tensor_copy(lg[:].rearrange("p t e -> p (t e)"), Z[:, 2, 0:NT * E]))
            link(v.tensor_reduce(m1[:], lg[:], AX.X, ALU.max))
            first_of(v, link, oh, lg, m1)
            link(v.tensor_scalar(r2[:], oh[:], NEG, None, ALU.mult))
            link(v.tensor_tensor(lg[:], lg[:], r2[:], ALU.add))
            link(v.tensor_reduce(m2[:], lg[:], AX.X, ALU.max))
            first_of(v, link, oh2, lg, m2)
            v.tensor_tensor(m3[:], m2[:], m1[:], ALU.subtract).then_inc(R["d"], 1)
            v.wait_ge(R["ex"], 2)
            link(v.tensor_scalar(m1[:], m3[:], 1.0, None, ALU.add))
            link(v.reciprocal(m1[:], m1[:]))
            link(v.tensor_tensor(m2[:], m3[:], m1[:], ALU.mult))
            link(v.tensor_tensor(oh[:], oh[:], per_token(m1), ALU.mult))
            link(v.tensor_tensor(oh2[:], oh2[:], per_token(m2), ALU.mult))
            v.tensor_tensor(gate[:].rearrange("p e t -> p t e"), oh[:], oh2[:], ALU.add).then_inc(M6["gate"], 1)
            v.wait_ge(M6["gate"], 1)
            done = 0
            for q in range(NT // 2):
                v.wait_ge(M6["o"], 2 * q + 2)
                for e in range(E // 2, E):
                    for t in (2 * q, 2 * q + 1):
                        if done >= 2:
                            v.wait_ge(M6["acc"], done - 1)
                        v.scalar_tensor_tensor(out=X[:, t, :], in0=Z[:, 2 * (t % 4) + 1, (e % 4) * P:(e % 4 + 1) * P],
                                               scalar=gate[:, e, t:t + 1], in1=X[:, t, :], op0=ALU.mult, op1=ALU.add).then_inc(M6["acc"], 1)
                        done += 1
                if q:
                    take_sums(q - 1)
            v.wait_ge(M6["acc"], done)
            take_sums(NT // 2 - 1)
            v.memset(spacer[:], 0.0).then_inc(M6["out"], 1)

        def layers_load(sp):
            def load(l, first):
                def of(name):
                    return a[name][bass.ds(l, 1)].rearrange("l p n -> (l p) n")

                def read(name, each=2):
                    if not first:
                        sp.wait_ge(L[name], each * l)

                read("qt")
                sp.dma_start(wq[:], of("L0_attn_wq")).then_inc(L["w"], 16)
                sp.dma_start(wk[:], of("L0_attn_wk")).then_inc(L["w"], 16)
                read("v")
                sp.dma_start(wv[:], of("L0_attn_wv")).then_inc(L["wv"], 16)
                read("yb")
                sp.dma_start(bo[:], a["L0_attn_bo"][bass.ds(l, 1)].rearrange("l n -> (l n)").partition_broadcast(P)).then_inc(L["bo"], 16)
                read("wo_", 4)
                sp.dma_start(wo[:], of("L0_attn_wo")).then_inc(L["wo"], 16)
                read("h1", 8)
                sp.dma_start(w1[:], of("L0_attn_w1")).then_inc(L["w1"], 16)
                read("w2_", 4)
                sp.dma_start(w2[:], a["L0_attn_w2"].rearrange("l (c p) n -> l p c n", p=P)[bass.ds(l, 1)]
                             .rearrange("l p c n -> (l p) c n")).then_inc(L["w2"], 16)

            peeled(sp, DEPTH, load)

        def experts_load(sp, q, first):
            for k in range(QE):
                if not first:
                    sp.wait_ge(M3["h"], (q - 1) * QE + k + 1)
                sp.dma_start(xw1[k][:], a["L0_ffn_W1"][q * QE + k]).then_inc(M3["w1" + "ab"[k // 2]], 16)
                if not first:
                    sp.wait_ge(M3["o"], (q - 1) * QE + k + 1)
                sp.dma_start(xw2[k][:], a["L0_ffn_W2"][q * QE + k].rearrange("(c p) n -> p c n", p=P)).then_inc(M3["w2" + "ab"[k // 2]], 16)

        @block.sync
        def _(sp):
            sp.dma_start(C[:], a["const"]).then_inc(s_tab, 16)
            sp.dma_start(X[:], x_d).then_inc(s_x, 16)
            for k, name in zip((0, 1, 2, 9), ("L0_xattn_Wq", "L0_xattn_Wk", "L0_xattn_Wv", "L0_xattn_Wo")):
                sp.dma_start(wraw[:, k, :], a[name]).then_inc(s_w1, 16)
            late = [(k, a[name]) for k, name in zip((3, 4, 5, 10, 11), ("L1_xattn_Wq", "L1_xattn_Wk", "L1_xattn_Wv", "L1_xattn_Wo", "L1_attn_Wout"))]
            for st in (1, 4):
                if st == 4:
                    sp.wait_ge(M3["there"], 16 * NT)
                    sp.dma_start(slot[:], slots_d).then_inc(M3["slots"], 16)
                    experts_load(sp, 1, False)
                    sp.wait_ge(M3["rTe"], 2)
                    sp.dma_start(slots_d, slot[:]).then_inc(M3["stored"], 16)

                def load(i, first):
                    if not first or st == 4:
                        sp.wait_ge(A["ctxT"], i if st == 1 else i + NT)
                    if st == 1:
                        for hf in range(2):
                            sp.dma_start(ctxbuf[hf * S:(hf + 1) * S], ctx_d[0:S, bass.ds(2 * i, 2), :]).then_inc(A["ctx"], 16)
                    else:
                        sp.dma_start(ctxbuf[:], ctx_d[:, bass.ds(2 * i, 2), :]).then_inc(A["ctx4"], 16)

                load(0, True)
                if st == 1:
                    for k, name in enumerate(("L0_attn_ln1_w", "L0_attn_ln1_b", "L0_attn_ln2_w", "L0_attn_ln2_b")):
                        sp.dma_start(vrow[6 * k:6 * k + 6, :], a[name]).then_inc(s_vec, 16)
                    sp.dma_start(vrow[24:25, :], a["L1_xattn_bq"].unsqueeze(0)).then_inc(s_vec, 16)
                    sp.dma_start(vrow[25:26, :], a["L1_xattn_bk"].unsqueeze(0)).then_inc(s_vec, 16)
                    sp.dma_start(vrow[26:29, :], a["L1_attn_bqkv"].rearrange("(c n) -> c n", n=P)).then_inc(s_vec, 16)
                    sp.dma_start(vrow[29:32, :], a["L1_attn_bqkv"].rearrange("(c n) -> c n", n=P)).then_inc(s_vec, 16)
                    for k, v in enumerate((a["L1_xattn_bo"], a["L1_attn_bout"], a["L1_attn_gamma"], a["L1_attn_beta"])):
                        sp.dma_start(vbc[:, 1 + k, :], v.partition_broadcast(P)).then_inc(s_vec, 16)
                    for k, v in enumerate((a["L1_xattn_bv"], a["L1_attn_bqkv"][2 * D:3 * D])):
                        for b in range(2):
                            sp.dma_start(vbd[:, 1 + k, b * D:(b + 1) * D], v.partition_broadcast(P)).then_inc(s_vec, 16)
                    sp.dma_start(wr[:, 0, :], a["L0_ffn_Wr"]).then_inc(s_vec, 16)
                    sp.dma_start(wgraw[:], a["L1_ffn_w_gate"]).then_inc(s_vec, 16)
                with sp.Fori(1, NT) as i:
                    load(i, False)
                if st == 1:
                    for k, w in late:
                        sp.dma_start(wraw[:, k, :], w).then_inc(s_const, 16)
                    sp.dma_start(wraw[:, 6:9, :], a["L1_attn_Wqkv"].rearrange("(c p) n -> p c n", p=P)).then_inc(s_const, 16)
                if st == 1:
                    sp.wait_ge(s_zero, 3)
                    sp.dma_start(slots_d[:, 0:NT, :], acc[:]).then_inc(s_clear, 16)
                    sp.dma_start(slots_d[:, NT:SLOTS, :], acc[:, 0:SLOTS - NT, :]).then_inc(s_clear, 16)
                    sp.dma_start(a["slots"][E * CAP:E * CAP + B * S].rearrange("(s p) n -> p s n", p=P), acc[:]).then_inc(s_clear, 16)
                    experts_load(sp, 0, True)
                if st == 1:
                    layers_load(sp)
            def load(e, first):
                if not first:
                    sp.wait_ge(M6["wt"], e)
                sp.dma_start(we2[:].rearrange("p c n -> p (c n)"), a["L1_ffn_w_out"][bass.ds(e, 1)]
                             .rearrange("e p n -> (e p) n")).then_inc(M6["wout"], 16)
                if not first:
                    sp.wait_ge(M6["m"], e)
                sp.dma_start(we1[:].rearrange("p (c n) -> p c n", c=FC), a["L1_ffn_w_in"].rearrange("e (c p) n -> e p c n", p=P)
                             [bass.ds(e, 1)].rearrange("e p c n -> (e p) c n")).then_inc(M6["win"], 16)

            peeled(sp, E, load)
            sp.wait_ge(M6["out"], 1)
            sp.dma_start(out_d, X[:]).then_inc(s_out, 16)
            sp.wait_ge(s_out, 16)

        @block.scalar
        def _(act):
            act.dma_start(brow[:, 0, :], a["L0_xattn_bq"].unsqueeze(0)).then_inc(s_vec1, 16)
            act.dma_start(brow[:, 1, :], a["L0_xattn_bk"].unsqueeze(0)).then_inc(s_vec1, 16)
            for b in range(2):
                act.dma_start(vbd[:, 0, b * D:(b + 1) * D], a["L0_xattn_bv"].partition_broadcast(P)).then_inc(s_vec1, 16)
            act.dma_start(vbc[:, 0, :], a["L0_xattn_bo"].partition_broadcast(P)).then_inc(s_vec1, 16)
            attention_act(act, 1)
            layers_act(act)
            moe_act(act)
            attention_act(act, 4)
            linear_act(act)
            moe6_act(act)

        NVEC = 16 * 18

        @block.tensor
        def _(pe):
            pe.wait_ge(s_tab, 16)
            pe.wait_ge(s_w1, 16 * 4)
            for k in range(3):
                t = pe.transpose(Z[:, 0, k * P:(k + 1) * P], wraw[:, k, :], ident)
            t.then_inc(s_sett, 1)
            pe.transpose(Z[:, 4, 0:P], wraw[:, 9, :], ident).then_inc(s_sett, 1)
            pe.wait_ge(s_setp, 1)
            for k, row in enumerate((brow, brot)):
                for j in range(2):
                    t = pe.matmul(Z[:, 6, (2 * k + j) * 2 * S:(2 * k + j + 1) * 2 * S], row[:, j, :],
                                  const("ones")[0:1, :], start=True, stop=True)
            t.then_inc(s_sett, 1)
            pe.wait_ge(s_set, 4)
            attention_pe(pe, 1)
            pe.wait_ge(s_vec, NVEC)
            pe.transpose(Z[:, 3, 0:32], vrow[:], ident[0:32, 0:32])
            pe.transpose(Z[:, 3, 32:40], wgraw[:], ident[0:8, 0:8]).then_inc(s_sett, 1)
            layers_pe(pe)
            moe_pe(pe)
            attention_pe(pe, 4)
            linear_pe(pe)
            moe6_pe(pe)

        @block.vector
        def _(v):
            v.memset(eps[:], LN_EPS)
            v.memset(denb[:, 0:1], 0.0)
            v.memset(denb[:, 1:2], FEAT_EPS)
            v.memset(power[:], -0.5).then_inc(s_set, 1)
            v.memset(vx[:], 0.0)
            v.memset(vx4[:], 0.0).then_inc(s_zero, 1)
            v.wait_ge(s_zero, 1)
            for jj in range(2):
                v.memset(value_cols(1, jj, P // 2), 1.0)
            v.memset(value_cols(4, 0, P // 2), 1.0).then_inc(s_zero, 1)
            v.memset(acc[:], 0.0).then_inc(s_zero, 1)
            v.wait_ge(s_tab, 16)
            v.tensor_copy(CB[:], C[:])
            v.memset(spacer[:], 0.0).then_inc(s_set, 1)
            v.wait_ge(s_x, 16)
            stats_all(v, N, 1, X)
            v.wait_ge(s_sett, 1)
            v.tensor_copy(wT[:, 0:3, :].rearrange("p k n -> p (k n)"), Z[:, 0, 0:3 * D]).then_inc(s_set, 1)
            v.wait_ge(s_set, 3)
            for k in range(2):
                w = wT[:, k, :].rearrange("p (h t d) -> p h t d", t=2, d=DH // 2)
                r = wrot[:, k, :].rearrange("p (h t d) -> p h t d", t=2, d=DH // 2)
                v.tensor_scalar(r[:, :, 0, :], w[:, :, 1, :], -1.0, None, ALU.mult)
                v.tensor_copy(r[:, :, 1, :], w[:, :, 0, :])
            v.wait_ge(s_sett, 2)
            for j in range(2):
                v.tensor_scalar(woM[:, 0, j, :], Z[:, 4, 0:P], const("hpar")[:, j:j + 1], None, ALU.mult)
            v.wait_ge(s_sett, 3)
            v.tensor_tensor(qkx[:, 0, :], Z[:, 6, 0:4 * S], const("cos2"), ALU.mult)
            v.tensor_tensor(qkx[:, 1, :], Z[:, 6, 4 * S:8 * S], const("sin2"), ALU.mult).then_inc(s_setd, 1)
            v.wait_ge(s_setd, 1)
            v.tensor_tensor(BQK[:].rearrange("p a s -> p (a s)"), qkx[:, 0, :], qkx[:, 1, :], ALU.add).then_inc(s_setd, 1)
            v.wait_ge(s_setd, 2)
            for k, mask in enumerate(("qpar", "kpair")):
                for j in range(2):
                    w = v.tensor_scalar(BM[:, 2 * k:2 * k + 2, j, :], BQK[:, 2 * k:2 * k + 2, :], const(mask)[:, j:j + 1], None, ALU.mult)
            w.then_inc(s_set, 1)
            v.wait_ge(s_zero, 3)
            v.wait_ge(s_vec1, 16 * 5)
            attention_dve(v, 1)
            v.wait_ge(s_sett, 4)
            v.tensor_copy(vcol[:], Z[:, 3, 0:32])
            v.tensor_copy(wr[:, 1, :], Z[:, 3, 32:40]).then_inc(s_setd, 1)
            v.wait_ge(s_setd, 3)
            v.tensor_scalar(bqm[:], const("qpar"), vcol[:, 24:25], None, ALU.mult)
            v.tensor_scalar(bkm[:], const("kpair"), vcol[:, 25:26], None, ALU.mult).then_inc(s_setd, 1)
            layers_dve(v)
            moe_dve(v)
            attention_dve(v, 4)
            linear_dve(v)
            moe6_dve(v)

        @block.gpsimd
        def _(g):
            g.wait_ge(s_vec1, 16 * 5)
            for j in range(2):
                w = brow[:, j, :].rearrange("p (h t d) -> p h t d", t=2, d=DH // 2)
                r = brot[:, j, :].rearrange("p (h t d) -> p h t d", t=2, d=DH // 2)
                g.tensor_scalar(r[:, :, 0, :], w[:, :, 1, :], -1.0, None, ALU.mult)
                t = g.tensor_copy(r[:, :, 1, :], w[:, :, 0, :])
            t.then_inc(s_setp, 1)
            attention_pool(g, 1)
            g.wait_ge(s_vec, NVEC)
            layers_pool(g)
            moe_pool(g)
            attention_pool(g, 4)
            linear_pool(g)
            moe6_pool(g)



def kernel(**inputs):
    import concourse.bacc as bacc
    from concourse.bass_utils import run_bass_kernel_spmd as run

    nc = bacc.Bacc("TRN2", target_bir_lowering=False, num_devices=1)
    arrays, args = {}, {}
    for name, array in [("const", const_table())] + list(inputs.items()):
        arrays[f"in_{name}"] = np.ascontiguousarray(array)
        args[name] = nc.dram_tensor(f"in_{name}", arrays[f"in_{name}"].shape, F32, kind="ExternalInput").ap()
    args["slots"] = nc.dram_tensor("slots", (E * CAP + B * S, D), F32).ap()
    out = nc.dram_tensor("out", (B, S, D), F32, kind="ExternalOutput").ap()
    perceiver_kernel(nc, args, out)
    return run(nc, [arrays], core_ids=[0]).results[0]["out"]
```
